# Optimizing a Trainium2 kernel written in Bass

```python
import numpy as np
import jax
import jax.numpy as jnp

def _softmax(x, axis=-1):
    return jax.nn.softmax(x, axis=axis)

def _gelu(x):
    return jax.nn.gelu(x, approximate=True)

def _silu(x):
    return jax.nn.silu(x)

def _sigmoid(x):
    return jax.nn.sigmoid(x)

def _layernorm(x, axis=-1, eps=1e-05):
    m = jnp.mean(x, axis=axis, keepdims=True)
    v = jnp.var(x, axis=axis, keepdims=True)
    return (x - m) / jnp.sqrt(v + eps)

def _scatter_add(tgt, idx, src, axis=0):
    return tgt.at[idx].add(src)

def _segment_sum(src, seg, n):
    return jax.ops.segment_sum(src, seg, n)
kernel_name = 'mk_flamingo_gated_d2_seqx_r8_e5b003'

def setup_inputs(seed: int=0):
    np.random.seed(seed)
    _w = jnp.asarray

    def _rec_inputs():
        import jax
        import jax.numpy as jnp
        _rk = jax.random.key(seed)
        x = -0.0003929 + 0.9999 * jax.random.normal(jax.random.fold_in(_rk, 1), (32, 64, 128), jnp.float32)
        _lenS = 64 - jax.random.randint(jax.random.fold_in(_rk, 7), (32,), 0, max(1, 64 // 4) + 1, jnp.int32)
        _lenS2 = 64 - jax.random.randint(jax.random.fold_in(_rk, 8), (32,), 0, max(1, 64 // 4) + 1, jnp.int32)
        _ctx_1024P = jax.random.normal(jax.random.fold_in(_rk, 11), (32, 16, 128), jnp.float32)
        _ctx_1024c = jax.random.dirichlet(jax.random.fold_in(_rk, 511), 0.3 * jnp.ones((16,), jnp.float32), (32, 64))
        _ctx_1024t = jnp.einsum('bsk,bkd->bsd', _ctx_1024c, _ctx_1024P)
        _ctx_1024t = _ctx_1024t * jax.lax.rsqrt(jnp.mean(jnp.square(_ctx_1024t)) + 1e-12) * 0.953939
        ctx_1024 = 2.81802e-05 + 1.00001 * (_ctx_1024t + 0.3 * jax.random.normal(jax.random.fold_in(_rk, 611), (32, 64, 128), jnp.float32))
        _validS = jnp.arange(64)[None, :] < _lenS[:, None]
        _validS2 = jnp.arange(64)[None, :] < _lenS2[:, None]
        _causal = jnp.tril(jnp.ones((64, 64), dtype=bool))
        mask_BxS2_ff1 = jnp.where(jnp.ones((32, 64), dtype=bool), 1.0, 0.0).astype(jnp.float32)
        mask_BxS2_ik0 = jnp.where(jnp.broadcast_to(_validS2[:, :], (32, 64)), 0, 1).astype(jnp.int32)
        _g = jax.random.normal(jax.random.fold_in(_rk, 9001), (2, 2), jnp.float32)
        _g = jnp.sign(_g) * jnp.maximum(jnp.abs(_g), 1.0) + (_g == 0) * 1.0
        g_xattn = _g[0]
        g_ffn = _g[1]
        return (x, ctx_1024, mask_BxS2_ff1, mask_BxS2_ik0, g_xattn, g_ffn)
    x, ctx_1024, mask_BxS2_ff1, mask_BxS2_ik0, g_xattn, g_ffn = _rec_inputs()

    def _L0_xattn_setup():
        import jax, jax.numpy as jnp
        import numpy as np
        D_MODEL = 128
        HEADS = 16
        DEPTH = D_MODEL // HEADS
        B, S = (4, 512)
        EPS_K = 1e-06
        EPS_LN = 1e-06

        def _layernorm(x, g, b):
            m = jnp.mean(x, axis=-1, keepdims=True)
            var = jnp.var(x, axis=-1, keepdims=True)
            return (x - m) * jax.lax.rsqrt(var + EPS_LN) * g + b

        def _split_heads(x):
            bsz, sl, _ = x.shape
            return x.reshape(bsz, sl, HEADS, DEPTH).transpose(0, 2, 1, 3)
        key = jax.random.key(seed)
        ks = jax.random.split(key, 8)
        lecun = 1.0 / np.sqrt(D_MODEL)
        glorot = np.sqrt(2.0 / (D_MODEL + D_MODEL))
        return {'q': jax.random.normal(ks[0], (B, S, D_MODEL), jnp.float32), 'k': jax.random.normal(ks[1], (B, S, D_MODEL), jnp.float32), 'v': jax.random.normal(ks[2], (B, S, D_MODEL), jnp.float32), 'mask': jnp.ones((B, S), jnp.float32), 'wq': jax.random.normal(ks[3], (D_MODEL, D_MODEL), jnp.float32) * lecun, 'wk': jax.random.normal(ks[4], (D_MODEL, D_MODEL), jnp.float32) * lecun, 'wv': jax.random.normal(ks[5], (D_MODEL, D_MODEL), jnp.float32) * lecun, 'ln_gamma': jnp.ones((D_MODEL,), jnp.float32), 'ln_beta': jnp.zeros((D_MODEL,), jnp.float32), 'dense_w': jax.random.normal(ks[6], (D_MODEL, D_MODEL), jnp.float32) * glorot, 'dense_b': jnp.zeros((D_MODEL,), jnp.float32)}
    _L0_xattn_all = _L0_xattn_setup()
    _L0_xattn_in = {k: v for k, v in _L0_xattn_all.items() if k in ('wq', 'wk', 'wv', 'ln_gamma', 'ln_beta', 'dense_w', 'dense_b')}
    del _L0_xattn_all

    def _L0_ffn_setup():
        import math
        import jax, jax.numpy as jnp
        import numpy as np
        H = 128
        F = 512
        E = 8
        TOP_K = 2
        CAP_FACTOR = 1.25
        MIN_CAP = 4
        SHARED_SCALE = 0.1

        def _top2_gating(logits, capacity):
            N, nE = logits.shape
            gates = jax.nn.softmax(logits, axis=-1)
            idx1 = jnp.argmax(gates, axis=-1)
            mask1 = jax.nn.one_hot(idx1, nE, dtype=gates.dtype)
            idx2 = jnp.argmax(gates * (1.0 - mask1), axis=-1)
            mask2 = jax.nn.one_hot(idx2, nE, dtype=gates.dtype)
            pos1 = jnp.cumsum(mask1, axis=0) - mask1
            mask1 = mask1 * (pos1 < capacity)
            pos2 = jnp.cumsum(mask2, axis=0) - mask2 + jnp.sum(mask1, axis=0, keepdims=True)
            mask2 = mask2 * (pos2 < capacity)
            g1 = jnp.sum(gates * mask1, axis=-1)
            g2 = jnp.sum(gates * mask2, axis=-1)
            denom = jnp.maximum(g1 + g2, jnp.finfo(gates.dtype).eps)
            g1, g2 = (g1 / denom, g2 / denom)
            loc1 = jnp.sum(pos1 * mask1, axis=-1).astype(jnp.int32)
            loc2 = jnp.sum(pos2 * mask2, axis=-1).astype(jnp.int32)
            oh1 = jax.nn.one_hot(loc1, capacity, dtype=gates.dtype)
            oh2 = jax.nn.one_hot(loc2, capacity, dtype=gates.dtype)
            combine = (g1[:, None] * mask1)[:, :, None] * oh1[:, None, :] + (g2[:, None] * mask2)[:, :, None] * oh2[:, None, :]
            dispatch = (combine > 0).astype(gates.dtype)
            return (combine, dispatch)
        key = jax.random.key(seed)
        ks = jax.random.split(key, 10)
        s_h = 1.0 / math.sqrt(H)
        s_f = 1.0 / math.sqrt(F)
        return {'hidden_states': jax.random.normal(ks[0], (2, 256, H), jnp.float32), 'router_w': jax.random.uniform(ks[1], (H, E), jnp.float32, -s_h, s_h), 'w1': jax.random.uniform(ks[2], (E, H, F), jnp.float32, -s_h, s_h), 'b1': jax.random.uniform(ks[3], (E, F), jnp.float32, -s_h, s_h), 'w2': jax.random.uniform(ks[4], (E, F, H), jnp.float32, -s_f, s_f), 'b2': jax.random.uniform(ks[5], (E, H), jnp.float32, -s_f, s_f), 'sw1': jax.random.uniform(ks[6], (H, F), jnp.float32, -s_h, s_h), 'sb1': jax.random.uniform(ks[7], (F,), jnp.float32, -s_h, s_h), 'sw2': jax.random.uniform(ks[8], (F, H), jnp.float32, -s_f, s_f), 'sb2': jax.random.uniform(ks[9], (H,), jnp.float32, -s_f, s_f)}
    _L0_ffn_all = _L0_ffn_setup()
    _L0_ffn_in = {k: v for k, v in _L0_ffn_all.items() if k in ('router_w', 'w1', 'b1', 'w2', 'b2', 'sw1', 'sb1', 'sw2', 'sb2')}
    del _L0_ffn_all

    def _L1_xattn_setup():
        import jax, jax.numpy as jnp
        import numpy as np
        D = 128
        NEG = -1000000000.0
        key = jax.random.key(seed)
        ks = jax.random.split(key, 9)
        B, Lq, Lk, d = (8, 256, 256, D)
        s = 1.0 / np.sqrt(d)
        return {'hm_tokens': jax.random.normal(ks[0], (B, Lq, d), jnp.float32), 'text_tokens': jax.random.normal(ks[1], (B, Lk, d), jnp.float32), 'text_mask': jax.random.randint(ks[2], (B, Lk), 0, 2, jnp.int32), 'Wq': jax.random.normal(ks[3], (d, d), jnp.float32) * s, 'bq': jnp.zeros((d,), jnp.float32), 'Wk': jax.random.normal(ks[4], (d, d), jnp.float32) * s, 'bk': jnp.zeros((d,), jnp.float32), 'Wv': jax.random.normal(ks[5], (d, d), jnp.float32) * s, 'bv': jnp.zeros((d,), jnp.float32)}
    _L1_xattn_all = _L1_xattn_setup()
    _L1_xattn_in = {k: v for k, v in _L1_xattn_all.items() if k in ('Wq', 'bq', 'Wk', 'bk', 'Wv', 'bv')}
    del _L1_xattn_all

    def _L1_ffn_setup():
        import math
        import jax, jax.numpy as jnp
        import numpy as np
        D_MODEL = 128
        D_FF = 512
        E = 8
        K = 2
        CF = 1.25
        CLAMP = 10000.0
        key = jax.random.key(seed)
        k0, k1, k2, k3 = jax.random.split(key, 4)
        B, S = (4, 256)
        x = jax.random.normal(k0, (B, S, D_MODEL), dtype=jnp.float32)
        ln_gamma = jnp.ones((D_MODEL,), jnp.float32)
        ln_beta = jnp.zeros((D_MODEL,), jnp.float32)
        rb = 0.02 * math.sqrt(3.0)
        Wr = jax.random.uniform(k1, (E, D_MODEL), jnp.float32, -rb, rb)
        b12 = math.sqrt(6.0 / (D_MODEL + 2 * D_FF))
        W12 = jax.random.uniform(k2, (E, 2 * D_FF, D_MODEL), jnp.float32, -b12, b12)
        b3 = math.sqrt(6.0 / (D_FF + D_MODEL))
        W3 = jax.random.uniform(k3, (E, D_MODEL, D_FF), jnp.float32, -b3, b3)
        return {'x': x, 'ln_gamma': ln_gamma, 'ln_beta': ln_beta, 'Wr': Wr, 'W12': W12, 'W3': W3}
    _L1_ffn_all = _L1_ffn_setup()
    _L1_ffn_in = {k: v for k, v in _L1_ffn_all.items() if k in ('ln_gamma', 'ln_beta', 'Wr', 'W12', 'W3')}
    del _L1_ffn_all
    return {'x': x, 'ctx_1024': ctx_1024, 'mask_BxS2_ff1': mask_BxS2_ff1, 'mask_BxS2_ik0': mask_BxS2_ik0, 'g_xattn': g_xattn, 'g_ffn': g_ffn, 'L0_xattn_wq': _L0_xattn_in['wq'], 'L0_xattn_wk': _L0_xattn_in['wk'], 'L0_xattn_wv': _L0_xattn_in['wv'], 'L0_xattn_ln_gamma': _L0_xattn_in['ln_gamma'], 'L0_xattn_ln_beta': _L0_xattn_in['ln_beta'], 'L0_xattn_dense_w': _L0_xattn_in['dense_w'], 'L0_xattn_dense_b': _L0_xattn_in['dense_b'], 'L0_ffn_router_w': _L0_ffn_in['router_w'], 'L0_ffn_w1': _L0_ffn_in['w1'], 'L0_ffn_b1': _L0_ffn_in['b1'], 'L0_ffn_w2': _L0_ffn_in['w2'], 'L0_ffn_b2': _L0_ffn_in['b2'], 'L0_ffn_sw1': _L0_ffn_in['sw1'], 'L0_ffn_sb1': _L0_ffn_in['sb1'], 'L0_ffn_sw2': _L0_ffn_in['sw2'], 'L0_ffn_sb2': _L0_ffn_in['sb2'], 'L1_xattn_Wq': _L1_xattn_in['Wq'], 'L1_xattn_bq': _L1_xattn_in['bq'], 'L1_xattn_Wk': _L1_xattn_in['Wk'], 'L1_xattn_bk': _L1_xattn_in['bk'], 'L1_xattn_Wv': _L1_xattn_in['Wv'], 'L1_xattn_bv': _L1_xattn_in['bv'], 'L1_ffn_ln_gamma': _L1_ffn_in['ln_gamma'], 'L1_ffn_ln_beta': _L1_ffn_in['ln_beta'], 'L1_ffn_Wr': _L1_ffn_in['Wr'], 'L1_ffn_W12': _L1_ffn_in['W12'], 'L1_ffn_W3': _L1_ffn_in['W3']}

def reference(x, ctx_1024, mask_BxS2_ff1, mask_BxS2_ik0, g_xattn, g_ffn, L0_xattn_wq, L0_xattn_wk, L0_xattn_wv, L0_xattn_ln_gamma, L0_xattn_ln_beta, L0_xattn_dense_w, L0_xattn_dense_b, L0_ffn_router_w, L0_ffn_w1, L0_ffn_b1, L0_ffn_w2, L0_ffn_b2, L0_ffn_sw1, L0_ffn_sb1, L0_ffn_sw2, L0_ffn_sb2, L1_xattn_Wq, L1_xattn_bq, L1_xattn_Wk, L1_xattn_bk, L1_xattn_Wv, L1_xattn_bv, L1_ffn_ln_gamma, L1_ffn_ln_beta, L1_ffn_Wr, L1_ffn_W12, L1_ffn_W3):
    import jax
    import jax.numpy as jnp

    def _L0_xattn_ref(q, k, v, mask, wq, wk, wv, ln_gamma, ln_beta, dense_w, dense_b):
        import jax, jax.numpy as jnp
        import numpy as np
        D_MODEL = 128
        HEADS = 16
        DEPTH = D_MODEL // HEADS
        B, S = (4, 512)
        EPS_K = 1e-06
        EPS_LN = 1e-06

        def _layernorm(x, g, b):
            m = jnp.mean(x, axis=-1, keepdims=True)
            var = jnp.var(x, axis=-1, keepdims=True)
            return (x - m) * jax.lax.rsqrt(var + EPS_LN) * g + b

        def _split_heads(x):
            bsz, sl, _ = x.shape
            return x.reshape(bsz, sl, HEADS, DEPTH).transpose(0, 2, 1, 3)
        bsz = q.shape[0]
        em = mask[:, None, :, None]
        qh = _split_heads(_layernorm(q @ wq, ln_gamma, ln_beta))
        kh = _split_heads(_layernorm(k @ wk, ln_gamma, ln_beta))
        vh = _split_heads(_layernorm(v @ wv, ln_gamma, ln_beta))
        q_prime = jax.nn.relu(qh) + EPS_K
        k_prime = (jax.nn.relu(kh) + EPS_K) * em
        vh = vh * em
        kv = jnp.einsum('bhnd,bhne->bhde', k_prime, vh)
        z = 1.0 / (jnp.einsum('bhnd,bhd->bhn', q_prime, k_prime.sum(axis=-2)) + EPS_K)
        att = jnp.einsum('bhnd,bhde,bhn->bhne', q_prime, kv, z)
        att = att.reshape(bsz, -1, D_MODEL)
        out = att @ dense_w + dense_b
        return _layernorm(out, ln_gamma, ln_beta)

    def _L0_ffn_ref(hidden_states, router_w, w1, b1, w2, b2, sw1, sb1, sw2, sb2):
        import math
        import jax, jax.numpy as jnp
        import numpy as np
        H = 128
        F = 512
        E = 8
        TOP_K = 2
        CAP_FACTOR = 1.25
        MIN_CAP = 4
        SHARED_SCALE = 0.1

        def _top2_gating(logits, capacity):
            N, nE = logits.shape
            gates = jax.nn.softmax(logits, axis=-1)
            idx1 = jnp.argmax(gates, axis=-1)
            mask1 = jax.nn.one_hot(idx1, nE, dtype=gates.dtype)
            idx2 = jnp.argmax(gates * (1.0 - mask1), axis=-1)
            mask2 = jax.nn.one_hot(idx2, nE, dtype=gates.dtype)
            pos1 = jnp.cumsum(mask1, axis=0) - mask1
            mask1 = mask1 * (pos1 < capacity)
            pos2 = jnp.cumsum(mask2, axis=0) - mask2 + jnp.sum(mask1, axis=0, keepdims=True)
            mask2 = mask2 * (pos2 < capacity)
            g1 = jnp.sum(gates * mask1, axis=-1)
            g2 = jnp.sum(gates * mask2, axis=-1)
            denom = jnp.maximum(g1 + g2, jnp.finfo(gates.dtype).eps)
            g1, g2 = (g1 / denom, g2 / denom)
            loc1 = jnp.sum(pos1 * mask1, axis=-1).astype(jnp.int32)
            loc2 = jnp.sum(pos2 * mask2, axis=-1).astype(jnp.int32)
            oh1 = jax.nn.one_hot(loc1, capacity, dtype=gates.dtype)
            oh2 = jax.nn.one_hot(loc2, capacity, dtype=gates.dtype)
            combine = (g1[:, None] * mask1)[:, :, None] * oh1[:, None, :] + (g2[:, None] * mask2)[:, :, None] * oh2[:, None, :]
            dispatch = (combine > 0).astype(gates.dtype)
            return (combine, dispatch)
        B, S, h = hidden_states.shape
        x = hidden_states.reshape(-1, h)
        N = x.shape[0]
        capacity = min(max(MIN_CAP, math.ceil(TOP_K * CAP_FACTOR * N / E)), N)
        logits = x @ router_w
        combine, dispatch = _top2_gating(logits, capacity)
        expert_in = jnp.einsum('nec,nh->ech', dispatch, x)
        hmid = jax.nn.silu(jnp.einsum('ech,ehf->ecf', expert_in, w1) + b1[:, None, :])
        expert_out = jnp.einsum('ecf,efh->ech', hmid, w2) + b2[:, None, :]
        y = jnp.einsum('nec,ech->nh', combine, expert_out)
        shared = jax.nn.silu(x @ sw1 + sb1) @ sw2 + sb2
        out = y + SHARED_SCALE * shared
        return out.reshape(B, S, h)

    def _L1_xattn_ref(hm_tokens, text_tokens, text_mask, Wq, bq, Wk, bk, Wv, bv):
        import jax, jax.numpy as jnp
        import numpy as np
        D = 128
        NEG = -1000000000.0
        d = hm_tokens.shape[-1]
        Q = hm_tokens @ Wq + bq
        K = text_tokens @ Wk + bk
        V = text_tokens @ Wv + bv
        scores = jnp.einsum('bqd,bkd->bqk', Q, K) / jnp.sqrt(jnp.float32(d))
        scores = jnp.where(text_mask[:, None, :] == 0, jnp.float32(NEG), scores)
        attn = jax.nn.softmax(scores, axis=-1)
        return jnp.einsum('bqk,bkd->bqd', attn, V)

    def _L1_ffn_ref(x, ln_gamma, ln_beta, Wr, W12, W3):
        import math
        import jax, jax.numpy as jnp
        import numpy as np
        D_MODEL = 128
        D_FF = 512
        E = 8
        K = 2
        CF = 1.25
        CLAMP = 10000.0
        B, S, D = x.shape
        T = B * S
        xf = x.reshape(T, D)
        mu = xf.mean(-1, keepdims=True)
        var = ((xf - mu) ** 2).mean(-1, keepdims=True)
        xn = (xf - mu) / jnp.sqrt(var + 1e-05) * ln_gamma + ln_beta
        logits = jnp.clip(xn @ Wr.T, -CLAMP, CLAMP)
        m = logits.max(-1, keepdims=True)
        ex = jnp.exp(logits - m)
        probs = ex / (ex.sum(-1, keepdims=True) + 1e-12)
        top_p, top_i = jax.lax.top_k(probs, K)
        Sslots = T * K
        experts = top_i.reshape(-1)
        weights = top_p.reshape(-1)
        tokens = jnp.repeat(jnp.arange(T, dtype=jnp.int32), K)
        order = jnp.argsort(experts, stable=True)
        e_s = experts[order]
        w_s = weights[order]
        t_s = tokens[order]
        counts = jnp.bincount(e_s, length=E)
        offsets = jnp.concatenate([jnp.zeros((1,), counts.dtype), jnp.cumsum(counts)])
        rank = jnp.arange(Sslots, dtype=counts.dtype) - offsets[e_s]
        cap = max(1, math.ceil(math.ceil(T * K * CF) / E))
        kept = rank < cap
        pos = jnp.where(kept, rank, cap)
        buf = jnp.zeros((E, cap, D), x.dtype).at[e_s, pos].set(xn[t_s], mode='drop')
        gu = jnp.einsum('ecd,efd->ecf', buf, W12)
        g, u = (gu[..., :D_FF], gu[..., D_FF:])
        h = jax.nn.silu(g) * u
        y = jnp.einsum('ecf,edf->ecd', h, W3)
        y_slot = y[e_s, jnp.minimum(pos, cap - 1)] * (w_s * kept.astype(x.dtype))[:, None]
        out = jnp.zeros((T, D), x.dtype).at[t_s].add(y_slot)
        return out.reshape(B, S, D)
    x = x + jnp.tanh(g_xattn[0]) * _L0_xattn_ref(_layernorm(x, axis=-1), ctx_1024, ctx_1024, mask_BxS2_ff1, L0_xattn_wq, L0_xattn_wk, L0_xattn_wv, L0_xattn_ln_gamma, L0_xattn_ln_beta, L0_xattn_dense_w, L0_xattn_dense_b)
    x = x + jnp.tanh(g_ffn[0]) * _L0_ffn_ref(_layernorm(x, axis=-1), L0_ffn_router_w, L0_ffn_w1, L0_ffn_b1, L0_ffn_w2, L0_ffn_b2, L0_ffn_sw1, L0_ffn_sb1, L0_ffn_sw2, L0_ffn_sb2)
    x = x + jnp.tanh(g_xattn[1]) * _L1_xattn_ref(_layernorm(x, axis=-1), ctx_1024, mask_BxS2_ik0, L1_xattn_Wq, L1_xattn_bq, L1_xattn_Wk, L1_xattn_bk, L1_xattn_Wv, L1_xattn_bv)
    x = x + jnp.tanh(g_ffn[1]) * _L1_ffn_ref(_layernorm(x, axis=-1), L1_ffn_ln_gamma, L1_ffn_ln_beta, L1_ffn_Wr, L1_ffn_W12, L1_ffn_W3)
    return x

_drawn_inputs = setup_inputs


def setup_inputs(seed=0):
    import zlib

    import numpy as np

    out = dict(_drawn_inputs(seed))
    spreads = {'g_ffn': (-1.0, 0.6),
     'L0_xattn_ln_gamma': (1.0, 0.2),
     'L0_xattn_ln_beta': (0.0, 0.1),
     'L0_xattn_dense_b': (0.0, 0.1),
     'L1_xattn_bq': (0.0, 0.481),
     'L1_xattn_bk': (0.0, 2.0),
     'L1_xattn_bv': (0.0, 0.1),
     'L1_ffn_ln_gamma': (1.0, 0.6),
     'L1_ffn_ln_beta': (0.0, 0.8)}
    factors = {'L0_ffn_b1': 8.0,
     'L0_ffn_b2': 5.689,
     'L0_ffn_sw1': 5.961,
     'L0_ffn_sb1': 8.0,
     'L0_ffn_sw2': 5.752,
     'L0_ffn_sb2': 26.0,
     'L1_ffn_Wr': 2.997}
    for name, (base, spread) in spreads.items():
        noise = np.random.default_rng([zlib.crc32(name.encode()), seed]).standard_normal(out[name].shape)
        drawn = base * np.exp(spread * noise) if base else spread * noise
        out[name] = jnp.asarray(drawn.astype(out[name].dtype))
    for name, factor in factors.items():
        out[name] = (out[name] * factor).astype(out[name].dtype)
    return out
```

```python
from contextlib import ExitStack

import numpy as np
import concourse.bass as bass
from concourse import mybir

P = 128
D = 128
TOKENS = 2048
TILES = TOKENS // P
SEQ = 64
E = 8
F = 512
FC = F // P
CAP = 640
ST = CAP // P
HALF = CAP // 2
SLOTS = E * CAP
GROUPS = 4
EPS = 1e-5
EPS_L0 = 1e-6
HEAD = 8
WIDTH = (F + FC * D, 2 * F + FC * D)

f32 = mybir.dt.float32
f32r = mybir.dt.float32r
i32 = mybir.dt.int32
u32 = mybir.dt.uint32
ALU = mybir.AluOpType
ACT = mybir.ActivationFunctionType
AX = mybir.AxisListType

SHAPE_COLS = dict(ident=128, before=128, ones=128, heads=128, own=4, rev=E, expert_base=E, restart=2 * E * TILES)
VEC_COLS = dict(gamma=128, beta=128, dense_b=128, bv=128, gamma1=128, beta1=128,
                gamma_t=1, beta_t=1, bq=1, bk=1, gates=4, em=TILES, eps5=1, eps6=1)
W_COLS = dict(wq=128, wkv=256, dense=512, router0=E, wq1=128, wk1=128, wv1=128, router1=E)


def columns(spec):
    at, out = 0, {}
    for k, n in spec.items():
        out[k] = (at, n)
        at += n
    return out, at


class Order:

    def __init__(self, eng, sem, before=0):
        self.eng, self.sem, self.before, self.n = eng, sem, before, 0

    def mark(self, ins):
        ins.then_inc(self.sem, 1)
        self.n += 1
        return self.n

    def wait(self, n=None):
        self.eng.wait_ge(self.sem, self.before + (self.n if n is None else n))

    def wait_apart(self):
        wait_apart(self.eng, self.sem, self.before + self.n)


def build(nc, io, stop=4, debug=None):
    ctx = ExitStack()
    with ctx:
        def sb(name, shape, dt=f32):
            return ctx.enter_context(nc.sbuf_tensor(name, shape, dt))

        def sem(name):
            return ctx.enter_context(nc.semaphore(name))

        class S:
            pass
        s = S()
        s.sem, s.sb = sem, sb
        sc, n_sc = columns(SHAPE_COLS)
        vc, n_vc = columns(VEC_COLS)
        wc, n_wc = columns(W_COLS)
        shape_t = sb("shape_t", [P, n_sc])
        vec_t = sb("vec_t", [P, n_vc])
        w_t = sb("w_t", [P, n_wc])
        s.c = lambda k: shape_t[:, sc[k][0]:sc[k][0] + sc[k][1]]
        s.v = lambda k: vec_t[:, vc[k][0]:vc[k][0] + vc[k][1]]
        s.w = lambda k: w_t[:, wc[k][0]:wc[k][0] + wc[k][1]]
        s.shape_t, s.vec_t, s.w_t = shape_t, vec_t, w_t
        s.X = sb("rows", [P, TILES, D])
        s.XN = sb("normed", [P, TILES, D])
        s.XTH = sb("normed_t_high", [D, TOKENS], f32r)
        s.XTL = sb("normed_t_low", [D, TOKENS], f32r)
        s.LG = sb("logits", [P, TILES, E])
        s.tg = sb("tanh_gates", [P, 4])
        s.ps = [ctx.enter_context(nc.psum_tensor(f"bank{b}", [P, 512], f32)) for b in range(8)]
        s.slot = [sb(f"slot{k}", [P, TILES], u32) for k in range(2)]
        s.fetch = [sb(f"fetch{k}", [P, TILES], u32) for k in range(2)]
        s.share = [sb(f"share{k}", [P, TILES]) for k in range(2)]
        s.bias = sb("bias", [P, (E + 1) * (FC + D)])
        s.warm = sb("warm", [P, 1])
        s.zero = sb("zero", [P, 1280])
        s.zeroed = sem("slots_zeroed")
        wait_apart.carrier = sem("carrier")
        linear_attention(nc, io, s)
        if stop >= 2:
            moe(nc, io, s, 0)
        if stop >= 3:
            softmax_attention(nc, io, s)
        if stop >= 4:
            moe(nc, io, s, 1)
            final(nc, io, s)
        if debug:
            debug(nc, io, s)


def wait_apart(eng, sem, value):
    eng.wait_ge(sem, value)
    eng.sem_inc(wait_apart.carrier, 1)


def row_stats(nc, o, src, st, mv, n, done):
    for j in range(n):
        o.mark(nc.vector.bn_stats(st[:, j, :], src(j)))
    o.wait_apart()
    for j in range(n):
        last = nc.vector.bn_aggr(mv[:, j, :], st[:, j, :])
    last.then_inc(done, 1)


def linear_attention(nc, io, s):
    HD = 2
    sem, sb = s.sem, s.sb
    with ExitStack() as local:
        def lb(name, shape, dt=f32):
            return local.enter_context(nc.sbuf_tensor(name, shape, dt))
        ctxT = [lb(f"a_ctxT{h}", [D, HD * P]) for h in range(2)]
        xn = [lb(f"a_xn{h}", [P, HD, D]) for h in range(2)]
        xnT = [lb(f"a_xnT{h}", [D, HD * P]) for h in range(2)]
        st = [lb(f"a_st{h}", [P, 3 * HD, 6]) for h in range(2)]
        mv = [lb(f"a_mv{h}", [P, 3 * HD, 2]) for h in range(2)]
        rs = [lb(f"a_rs{h}", [P, 3 * HD]) for h in range(2)]
        nm = [lb(f"a_nm{h}", [P, 3 * HD]) for h in range(2)]
        kv = [lb(f"a_kv{h}", [P, HD, 2, D]) for h in range(2)]
        qn = [lb(f"a_qn{h}", [P, HD, D]) for h in range(2)]
        qT = [lb(f"a_qT{h}", [D, HD * P]) for h in range(2)]
        kvb = [lb(f"a_kvb{h}", [D, 2, HD, 2, D]) for h in range(2)]
        den = [lb(f"a_den{h}", [D, HD * P]) for h in range(2)]
        attT = [lb(f"a_attT{h}", [D, HD * P]) for h in range(2)]
        attS = [lb(f"a_attS{h}", [D, HD * P]) for h in range(2)]
        attX = [lb(f"a_attX{h}", [D, 4 * HD * P]) for h in range(2)]
        o1 = [lb(f"a_o{h}", [P, HD, D]) for h in range(2)]
        gB = lb("a_gammaB", [P, D])
        bB = lb("a_betaB", [P, D])
        xb = [lb(f"a_xb{h}", [P, HD, D]) for h in range(2)]
        psT, psKV, psM, psN = s.ps[0:2], s.ps[2:4], s.ps[4:6], s.ps[6:8]

        loaded = [sem(f"a_loaded{k}") for k in range(3)]
        x_in = sem("a_x_in")
        ctx_in = [sem(f"a_ctx_in{h}") for h in range(2)]
        gates_ok, gB_ok = sem("a_gates_ok"), sem("a_gB_ok")
        xn_ok, xnT_ps, xnT_ok = sem("a_xn_ok"), sem("a_xnT_ps"), sem("a_xnT_ok")
        kv_ps, q_ps = sem("a_kv_ps"), sem("a_q_ps")
        stats_ok, kvn_ok, qn_ok, kv_ok = sem("a_stats_ok"), sem("a_kvn_ok"), sem("a_qn_ok"), sem("a_kv_ok")
        qT_ps, qTr_ok, qT_ok = sem("a_qT_ps"), sem("a_qTr_ok"), sem("a_qT_ok")
        m_ps, kvb_ok = sem("a_m_ps"), sem("a_kvb_ok")
        n_ps, att_ok, o_ps = sem("a_n_ps"), sem("a_att_ok"), sem("a_o_ps")
        xb_ok, x1n_ok, x1T_ps, x1T_ok, lg_ps, lg_ok, hl_ok = (sem("a_xb_ok"), sem("a_x1n_ok"), sem("a_x1T_ps"),
                                                             sem("a_x1T_ok"), sem("a_lg_ps"), sem("a_lg_ok"), sem("a_hl_ok"))
        dve_order, pool_order = sem("a_dve_order"), sem("a_pool_order")
        agg_ok, rs_ok = sem("a_agg_ok"), sem("a_rs_ok")
        with nc.Block() as block:
            @block.sync
            def _(sp):
                sp.dma_start(s.X[:, 0:4, :], io["x"].rearrange("(t p) d -> p t d", p=P)[:, 0:4, :]).then_inc(x_in, 16)
                sp.dma_start(s.shape_t[:], io["shape"]).then_inc(loaded[0], 16)
                for h in range(2):
                    sp.dma_start(ctxT[h][:], io["ctxT"][:, 256 * h:256 * h + 256]).then_inc(ctx_in[h], 16)
                with sp.Fori(1, GROUPS) as i:
                    sp.wait_ge(x_in, 16 * i)
                    sp.dma_start(s.X[:, bass.ds(4 * i, 4), :],
                                 io["x"].rearrange("(t p) d -> p t d", p=P)[:, bass.ds(4 * i, 4), :]).then_inc(x_in, 16)
                    for h in range(2):
                        sp.wait_ge(kv_ps, 2 * i - 1 + h)
                        sp.dma_start(ctxT[h][:], io["ctxT"][:, bass.ds(512 * i + 256 * h, 256)]).then_inc(ctx_in[h], 16)

            @block.scalar
            def _(act):
                act.dma_start(s.vec_t[:], io["vec"]).then_inc(loaded[1], 16)
                act.dma_start(s.w_t[:], io["w"]).then_inc(loaded[2], 16)
                act.wait_ge(loaded[1], 16)
                nc.scalar.activation(s.tg[:], s.v("gates"), ACT.Tanh).then_inc(gates_ok, 1)
                with act.Fori(0, GROUPS) as i:
                    def deviation(h, k, n, eps):
                        act.wait_ge(agg_ok, 8 * i + k + 1)
                        nc.scalar.activation(rs[h][:, 0:n], mv[h][:, 0:n, 1], ACT.Sqrt, bias=eps[:, 0:1]).then_inc(rs_ok, 1)

                    for h in range(2):
                        deviation(h, h, HD, s.v("eps5"))
                    for h in range(2):
                        act.wait_ge(xnT_ps, 2 * i + h + 1)
                        nc.scalar.activation(xnT[h][:], psT[h][:, 0:256], ACT.Copy).then_inc(xnT_ok, 1)
                    for h in range(2):
                        deviation(h, 2 + h, 3 * HD, s.v("eps6"))
                    for h in range(2):
                        act.wait_ge(stats_ok, 2 * i + h + 1)
                        for j in range(HD):
                            for c in range(2):
                                n = 2 * j + c
                                last = nc.scalar.activation(kv[h][:, j, c, :], psKV[h][:, 256 * j + 128 * c:256 * j + 128 * c + 128],
                                                            ACT.Identity, bias=nm[h][:, n:n + 1], scale=rs[h][:, n:n + 1])
                        last.then_inc(kvn_ok, 1)
                        for j in range(HD):
                            n = 4 + j
                            last = nc.scalar.activation(qn[h][:, j, :], psT[h][:, 256 + 128 * j:384 + 128 * j],
                                                        ACT.Identity, bias=nm[h][:, n:n + 1], scale=rs[h][:, n:n + 1])
                        last.then_inc(qn_ok, 1)
                    for h in range(2):
                        act.wait_ge(qT_ps, 2 * i + h + 1)
                        nc.scalar.activation(qT[h][:], psT[h][:, 0:256], ACT.Relu,
                                             bias=s.v("beta_t"), scale=s.v("gamma_t")).then_inc(qTr_ok, 1)
                    for h in range(2):
                        deviation(h, 4 + h, HD, s.v("eps6"))
                    for h in range(2):
                        deviation(h, 6 + h, HD, s.v("eps5"))
                    for h in range(2):
                        act.wait_ge(x1T_ps, 2 * i + h + 1)
                        nc.scalar.activation(xnT[h][:], psT[h][:, 0:256], ACT.Copy).then_inc(x1T_ok, 1)
                    for h in range(2):
                        act.wait_ge(lg_ps, 2 * i + h + 1)
                        nc.scalar.activation(s.LG[:, bass.ds(4 * i + 2 * h, 2), :],
                                             psT[h][:, 256:256 + 2 * E].rearrange("p (t e) -> p t e", e=E), ACT.Copy).then_inc(lg_ok, 1)

            @block.gpsimd
            def _(pool):
                o = Order(pool, pool_order)
                o.mark(nc.gpsimd.memset(s.zero[:], 0.0))
                o.wait()
                for k in range(2):
                    for c in range(4):
                        pool.dma_start(io[f"slots{k}"].rearrange("(c p a) d -> c p (a d)", c=4, p=P)[c, :, :], s.zero[:]).then_inc(s.zeroed, 16)
                pool.wait_ge(gates_ok, 1)
                pool.wait_ge(loaded[1], 16)
                nc.gpsimd.tensor_scalar(gB[:], s.v("gamma"), s.tg[:, 0:1], None, ALU.mult)
                nc.gpsimd.tensor_scalar(bB[:], s.v("beta"), s.tg[:, 0:1], None, ALU.mult).then_inc(gB_ok, 1)
                pool.wait_ge(gB_ok, 1)
                PO = 6
                with pool.Fori(0, GROUPS) as i:
                    o = Order(pool, pool_order, PO * i + 1)

                    for h in range(2):
                        pool.wait_ge(kvn_ok, 2 * i + h + 1)
                        kvf = kv[h][:].rearrange("p t c d -> p (t c) d")
                        gb = s.v("gamma").unsqueeze(1).broadcast_to([P, 2 * HD, D])
                        bb = s.v("beta").unsqueeze(1).broadcast_to([P, 2 * HD, D])
                        nmask = s.v("em")[:, bass.ds(4 * i + 2 * h, 2)].unsqueeze(2).broadcast_to([P, HD, 2 * D])
                        o.mark(nc.gpsimd.tensor_tensor(kvf, kvf, gb, ALU.mult))
                        o.wait()
                        o.mark(nc.gpsimd.tensor_tensor(kvf, kvf, bb, ALU.add))
                        o.wait_apart()
                        o.mark(nc.gpsimd.tensor_scalar(kv[h][:, :, 0, :], kv[h][:, :, 0, :], 0.0, 1e-6, ALU.max, ALU.add))
                        o.wait()
                        kvm = kv[h][:].rearrange("p t c d -> p t (c d)")
                        nc.gpsimd.tensor_tensor(kvm, kvm, nmask, ALU.mult).then_inc(kv_ok, 1)
                    for h in range(2):
                        wait_apart(pool, qTr_ok, 2 * i + h + 1)
                        nc.gpsimd.tensor_scalar(qT[h][:], qT[h][:], 1e-6, None, ALU.add).then_inc(qT_ok, 1)
                        wait_apart(pool, x_in, 16 * i + 16)
                        nc.gpsimd.tensor_tensor(xb[h][:], s.X[:, bass.ds(4 * i + 2 * h, 2), :],
                                                bB[:].unsqueeze(1).broadcast_to([P, HD, D]), ALU.add).then_inc(xb_ok, 1)
                    for h in range(2):
                        wait_apart(pool, x1T_ok, 2 * i + h + 1)
                        at = bass.ds(512 * i + 256 * h, 256)
                        nc.gpsimd.tensor_copy(s.XTH[:, at], xnT[h][:]).then_inc(hl_ok, 1)
                        wait_apart(pool, hl_ok, 4 * i + 2 * h + 1)
                        nc.gpsimd.tensor_tensor(s.XTL[:, at], xnT[h][:], s.XTH[:, at].bitcast(f32), ALU.subtract).then_inc(hl_ok, 1)
                    assert o.n == PO, o.n
                pool.wait_ge(s.zeroed, 16 * 8)

            @block.vector
            def _(dve):
                dve.wait_ge(loaded[1], 16)
                dve.wait_ge(loaded[0], 16)
                DO = 52
                with dve.Fori(0, GROUPS) as i:
                    o = Order(dve, dve_order, DO * i)
                    wait_apart(dve, x_in, 16 * i + 16)
                    tile = lambda h, j: s.X[:, bass.ds(4 * i + 2 * h + j, 1), :].rearrange("p a d -> p (a d)")

                    def inverse(h, k, n):
                        dve.wait_ge(rs_ok, 8 * i + k + 1)
                        o.mark(nc.vector.reciprocal(rs[h][:, 0:n], rs[h][:, 0:n]))
                        o.wait()

                    def normalise(h, k):
                        inverse(h, k, HD)
                        for j in range(HD):
                            last = nc.vector.tensor_scalar(xn[h][:, j, :], tile(h, j), mv[h][:, j, 0:1], rs[h][:, j:j + 1],
                                                           ALU.subtract, ALU.mult)
                        return last

                    for h in range(2):
                        row_stats(nc, o, lambda j: tile(h, j), st[h], mv[h], HD, agg_ok)
                    for h in range(2):
                        normalise(h, h).then_inc(xn_ok, 1)
                    for h in range(2):
                        wait_apart(dve, kv_ps, 2 * i + h + 1)
                        wait_apart(dve, q_ps, 2 * i + h + 1)
                        row_stats(nc, o, lambda n: psKV[h][:, 128 * n:128 * n + 128] if n < 4 else
                                  psT[h][:, 128 * n - 256:128 * n - 128], st[h], mv[h], 6, agg_ok)
                    for h in range(2):
                        inverse(h, 2 + h, 3 * HD)
                        nc.vector.scalar_tensor_tensor(nm[h][:], mv[h][:, :, 0], -1.0, rs[h][:], ALU.mult, ALU.mult).then_inc(stats_ok, 1)
                    for h in range(2):
                        dve.wait_ge(m_ps, 2 * i + h + 1)
                        for b in range(2):
                            last = nc.vector.tensor_tensor(kvb[h][:, b, :, :, :].rearrange("d t c e -> d (t c) e"),
                                                           psM[b][:].rearrange("d (t e) -> d t e", e=D),
                                                           s.c("heads").unsqueeze(1).broadcast_to([D, 4, D]), ALU.mult)
                        last.then_inc(kvb_ok, 1)
                    for h in range(2):
                        dve.wait_ge(n_ps, 2 * i + h + 1)
                        o.mark(nc.vector.tensor_scalar(den[h][:], psN[h][:, 256:512], 1e-6, None, ALU.add))
                        o.wait()
                        o.mark(nc.vector.reciprocal(den[h][:], den[h][:]))
                        o.wait()
                        o.mark(nc.vector.tensor_tensor(attT[h][:], psN[h][:, 0:256], den[h][:], ALU.mult))
                        o.wait()
                        for q in range(4):
                            for a in range(4):
                                src = attT[h][32 * q:32 * q + 32, :].rearrange("p (j n a b) -> p a b j n", j=2 * HD, n=4, a=4)[:, a]
                                dst = attS[h][32 * a:32 * a + 32, :].rearrange("p (b j q n) -> p q b j n", b=4, j=2 * HD, q=4)[:, q]
                                last = nc.vector.tensor_copy(dst, src)
                        o.mark(last)
                        o.wait()
                        nc.vector.tensor_tensor(attX[h][:].rearrange("p (m h n) -> p m h n", h=4, n=4),
                                                attS[h][:].rearrange("p (m n) -> p m n", n=4).unsqueeze(2).broadcast_to([P, 64, 4, 4]),
                                                s.c("own").unsqueeze(1).unsqueeze(3).broadcast_to([P, 64, 4, 4]), ALU.mult).then_inc(att_ok, 1)
                    for h in range(2):
                        dve.wait_ge(o_ps, 2 * i + h + 1)
                        o.mark(nc.vector.tensor_tensor(o1[h][:], psT[h][:, 0:256].rearrange("p (t d) -> p t d", d=D),
                                                       s.v("dense_b").unsqueeze(1).broadcast_to([P, HD, D]), ALU.add))
                        o.wait_apart()
                        row_stats(nc, o, lambda j: o1[h][:, j, :], st[h], mv[h], HD, agg_ok)
                    for h in range(2):
                        if h == 0:
                            dve.wait_ge(gB_ok, 1)
                        inverse(h, 4 + h, HD)
                        for j in range(HD):
                            o.mark(nc.vector.scalar_tensor_tensor(o1[h][:, j, :], o1[h][:, j, :], mv[h][:, j, 0:1], gB[:],
                                                                  ALU.subtract, ALU.mult))
                        dve.wait_ge(xb_ok, 2 * i + h + 1)
                        o.wait()
                        for j in range(HD):
                            o.mark(nc.vector.scalar_tensor_tensor(tile(h, j), o1[h][:, j, :], rs[h][:, j:j + 1], xb[h][:, j, :],
                                                                  ALU.mult, ALU.add))
                        o.wait_apart()
                        row_stats(nc, o, lambda j: tile(h, j), st[h], mv[h], HD, agg_ok)
                    for h in range(2):
                        normalise(h, 6 + h).then_inc(x1n_ok, 1)
                        dve.wait_ge(x1n_ok, 2 * i + h + 1)
                        o.mark(nc.vector.tensor_copy(s.XN[:, bass.ds(4 * i + 2 * h, 2), :], xn[h][:]))
                    o.wait()
                    assert o.n == DO, o.n

            @block.tensor
            def _(pe):
                pe.wait_ge(loaded[0], 16)
                pe.wait_ge(loaded[2], 16)
                with pe.Fori(0, GROUPS) as i:
                    for h in range(2):
                        pe.wait_ge(xn_ok, 2 * i + h + 1)
                        for j in range(HD):
                            last = nc.tensor.transpose(psT[h][:, 128 * j:128 * j + 128], xn[h][:, j, :], s.c("ident"))
                        last.then_inc(xnT_ps, 1)
                    for h in range(2):
                        pe.wait_ge(ctx_in[h], 16 * i + 16)
                        for j in range(HD):
                            last = nc.tensor.matmul(psKV[h][:, 256 * j:256 * j + 256], ctxT[h][:, 128 * j:128 * j + 128],
                                                    s.w("wkv"), start=True, stop=True)
                        last.then_inc(kv_ps, 1)
                    for h in range(2):
                        pe.wait_ge(xnT_ok, 2 * i + h + 1)
                        for j in range(HD):
                            last = nc.tensor.matmul(psT[h][:, 256 + 128 * j:384 + 128 * j], xnT[h][:, 128 * j:128 * j + 128],
                                                    s.w("wq"), start=True, stop=True)
                        last.then_inc(q_ps, 1)
                    for h in range(2):
                        pe.wait_ge(qn_ok, 2 * i + h + 1)
                        for j in range(HD):
                            last = nc.tensor.transpose(psT[h][:, 128 * j:128 * j + 128], qn[h][:, j, :], s.c("ident"))
                        last.then_inc(qT_ps, 1)
                    for h in range(2):
                        pe.wait_ge(kv_ok, 2 * i + h + 1)
                        if h:
                            pe.wait_ge(kvb_ok, 2 * i + 1)
                        for j in range(HD):
                            for b in range(2):
                                rows = slice(SEQ * b, SEQ * b + SEQ)
                                nc.tensor.matmul(psM[b][:, 256 * j:256 * j + 128], kv[h][rows, j, 0, :], kv[h][rows, j, 1, :],
                                                 start=True, stop=True)
                                last = nc.tensor.matmul(psM[b][:, 256 * j + 128:256 * j + 256], kv[h][rows, j, 0, :],
                                                        s.c("ones")[rows, :], start=True, stop=True)
                        last.then_inc(m_ps, 1)
                    for h in range(2):
                        pe.wait_ge(kvb_ok, 2 * i + h + 1)
                        pe.wait_ge(qT_ok, 2 * i + h + 1)
                        for j in range(HD):
                            for b in range(2):
                                for c in range(2):
                                    at = 128 * j + SEQ * b
                                    last = nc.tensor.matmul(psN[h][:, 256 * c + at:256 * c + at + SEQ], kvb[h][:, b, j, c, :],
                                                            qT[h][:, at:at + SEQ], start=True, stop=True)
                        last.then_inc(n_ps, 1)
                    for h in range(2):
                        pe.wait_ge(att_ok, 2 * i + h + 1)
                        for j in range(HD):
                            for b in range(4):
                                last = nc.tensor.matmul(psT[h][:, 128 * j:128 * j + 128], attX[h][:, 256 * b + 128 * j:256 * b + 128 * j + 128],
                                                        s.w("dense")[:, 128 * b:128 * b + 128], start=b == 0, stop=b == 3)
                        last.then_inc(o_ps, 1)
                    for h in range(2):
                        pe.wait_ge(x1n_ok, 2 * i + h + 1)
                        for j in range(HD):
                            last = nc.tensor.transpose(psT[h][:, 128 * j:128 * j + 128], xn[h][:, j, :], s.c("ident"))
                        last.then_inc(x1T_ps, 1)
                    for h in range(2):
                        pe.wait_ge(x1T_ok, 2 * i + h + 1)
                        for j in range(HD):
                            last = nc.tensor.matmul(psT[h][:, 256 + E * j:256 + E * j + E], xnT[h][:, 128 * j:128 * j + 128],
                                                    s.w("router0"), start=True, stop=True)
                        last.then_inc(lg_ps, 1)
                    for h in range(2):
                        pe.wait_ge(lg_ok, 2 * i + h + 1)
                        pe.wait_ge(hl_ok, 4 * i + 2 * h + 2)


def moe(nc, io, s, layer):
    route(nc, io, s, layer)
    experts(nc, io, s, layer)


def route(nc, io, s, layer):
    sem = s.sem
    pre = f"g{layer}_"
    with ExitStack() as local:
        def lb(name, shape, dt=f32):
            return local.enter_context(nc.sbuf_tensor(pre + name, shape, dt))
        TE = TILES * E
        top, total, inv, rank = (lb(n, [P, TILES]) for n in ("top", "total", "inv", "rank"))
        ex, gate, cand = (lb(n, [P, TILES, E]) for n in ("ex", "gate", "cand"))
        mask, pos, keep, val = (lb(n, [P, 2, TILES, E]) for n in ("mask", "pos", "keep", "val"))
        per_tile, upto = lb("per_tile", [P, 2, E, TILES]), lb("upto", [P, 2, E, TILES])
        base2 = lb("base2", [P, E])
        kept, slotf, weight = (lb(n, [P, 2, TILES]) for n in ("kept", "slotf", "weight"))
        psR = s.ps[0]
        sh_ok, ex_ok, mask_ok, r_ps, slots_ok = (sem(pre + n) for n in ("sh_ok", "ex_ok", "mask_ok", "r_ps", "slots_ok"))
        order, scattered = sem(pre + "order"), sem(pre + "scattered")
        if layer == 0:
            raw = lb("raw", [P, 2 * F])
            wh, wl = lb("wh", [P, 2 * F], f32r), lb("wl", [P, 2 * F], f32r)
            hf, hh, hl = lb("hf", [P, FC, 512]), lb("hh", [P, FC, 512], f32r), lb("hl", [P, FC, 512], f32r)
            c, cb2 = lb("c", [P, 1]), lb("cb2", [P, D])
            hb, psY = s.ps[1:5], s.ps[5:7]
            w_in, b_in, wh_ok, wl_ok = (sem(pre + n) for n in ("w_in", "b_in", "wh_ok", "wl_ok"))
            h_ps, hf_ok, hh_ok, hl_ok, y_ps, y_ok = (sem(pre + n) for n in ("h_ps", "hf_ok", "hh_ok", "hl_ok", "y_ps", "y_ok"))
        with nc.Block() as block:
            @block.sync
            def _(sp):
                if layer == 0:
                    sp.dma_start(raw[:], io["experts0"][E, :, :]).then_inc(w_in, 16)
                    sp.dma_start(s.bias[:], io["bias0"]).then_inc(b_in, 16)
                    sp.wait_ge(w_in, 16)
                    sp.wait_ge(b_in, 16)

            @block.scalar
            def _(act):
                if layer == 0:
                    act.wait_ge(w_in, 16)
                    nc.scalar.activation(wh[:], raw[:], ACT.Copy).then_inc(wh_ok, 1)
                act.wait_ge(sh_ok, 1)
                nc.scalar.activation(ex[:], ex[:], ACT.Exp).then_inc(ex_ok, 1)
                if layer == 0:
                    act.wait_ge(b_in, 16)
                    nc.scalar.activation(s.warm[:], s.c("ones")[:, 0:1], ACT.Silu)
                    with act.Fori(0, TOKENS // 512) as i:
                        for k in range(FC):
                            act.wait_ge(h_ps, FC * i + k + 1)
                            nc.scalar.activation(hf[:, k, :], hb[k][:], ACT.Silu, bias=s.bias[:, FC * E + k:FC * E + k + 1]).then_inc(hf_ok, 1)
                            act.wait_ge(hf_ok, FC * i + k + 1)
                            nc.scalar.activation(hh[:, k, :], hf[:, k, :], ACT.Copy).then_inc(hh_ok, 1)

            @block.gpsimd
            def _(pool):
                pool.wait_ge(slots_ok, 1)
                for t in range(TILES):
                    for k in range(2):
                        pool.indirect_dma_start(out=io[f"slots{layer}"], out_offset=bass.IndirectOffsetOnAxis(ap=s.slot[k][:, t:t + 1], axis=0),
                                                in_=s.XN[:, t, :], in_offset=None, bounds_check=SLOTS - 1, oob_is_err=False).then_inc(scattered, 16)
                pool.wait_ge(scattered, 16 * 2 * TILES)

            @block.vector
            def _(dve):
                o = Order(dve, order)

                def step(ins):
                    o.mark(ins)
                    o.wait()

                def b3(t):
                    return t.unsqueeze(2).broadcast_to([P, TILES, E])

                def rows(c):
                    return s.c(c).unsqueeze(1).broadcast_to([P, TILES, E])

                V = nc.vector
                logits = s.LG[:]
                if layer == 1:
                    step(V.tensor_scalar(logits, logits, -1e4, 1e4, ALU.max, ALU.min))
                step(V.tensor_reduce(top[:], logits, AX.X, ALU.max))
                V.tensor_tensor(ex[:], logits, b3(top[:]), ALU.subtract).then_inc(sh_ok, 1)
                if layer == 0:
                    dve.wait_ge(wh_ok, 1)
                    V.tensor_tensor(wl[:], raw[:], wh[:].bitcast(f32), ALU.subtract).then_inc(wl_ok, 1)
                    step(V.tensor_scalar(c[:], s.tg[:, 2:3], 0.1, None, ALU.mult))
                    dve.wait_ge(b_in, 16)
                    step(V.tensor_scalar(cb2[:], s.bias[:, FC * (E + 1) + D * E:FC * (E + 1) + D * (E + 1)], c[:, 0:1], None, ALU.mult))
                dve.wait_ge(ex_ok, 1)
                step(V.tensor_reduce(total[:], ex[:], AX.X, ALU.add))
                if layer == 1:
                    step(V.tensor_scalar(total[:], total[:], 1e-12, None, ALU.add))
                step(V.reciprocal(inv[:], total[:]))
                step(V.tensor_tensor(gate[:], ex[:], b3(inv[:]), ALU.mult))
                for k in range(2):
                    left = gate if k == 0 else ex
                    if k == 1 and layer == 0:
                        step(V.tensor_tensor(cand[:], gate[:], mask[:, 0], ALU.mult))
                        step(V.tensor_tensor(ex[:], gate[:], cand[:], ALU.subtract))
                    elif k == 1:
                        step(V.scalar_tensor_tensor(ex[:].rearrange("p t e -> p (t e)"), mask[:, 0].rearrange("p t e -> p (t e)"), -2.0,
                                                    gate[:].rearrange("p t e -> p (t e)"), ALU.mult, ALU.add))
                    step(V.tensor_reduce(top[:], left[:], AX.X, ALU.max))
                    step(V.tensor_tensor(cand[:], left[:], b3(top[:]), ALU.is_equal))
                    step(V.tensor_tensor(cand[:], cand[:], rows("rev"), ALU.mult))
                    step(V.tensor_reduce(rank[:], cand[:], AX.X, ALU.max))
                    ins = V.tensor_tensor(mask[:, k], rows("rev"), b3(rank[:]), ALU.is_equal)
                    step(ins) if k == 0 else ins.then_inc(mask_ok, 1)
                dve.wait_ge(r_ps, 1)
                step(V.tensor_copy(per_tile[:, 0], psR[:, 256:384].rearrange("p (t e) -> p e t", t=TILES)))
                step(V.tensor_copy(per_tile[:, 1], psR[:, 384:512].rearrange("p (t e) -> p e t", t=TILES)))
                flat = "p k e t -> p (k e t)"
                step(V.tensor_tensor_scan(upto[:].rearrange(flat), s.c("restart"), per_tile[:].rearrange(flat), 0.0, ALU.mult, ALU.add))
                if layer == 0:
                    step(V.tensor_scalar(base2[:], upto[:, 0, :, TILES - 1], float(CAP), None, ALU.min))
                step(V.tensor_tensor(per_tile[:].rearrange(flat), upto[:].rearrange(flat), per_tile[:].rearrange(flat), ALU.subtract))
                for k in range(2):
                    step(V.tensor_tensor(pos[:, k], psR[:, 128 * k:128 * k + 128].rearrange("p (t e) -> p t e", e=E),
                                         per_tile[:, k].rearrange("p e t -> p t e"), ALU.add))
                if layer == 0:
                    step(V.tensor_tensor(pos[:, 1], pos[:, 1], base2[:].unsqueeze(1).broadcast_to([P, TILES, E]), ALU.add))
                else:
                    step(V.tensor_tensor(pos[:, 0], pos[:, 0], pos[:, 1], ALU.add))
                    step(V.tensor_copy(pos[:, 1], pos[:, 0]))
                all_ = "p k t e -> p (k t) e"
                one = "p k t e -> p (k t e)"
                step(V.scalar_tensor_tensor(keep[:].rearrange(one), pos[:].rearrange(one), float(CAP), mask[:].rearrange(one), ALU.is_lt, ALU.mult))
                step(V.tensor_reduce(kept[:].rearrange("p k t -> p (k t)"), keep[:].rearrange(all_), AX.X, ALU.add))
                step(V.tensor_tensor(val[:].rearrange(all_), pos[:].rearrange(all_), s.c("expert_base").unsqueeze(1).broadcast_to([P, 2 * TILES, E]), ALU.add))
                step(V.tensor_tensor(val[:].rearrange(one), val[:].rearrange(one), keep[:].rearrange(one), ALU.mult))
                step(V.tensor_reduce(slotf[:].rearrange("p k t -> p (k t)"), val[:].rearrange(all_), AX.X, ALU.add))
                for k in range(2):
                    step(V.tensor_copy(s.fetch[k][:], slotf[:, k]))
                step(V.scalar_tensor_tensor(slotf[:].rearrange("p k t -> p (k t)"), kept[:].rearrange("p k t -> p (k t)"), -2.0 * SLOTS,
                                            slotf[:].rearrange("p k t -> p (k t)"), ALU.mult, ALU.add))
                for k in range(2):
                    step(V.tensor_scalar(s.slot[k][:], slotf[:, k], 2.0 * SLOTS, None, ALU.add))
                V.memset(top[:, 0:1], 0.0).then_inc(slots_ok, 1)
                for k in range(2):
                    step(V.tensor_tensor(val[:, k], keep[:, k], gate[:], ALU.mult))
                step(V.tensor_reduce(weight[:].rearrange("p k t -> p (k t)"), val[:].rearrange(all_), AX.X, ALU.add))
                if layer == 0:
                    step(V.tensor_tensor(total[:], weight[:, 0], weight[:, 1], ALU.add))
                    step(V.tensor_scalar(total[:], total[:], float(np.finfo(np.float32).eps), None, ALU.max))
                    step(V.reciprocal(inv[:], total[:]))
                    for k in range(2):
                        step(V.tensor_tensor(weight[:, k], weight[:, k], inv[:], ALU.mult))
                for k in range(2):
                    step(V.tensor_scalar(s.share[k][:], weight[:, k], s.tg[:, 2 + layer:3 + layer], None, ALU.mult))
                if layer == 0:
                    DO = 1
                    done = o.n
                    with dve.Fori(0, TOKENS // 512) as i:
                        p = Order(dve, order, DO * i + done)
                        for k in range(FC):
                            dve.wait_ge(hh_ok, FC * i + k + 1)
                            V.tensor_tensor(hl[:, k, :], hf[:, k, :], hh[:, k, :].bitcast(f32), ALU.subtract).then_inc(hl_ok, 1)
                        dve.wait_ge(y_ps, i + 1)
                        at = bass.ds(4 * i, 4)
                        p.mark(V.scalar_tensor_tensor(s.X[:, at, :].rearrange("p t d -> p (t d)"), psY[0][:], c[:, 0:1],
                                                      s.X[:, at, :].rearrange("p t d -> p (t d)"), ALU.mult, ALU.add))
                        p.wait()
                        V.tensor_tensor(s.X[:, at, :], s.X[:, at, :], cb2[:].unsqueeze(1).broadcast_to([P, 4, D]), ALU.add).then_inc(y_ok, 1)
                        assert p.n == DO

            @block.tensor
            def _(pe):
                pe.wait_ge(mask_ok, 1)
                flat = mask[:].rearrange("p k t e -> p (k t e)")
                nc.tensor.matmul(psR[:, 0:256], s.c("before"), flat, start=True, stop=True)
                nc.tensor.matmul(psR[:, 256:512], s.c("ones"), flat, start=True, stop=True).then_inc(r_ps, 1)
                if layer == 0:
                    pe.wait_ge(wl_ok, 1)
                    with pe.Fori(0, TOKENS // 512) as i:
                        at = bass.ds(512 * i, 512)
                        for k in range(FC):
                            w = slice(P * k, P * k + P)
                            nc.tensor.matmul(hb[k][:], wh[:, w], s.XTH[:, at], start=True, stop=False)
                            nc.tensor.matmul(hb[k][:], wh[:, w], s.XTL[:, at], start=False, stop=False)
                            nc.tensor.matmul(hb[k][:], wl[:, w], s.XTH[:, at], start=False, stop=True).then_inc(h_ps, 1)
                        for k in range(FC):
                            pe.wait_ge(hl_ok, FC * i + k + 1)
                            w = slice(F + D * k, F + D * k + D)
                            for j in range(4):
                                tok, out = slice(P * j, P * j + P), psY[0][:, P * j:P * j + P]
                                nc.tensor.matmul(out, hh[:, k, tok], wh[:, w], start=k == 0 and j == 0, stop=False, skip_group_check=True)
                                nc.tensor.matmul(out, hh[:, k, tok], wl[:, w], start=False, stop=False, skip_group_check=True)
                                last = nc.tensor.matmul(out, hl[:, k, tok], wh[:, w], start=False, stop=k == FC - 1, skip_group_check=True)
                        last.then_inc(y_ps, 1)
                        pe.wait_ge(y_ok, i + 1)


def experts(nc, io, s, layer):
    sem = s.sem
    pre = f"e{layer}_"
    NW = WIDTH[layer]
    W2 = (F, 2 * F)[layer]
    U = 2 * FC
    with ExitStack() as local:
        def lb(name, shape, dt=f32):
            return local.enter_context(nc.sbuf_tensor(pre + name, shape, dt))
        raw = [lb(f"raw{q}", [P, NW]) for q in range(2)]
        wh = [lb(f"wh{q}", [P, NW], f32r) for q in range(2)]
        wl = [lb(f"wl{q}", [P, NW], f32r) for q in range(2)]
        rows = lb("rows", [P, ST, D])
        xh, xl = lb("xh", [D, CAP], f32r), lb("xl", [D, CAP], f32r)
        hf = [lb(f"hf{r}", [P, HALF]) for r in range(4)]
        sg = [lb(f"sg{r}", [P, HALF]) for r in range(4)]
        hh, hl = lb("hh", [P, FC, CAP], f32r), lb("hl", [P, FC, CAP], f32r)
        y = lb("y", [P, ST, D])
        hb, psX, psY = s.ps[0:4], s.ps[4:6], s.ps[6:8]
        w_in = [sem(pre + f"w_in{q}") for q in range(2)]
        rows_in, stored = sem(pre + "rows_in"), sem(pre + "stored")
        wh_ok, wl_ok, x_ps, xh_ok, xl_ok = (sem(pre + n) for n in ("wh_ok", "wl_ok", "x_ps", "xh_ok", "xl_ok"))
        h_ps, sg_ok, hf_ok, hh_ok, hl_ok = (sem(pre + n) for n in ("h_ps", "sg_ok", "hf_ok", "hh_ok", "hl_ok"))
        y_ps, y_free, y_ok = (sem(pre + n) for n in ("y_ps", "y_free", "y_ok"))
        slots, made = io[f"slots{layer}"], io[f"made{layer}"]

        def each(eng, body):
            with eng.Fori(0, E // 2 - 1) as i:
                body(i, 0, True, True)
                body(i, 1, True, True)
            body(E // 2 - 1, 0, True, False)
            body(E // 2 - 1, 1, False, False)

        def expert_rows(dram, e):
            return dram.rearrange("(e s p) d -> e p s d", s=ST, p=P)[bass.ds(e, 1), :, :, :].rearrange("e p s d -> (e p) s d")

        def unit(n):
            return n // 2, slice(HALF * (n % 2), HALF * (n % 2) + HALF)

        with nc.Block() as block:
            @block.sync
            def _(sp):
                weights = io[f"experts{layer}"]
                sp.dma_start(rows[:], expert_rows(slots, 0)).then_inc(rows_in, 16)
                for q in range(2):
                    sp.dma_start(raw[q][:], weights[q, :, :]).then_inc(w_in[q], 16)
                sp.sem_inc(stored, 16)

                def body(i, q, more, two_more):
                    e = 2 * i + q
                    if more:
                        sp.wait_ge(x_ps, e + 1)
                        sp.dma_start(rows[:], expert_rows(slots, e + 1)).then_inc(rows_in, 16)
                    if two_more:
                        sp.wait_ge(wl_ok, e + 1)
                        sp.dma_start(raw[q][:], weights[bass.ds(e + 2, 1), :, :].rearrange("e p n -> (e p) n")).then_inc(w_in[q], 16)
                    sp.wait_ge(y_ok, e + 2)
                    sp.dma_start(expert_rows(made, e), y[:]).then_inc(stored, 16)
                each(sp, body)
                sp.wait_ge(stored, 16 * (E + 1))

            @block.scalar
            def _(act):
                nc.scalar.activation(s.warm[:], s.c("ones")[:, 0:1], ACT.Silu)

                def high(q, turn):
                    act.wait_ge(w_in[q], 16 * turn)
                    nc.scalar.activation(wh[q][:], raw[q][:], ACT.Copy).then_inc(wh_ok, 1)

                def high_rows(e):
                    act.wait_ge(x_ps, e + 1)
                    nc.scalar.activation(xh[:, 0:512], psX[0][:], ACT.Copy)
                    nc.scalar.activation(xh[:, 512:CAP], psX[1][:, 0:P], ACT.Copy).then_inc(xh_ok, 1)

                high(0, 1)
                high_rows(0)

                def body(i, q, more, two_more):
                    e = 2 * i + q
                    for n in range(U):
                        k, _ = unit(n)
                        act.wait_ge(h_ps, U * e + n + 1)
                        if layer == 0:
                            if n >= 4:
                                act.wait_ge(hl_ok, U * e + n - 3)
                            act.sem_inc(wait_apart.carrier, 1)
                            nc.scalar.activation(hf[n % 4][:], hb[n % 4][:, 0:HALF], ACT.Silu,
                                                 bias=s.bias[:, bass.ds(FC * e + k, 1)]).then_inc(hf_ok, 1)
                        else:
                            if n >= 4:
                                act.wait_ge(hf_ok, U * e + n - 3)
                            nc.scalar.activation(sg[n % 4][:], hb[2 * (n % 2)][:, 0:HALF], ACT.Silu).then_inc(sg_ok, 1)
                        if n == 5 and more:
                            high(1 - q, i + 1 + q)
                    if more:
                        high_rows(e + 1)
                each(act, body)

            @block.gpsimd
            def _(pool):
                def low(e, q):
                    pool.wait_ge(wh_ok, e + 1)
                    nc.gpsimd.tensor_tensor(wl[q][:], raw[q][:], wh[q][:].bitcast(f32), ALU.subtract).then_inc(wl_ok, 1)

                low(0, 0)

                def body(i, q, more, two_more):
                    e = 2 * i + q
                    for n in range(U):
                        k, half = unit(n)
                        wait_apart(pool, hf_ok, U * e + n + 1)
                        nc.gpsimd.tensor_scalar(hh[:, k, half], hf[n % 4][:], 1.0, None, ALU.mult).then_inc(hh_ok, 1)
                        if n == 6 and more:
                            low(e + 1, 1 - q)
                each(pool, body)

            @block.vector
            def _(dve):
                def low_rows(e):
                    dve.wait_ge(xh_ok, e + 1)
                    nc.vector.tensor_tensor(xl[:, 0:512], psX[0][:], xh[:, 0:512].bitcast(f32), ALU.subtract)
                    nc.vector.tensor_tensor(xl[:, 512:CAP], psX[1][:, 0:P], xh[:, 512:CAP].bitcast(f32), ALU.subtract).then_inc(xl_ok, 1)

                def low_hidden(e, n):
                    k, half = unit(n)
                    dve.wait_ge(hh_ok, U * e + n + 1)
                    nc.vector.tensor_tensor(hl[:, k, half], hf[n % 4][:], hh[:, k, half].bitcast(f32), ALU.subtract).then_inc(hl_ok, 1)

                dve.sem_inc(y_ok, 1)
                low_rows(0)

                def body(i, q, more, two_more):
                    e = 2 * i + q
                    for n in range(U + 1):
                        if layer == 1 and n < U:
                            dve.wait_ge(sg_ok, U * e + n + 1)
                            nc.vector.tensor_tensor(hf[n % 4][:], sg[n % 4][:], hb[2 * (n % 2) + 1][:, 0:HALF], ALU.mult).then_inc(hf_ok, 1)
                        if n:
                            low_hidden(e, n - 1)
                    if more:
                        low_rows(e + 1)
                    dve.wait_ge(y_ps, e + 1)
                    dve.wait_ge(stored, 16 * e + 16)
                    if layer == 0:
                        b2 = s.bias[:, bass.ds(FC * (E + 1) + D * e, D)].unsqueeze(1)
                        nc.vector.tensor_tensor(y[:, 0:4, :], psY[0][:].rearrange("p (s d) -> p s d", d=D), b2.broadcast_to([P, 4, D]), ALU.add)
                        nc.vector.tensor_tensor(y[:, 4:5, :], psY[1][:, 0:D].rearrange("p (s d) -> p s d", d=D), b2, ALU.add).then_inc(y_ok, 1)
                    else:
                        nc.vector.tensor_copy(y[:, 0:4, :], psY[0][:].rearrange("p (s d) -> p s d", d=D))
                        nc.vector.tensor_copy(y[:, 4, :], psY[1][:, 0:D]).then_inc(y_ok, 1)
                each(dve, body)

            @block.tensor
            def _(pe):
                def transpose_rows(e):
                    pe.wait_ge(rows_in, 16 * e + 16)
                    for j in range(ST):
                        last = nc.tensor.transpose(psX[j // 4][:, P * (j % 4):P * (j % 4) + P], rows[:, j, :], s.c("ident"))
                    last.then_inc(x_ps, 1)

                def hidden(e, q, n):
                    k, half = unit(n)
                    ring = 4 if layer == 0 else 2
                    if n >= ring:
                        pe.wait_ge(hf_ok, U * e + n - ring + 1)
                    for g in range(1 + layer):
                        bank = hb[n % 4] if layer == 0 else hb[2 * (n % 2) + g]
                        w = slice(F * g + P * k, F * g + P * k + P)
                        nc.tensor.matmul(bank[:, 0:HALF], wh[q][:, w], xh[:, half], start=True, stop=False)
                        nc.tensor.matmul(bank[:, 0:HALF], wh[q][:, w], xl[:, half], start=False, stop=False)
                        last = nc.tensor.matmul(bank[:, 0:HALF], wl[q][:, w], xh[:, half], start=False, stop=True)
                    last.then_inc(h_ps, 1)

                def output(e, q, k):
                    pe.wait_ge(hl_ok, U * e + 2 * k + 2)
                    w = slice(W2 + D * k, W2 + D * k + D)
                    for j in range(ST):
                        at, out = slice(P * j, P * j + P), psY[j // 4][:, P * (j % 4):P * (j % 4) + P]
                        nc.tensor.matmul(out, hh[:, k, at], wh[q][:, w], start=k == 0 and j % 4 == 0, stop=False, skip_group_check=True)
                        nc.tensor.matmul(out, hh[:, k, at], wl[q][:, w], start=False, stop=False, skip_group_check=True)
                        last = nc.tensor.matmul(out, hl[:, k, at], wh[q][:, w], start=False, stop=k == FC - 1, skip_group_check=True)
                    return last

                transpose_rows(0)

                def body(i, q, more, two_more):
                    e = 2 * i + q
                    pe.wait_ge(xl_ok, e + 1)
                    pe.wait_ge(wl_ok, e + 1)
                    for n in range(4):
                        hidden(e, q, n)
                    pe.wait_ge(y_ok, e + 1)
                    output(e, q, 0)
                    for n in range(4, 6):
                        hidden(e, q, n)
                    output(e, q, 1)
                    for n in range(6, 8):
                        hidden(e, q, n)
                    if more:
                        transpose_rows(e + 1)
                    output(e, q, 2)
                    output(e, q, 3).then_inc(y_ps, 1)
                each(pe, body)


def softmax_attention(nc, io, s):
    HD = 2
    sem = s.sem
    scale = float(D) ** -0.5
    with ExitStack() as local:
        def lb(name, shape, dt=f32):
            return local.enter_context(nc.sbuf_tensor("c_" + name, shape, dt))

        def pair(name, shape, dt=f32):
            return [lb(f"{name}{h}", shape, dt) for h in range(2)]
        ctxT, x2, xn, xnT = pair("ctxT", [D, 256]), pair("x2", [P, HD, D]), pair("xn", [P, HD, D]), pair("xnT", [D, 256])
        index, got = pair("index", [P, 2, HD], u32), pair("got", [P, 2, HD, D])
        st, mv, ve, rs = pair("st", [P, HD, 6]), pair("mv", [P, HD, 2]), pair("ve", [P, HD]), pair("rs", [P, HD])
        QT, KT, V = pair("QT", [D, 256]), pair("KT", [D, 256]), pair("V", [P, HD, D])
        sc, Pb, PT = pair("sc", [P, HD, SEQ]), pair("Pb", [P, HD, P]), pair("PT", [P, 256])
        mx, sm = pair("mx", [P, HD]), pair("sm", [P, HD])
        valid, masked = lb("valid", [P, TILES, SEQ]), lb("masked", [P, TILES, SEQ])
        keymask = lb("keymask", [P, TILES, SEQ], i32)
        minus_half = lb("minus_half", [P, HD])
        psT, psK, psS, psV = s.ps[0:2], s.ps[2:4], s.ps[4:6], s.ps[6:8]
        ctx_in, gathered = [sem(f"c_ctx_in{h}") for h in range(2)], [sem(f"c_gathered{h}") for h in range(2)]
        names = ("mask_in mask_ok zeros_ok half_ok x2_ok agg_ok rs_ok xn_ok xnT_ps xnT_ok q_ps q_ok kv_ps kT_ok v_ok s_ps sc_ok "
                 "p_ok pT_ps pT_ok o_ps x3n_ok x3T_ps x3T_ok lg_ps lg_ok dve_order pool_order").split()
        n_ = {k: sem("c_" + k) for k in names}
        with nc.Block() as block:
            @block.sync
            def _(sp):
                sp.dma_start(keymask[:].rearrange("p t k -> p (t k)"), io["keymask"]).then_inc(n_["mask_in"], 16)
                for h in range(2):
                    sp.dma_start(ctxT[h][:], io["ctxT"][:, 256 * h:256 * h + 256]).then_inc(ctx_in[h], 16)
                with sp.Fori(1, GROUPS) as i:
                    for h in range(2):
                        sp.wait_ge(n_["kv_ps"], 2 * i - 1 + h)
                        sp.dma_start(ctxT[h][:], io["ctxT"][:, bass.ds(512 * i + 256 * h, 256)]).then_inc(ctx_in[h], 16)
                for h in range(2):
                    sp.wait_ge(ctx_in[h], 16 * GROUPS)

            @block.gpsimd
            def _(pool):
                for h in range(2):
                    nc.gpsimd.memset(Pb[h][:], 0.0)
                nc.gpsimd.memset(minus_half[:], -0.5).then_inc(n_["zeros_ok"], 1)
                pool.wait_ge(n_["zeros_ok"], 1)
                with pool.Fori(0, GROUPS) as i:
                    def rstd(h, k):
                        pool.wait_ge(n_["agg_ok"], 6 * i + k + 1)
                        nc.gpsimd.tensor_tensor(rs[h][:], ve[h][:], minus_half[:], ALU.pow).then_inc(n_["rs_ok"], 1)

                    for h in range(2):
                        wait_apart(pool, n_["x2_ok"], 2 * i + h + 1)
                        for k in range(2):
                            last = nc.gpsimd.tensor_copy(index[h][:, k, :], s.fetch[k][:, bass.ds(4 * i + 2 * h, HD)])
                        last.then_inc(n_["pool_order"], 1)
                        wait_apart(pool, n_["pool_order"], 2 * i + h + 1)
                        for k in range(2):
                            for j in range(HD):
                                pool.indirect_dma_start(out=got[h][:, k, j, :], out_offset=None, in_=io["made0"],
                                                        in_offset=bass.IndirectOffsetOnAxis(ap=index[h][:, k, j:j + 1], axis=0),
                                                        bounds_check=SLOTS - 1, oob_is_err=False).then_inc(gathered[h], 16)
                    for k in range(6):
                        rstd(k % 2, k)

            @block.scalar
            def _(act):
                nc.scalar.activation(s.warm[:], s.c("ones")[:, 0:1], ACT.Exp)
                with act.Fori(0, GROUPS) as i:
                    for h in range(2):
                        act.wait_ge(n_["kv_ps"], 2 * i + h + 1)
                        nc.scalar.activation(KT[h][:], psK[h][:, 0:256], ACT.Identity, bias=s.v("bk")).then_inc(n_["kT_ok"], 1)
                    for h in range(2):
                        act.wait_ge(n_["xnT_ps"], 2 * i + h + 1)
                        nc.scalar.activation(xnT[h][:], psT[h][:, 0:256], ACT.Copy).then_inc(n_["xnT_ok"], 1)
                    for h in range(2):
                        act.wait_ge(n_["q_ps"], 2 * i + h + 1)
                        nc.scalar.activation(QT[h][:], psT[h][:, 256:512], ACT.Identity, bias=s.v("bq")).then_inc(n_["q_ok"], 1)
                    for h in range(2):
                        act.wait_ge(n_["sc_ok"], 2 * i + h + 1)
                        for b in range(2):
                            at = slice(SEQ * b, SEQ * b + SEQ)
                            last = nc.scalar.activation(Pb[h][at, :, at], sc[h][at, :, :], ACT.Exp, scale=scale)
                        last.then_inc(n_["p_ok"], 1)
                    for h in range(2):
                        act.wait_ge(n_["pT_ps"], 2 * i + h + 1)
                        nc.scalar.activation(PT[h][:], psS[h][:, 128:384], ACT.Copy).then_inc(n_["pT_ok"], 1)
                    for h in range(2):
                        act.wait_ge(n_["x3T_ps"], 2 * i + h + 1)
                        nc.scalar.activation(xnT[h][:], psT[h][:, 0:256], ACT.Copy).then_inc(n_["x3T_ok"], 1)
                    for h in range(2):
                        act.wait_ge(n_["lg_ps"], 2 * i + h + 1)
                        nc.scalar.activation(s.LG[:, bass.ds(4 * i + 2 * h, 2), :],
                                             psT[h][:, 256:256 + 2 * E].rearrange("p (t e) -> p t e", e=E), ACT.Copy).then_inc(n_["lg_ok"], 1)

            @block.vector
            def _(dve):
                V_ = nc.vector
                dve.sem_inc(n_["x2_ok"], 2)
                o = Order(dve, n_["dve_order"])
                dve.wait_ge(n_["mask_in"], 16)
                o.mark(V_.tensor_copy(masked[:], keymask[:]))
                o.wait()
                o.mark(V_.tensor_scalar(valid[:], masked[:], 0.0, None, ALU.not_equal))
                o.wait()
                big = 1e9 / scale
                o.mark(V_.tensor_scalar(masked[:], valid[:], big, -big, ALU.mult, ALU.add))
                o.wait()
                before = o.n
                DO = 56
                with dve.Fori(0, GROUPS) as i:
                    o = Order(dve, n_["dve_order"], DO * i + before)
                    tile = lambda h, j: s.X[:, bass.ds(4 * i + 2 * h + j, 1), :].rearrange("p a d -> p (a d)")

                    def variance(h, src):
                        for j in range(HD):
                            o.mark(V_.bn_stats(st[h][:, j, :], src(j)))
                        o.wait_apart()
                        for j in range(HD):
                            o.mark(V_.bn_aggr(mv[h][:, j, :], st[h][:, j, :]))
                        o.wait()
                        V_.tensor_scalar(ve[h][:], mv[h][:, :, 1], EPS, None, ALU.add).then_inc(n_["agg_ok"], 1)

                    def normalise(h, k, src):
                        dve.wait_ge(n_["rs_ok"], 6 * i + k + 1)
                        for j in range(HD):
                            last = V_.tensor_scalar(xn[h][:, j, :], src(j), mv[h][:, j, 0:1], rs[h][:, j:j + 1], ALU.subtract, ALU.mult)
                        return last

                    for h in range(2):
                        dve.wait_ge(n_["kv_ps"], 2 * i + h + 1)
                        V_.tensor_tensor(V[h][:], psV[h][:, 0:256].rearrange("p (t d) -> p t d", d=D),
                                         s.v("bv").unsqueeze(1).broadcast_to([P, HD, D]), ALU.add).then_inc(n_["v_ok"], 1)
                    for h in range(2):
                        wait_apart(dve, gathered[h], 64 * i + 64)
                        for k in range(2):
                            for j in range(HD):
                                to = x2[h][:, j, :]
                                o.mark(V_.scalar_tensor_tensor(to, got[h][:, k, j, :], s.share[k][:, bass.ds(4 * i + 2 * h + j, 1)],
                                                               tile(h, j) if k == 0 else to, ALU.mult, ALU.add))
                            if k == 0:
                                o.wait_apart()
                        V_.memset(mx[h][:, 0:1], 0.0).then_inc(n_["x2_ok"], 1)
                        o.wait_apart()
                        variance(h, lambda j: x2[h][:, j, :])
                    for h in range(2):
                        normalise(h, h, lambda j: x2[h][:, j, :]).then_inc(n_["xn_ok"], 1)
                    for h in range(2):
                        dve.wait_ge(n_["s_ps"], 2 * i + h + 1)
                        at = bass.ds(4 * i + 2 * h, HD)
                        o.mark(V_.tensor_tensor(sc[h][:], psS[h][:, 0:128].rearrange("p (t k) -> p t k", k=SEQ), valid[:, at, :], ALU.mult))
                        o.wait()
                        o.mark(V_.tensor_tensor(sc[h][:], sc[h][:], masked[:, at, :], ALU.add))
                        o.wait()
                        o.mark(V_.tensor_reduce(mx[h][:], sc[h][:], AX.X, ALU.max))
                        o.wait()
                        V_.tensor_tensor(sc[h][:], sc[h][:], mx[h][:].unsqueeze(2).broadcast_to([P, HD, SEQ]), ALU.subtract).then_inc(n_["sc_ok"], 1)
                    for h in range(2):
                        dve.wait_ge(n_["p_ok"], 2 * i + h + 1)
                        o.mark(V_.tensor_reduce(sm[h][:], Pb[h][:], AX.X, ALU.add))
                        o.wait()
                        o.mark(V_.reciprocal(sm[h][:], sm[h][:]))
                        o.wait()
                        o.mark(V_.tensor_scalar(sm[h][:], sm[h][:], s.tg[:, 1:2], None, ALU.mult))
                    o.wait()
                    for h in range(2):
                        dve.wait_ge(n_["o_ps"], 2 * i + h + 1)
                        for j in range(HD):
                            o.mark(V_.scalar_tensor_tensor(tile(h, j), psT[h][:, 128 * j:128 * j + 128], sm[h][:, j:j + 1], x2[h][:, j, :],
                                                           ALU.mult, ALU.add))
                        o.wait_apart()
                        variance(h, lambda j: tile(h, j))
                    for h in range(2):
                        o.mark(normalise(h, 2 + h, lambda j: tile(h, j)))
                        o.wait_apart()
                        variance(h, lambda j: xn[h][:, j, :])
                    for h in range(2):
                        o.mark(normalise(h, 4 + h, lambda j: xn[h][:, j, :]))
                        o.wait()
                        o.mark(V_.tensor_tensor(xn[h][:], xn[h][:], s.v("gamma1").unsqueeze(1).broadcast_to([P, HD, D]), ALU.mult))
                        o.wait()
                        V_.tensor_tensor(xn[h][:], xn[h][:], s.v("beta1").unsqueeze(1).broadcast_to([P, HD, D]), ALU.add).then_inc(n_["x3n_ok"], 1)
                        dve.wait_ge(n_["x3n_ok"], 2 * i + h + 1)
                        o.mark(V_.tensor_copy(s.XN[:, bass.ds(4 * i + 2 * h, 2), :], xn[h][:]))
                    o.wait()
                    assert o.n == DO, o.n

            @block.tensor
            def _(pe):
                with pe.Fori(0, GROUPS) as i:
                    for h in range(2):
                        pe.wait_ge(ctx_in[h], 16 * i + 16)
                        nc.tensor.matmul(psK[h][:, 0:256], s.w("wk1"), ctxT[h][:], start=True, stop=True)
                        for j in range(HD):
                            last = nc.tensor.matmul(psV[h][:, 128 * j:128 * j + 128], ctxT[h][:, 128 * j:128 * j + 128],
                                                    s.w("wv1"), start=True, stop=True)
                        last.then_inc(n_["kv_ps"], 1)
                    for h in range(2):
                        pe.wait_ge(n_["xn_ok"], 2 * i + h + 1)
                        for j in range(HD):
                            last = nc.tensor.transpose(psT[h][:, 128 * j:128 * j + 128], xn[h][:, j, :], s.c("ident"))
                        last.then_inc(n_["xnT_ps"], 1)
                    for h in range(2):
                        pe.wait_ge(n_["xnT_ok"], 2 * i + h + 1)
                        nc.tensor.matmul(psT[h][:, 256:512], s.w("wq1"), xnT[h][:], start=True, stop=True).then_inc(n_["q_ps"], 1)
                    for h in range(2):
                        pe.wait_ge(n_["q_ok"], 2 * i + h + 1)
                        pe.wait_ge(n_["kT_ok"], 2 * i + h + 1)
                        for j in range(HD):
                            for b in range(2):
                                at = slice(128 * j + SEQ * b, 128 * j + SEQ * b + SEQ)
                                last = nc.tensor.matmul(psS[h][SEQ * b:SEQ * b + SEQ, SEQ * j:SEQ * j + SEQ], QT[h][:, at], KT[h][:, at],
                                                        start=True, stop=True)
                        last.then_inc(n_["s_ps"], 1)
                    for h in range(2):
                        pe.wait_ge(n_["p_ok"], 2 * i + h + 1)
                        for j in range(HD):
                            last = nc.tensor.transpose(psS[h][:, 128 + 128 * j:256 + 128 * j], Pb[h][:, j, :], s.c("ident"))
                        last.then_inc(n_["pT_ps"], 1)
                    for h in range(2):
                        pe.wait_ge(n_["pT_ok"], 2 * i + h + 1)
                        pe.wait_ge(n_["v_ok"], 2 * i + h + 1)
                        for j in range(HD):
                            last = nc.tensor.matmul(psT[h][:, 128 * j:128 * j + 128], PT[h][:, 128 * j:128 * j + 128], V[h][:, j, :],
                                                    start=True, stop=True)
                        last.then_inc(n_["o_ps"], 1)
                    for h in range(2):
                        pe.wait_ge(n_["x3n_ok"], 2 * i + h + 1)
                        for j in range(HD):
                            last = nc.tensor.transpose(psT[h][:, 128 * j:128 * j + 128], xn[h][:, j, :], s.c("ident"))
                        last.then_inc(n_["x3T_ps"], 1)
                    for h in range(2):
                        pe.wait_ge(n_["x3T_ok"], 2 * i + h + 1)
                        for j in range(HD):
                            last = nc.tensor.matmul(psT[h][:, 256 + E * j:256 + E * j + E], xnT[h][:, 128 * j:128 * j + 128],
                                                    s.w("router1"), start=True, stop=True)
                        last.then_inc(n_["lg_ps"], 1)
                    for h in range(2):
                        pe.wait_ge(n_["lg_ok"], 2 * i + h + 1)


def final(nc, io, s):
    HD = 2
    with ExitStack() as local:
        def lb(name, shape, dt=f32):
            return local.enter_context(nc.sbuf_tensor("f_" + name, shape, dt))
        index, got, y = ([lb(f"{n}{h}", shape, dt) for h in range(2)] for n, shape, dt in
                         (("index", [P, 2, HD], u32), ("got", [P, 2, HD, D], f32), ("y", [P, HD, D], f32)))
        gathered, stored = [s.sem(f"f_gathered{h}") for h in range(2)], [s.sem(f"f_stored{h}") for h in range(2)]
        y_ok, first_ok, index_ok = s.sem("f_y_ok"), s.sem("f_first_ok"), s.sem("f_index_ok")
        out = io["out"].rearrange("(t p) d -> p t d", p=P)
        with nc.Block() as block:
            @block.gpsimd
            def _(pool):
                with pool.Fori(0, GROUPS) as i:
                    for h in range(2):
                        wait_apart(pool, y_ok, 2 * i + h + 1)
                        for k in range(2):
                            last = nc.gpsimd.tensor_copy(index[h][:, k, :], s.fetch[k][:, bass.ds(4 * i + 2 * h, HD)])
                        last.then_inc(index_ok, 1)
                        wait_apart(pool, index_ok, 2 * i + h + 1)
                        for k in range(2):
                            for j in range(HD):
                                pool.indirect_dma_start(out=got[h][:, k, j, :], out_offset=None, in_=io["made1"],
                                                        in_offset=bass.IndirectOffsetOnAxis(ap=index[h][:, k, j:j + 1], axis=0),
                                                        bounds_check=SLOTS - 1, oob_is_err=False).then_inc(gathered[h], 16)

            @block.vector
            def _(dve):
                dve.sem_inc(y_ok, 2)
                with dve.Fori(0, GROUPS) as i:
                    for h in range(2):
                        wait_apart(dve, gathered[h], 64 * i + 64)
                        wait_apart(dve, stored[h], 16 * i + 16)
                        for k in range(2):
                            for j in range(HD):
                                x = s.X[:, bass.ds(4 * i + 2 * h + j, 1), :].rearrange("p a d -> p (a d)")
                                last = nc.vector.scalar_tensor_tensor(y[h][:, j, :], got[h][:, k, j, :],
                                                                      s.share[k][:, bass.ds(4 * i + 2 * h + j, 1)],
                                                                      x if k == 0 else y[h][:, j, :], ALU.mult, ALU.add)
                            if k == 0:
                                last.then_inc(first_ok, 1)
                                wait_apart(dve, first_ok, 2 * i + h + 1)
                        last.then_inc(y_ok, 1)

            @block.sync
            def _(sp):
                for h in range(2):
                    sp.sem_inc(stored[h], 16)
                with sp.Fori(0, GROUPS) as i:
                    for h in range(2):
                        sp.wait_ge(y_ok, 2 * i + h + 3)
                        sp.dma_start(out[:, bass.ds(4 * i + 2 * h, HD), :], y[h][:]).then_inc(stored[h], 16)
                for h in range(2):
                    sp.wait_ge(stored[h], 16 * (GROUPS + 1))


def layout(i):
    f = lambda k: np.asarray(i[k])
    row = lambda a: np.broadcast_to(a.reshape(1, -1), (P, a.size))
    e0 = lambda k, n: f(k)
    shape = np.zeros((P, columns(SHAPE_COLS)[1]), np.float32)
    sc = columns(SHAPE_COLS)[0]
    put = lambda k, a: shape.__setitem__((slice(None), slice(sc[k][0], sc[k][0] + sc[k][1])), a)
    put("ident", np.eye(P))
    put("before", np.triu(np.ones((P, P)), 1))
    put("ones", 1.0)
    put("heads", np.kron(np.eye(D // HEAD), np.ones((HEAD, HEAD))))
    put("own", np.kron(np.ones((4, 1)), np.kron(np.eye(4), np.ones((HEAD, 1)))))
    put("rev", E - np.arange(E))
    put("expert_base", CAP * np.arange(E))
    put("restart", (np.arange(2 * E * TILES) % TILES > 0) * 1.0)
    vec = np.concatenate([row(f("L0_xattn_ln_gamma")), row(f("L0_xattn_ln_beta")), row(f("L0_xattn_dense_b")), row(f("L1_xattn_bv")),
                          row(f("L1_ffn_ln_gamma")), row(f("L1_ffn_ln_beta")), f("L0_xattn_ln_gamma")[:, None],
                          f("L0_xattn_ln_beta")[:, None], f("L1_xattn_bq")[:, None], f("L1_xattn_bk")[:, None],
                          row(f("g_xattn")), row(f("g_ffn")), f("mask_BxS2_ff1").reshape(TILES, P).T,
                          np.full((P, 1), EPS, np.float32), np.full((P, 1), EPS_L0, np.float32)], axis=1)
    dense = np.broadcast_to(f("L0_xattn_dense_w").reshape(4, 4, 1, HEAD, D), (4, 4, 4, HEAD, D)).transpose(0, 2, 3, 1, 4).reshape(P, 4 * D)
    w = np.concatenate([f("L0_xattn_wq"), f("L0_xattn_wk"), f("L0_xattn_wv"), dense, f("L0_ffn_router_w"),
                        f("L1_xattn_Wq"), f("L1_xattn_Wk"), f("L1_xattn_Wv"), f("L1_ffn_Wr").T], axis=1)
    second = lambda a: a.reshape(-1, FC, P, D).transpose(0, 2, 1, 3).reshape(-1, P, FC * D)
    w1 = np.concatenate([f("L0_ffn_w1"), f("L0_ffn_sw1")[None]])
    w2 = np.concatenate([f("L0_ffn_w2"), f("L0_ffn_sw2")[None]])
    b1 = np.concatenate([f("L0_ffn_b1"), f("L0_ffn_sb1")[None]])
    b2 = np.concatenate([f("L0_ffn_b2"), f("L0_ffn_sb2")[None]])
    bias0 = np.concatenate([b1.reshape((E + 1) * FC, P).T, row(b2)], axis=1)
    pack1 = np.concatenate([f("L1_ffn_W12").transpose(0, 2, 1), second(f("L1_ffn_W3").transpose(0, 2, 1))], axis=2)
    return {
        "x": f("x").reshape(TOKENS, D), "ctxT": f("ctx_1024").reshape(TOKENS, D).T, "shape": shape, "vec": vec, "w": w,
        "experts0": np.concatenate([w1, second(w2)], axis=2), "bias0": bias0, "experts1": pack1,
        "keymask": np.repeat(f("mask_BxS2_ik0").reshape(TILES, 2, SEQ).transpose(1, 0, 2).reshape(2, -1), SEQ, axis=0),
    }


def declare(nc, arrays):
    io = {}
    for name, a in arrays.items():
        io[name] = nc.dram_tensor(f"in_{name}", a.shape, mybir.dt.from_np(a.dtype), kind="ExternalInput").ap()
    io["out"] = nc.dram_tensor("out_dram", (TOKENS, D), f32, kind="ExternalOutput").ap()
    for k in range(2):
        io[f"slots{k}"] = nc.dram_tensor(f"slots{k}", (SLOTS, D), f32, kind="Internal").ap()
        io[f"made{k}"] = nc.dram_tensor(f"made{k}", (SLOTS, D), f32, kind="Internal").ap()
    return io


def kernel(**inputs):
    import concourse.bacc as _bacc
    from concourse.bass_utils import run_bass_kernel_spmd as _run

    nc = _bacc.Bacc("TRN2", target_bir_lowering=False, num_devices=1)
    arrays = {k: np.ascontiguousarray(a) for k, a in layout(inputs).items()}
    build(nc, declare(nc, arrays))
    r = _run(nc, [{f"in_{k}": a for k, a in arrays.items()}], core_ids=[0])
    return r.results[0]["out_dram"].reshape(32, SEQ, D)
```

```python
from contextlib import ExitStack

import numpy as np
import concourse.bass as bass
from concourse import mybir

P = 128
D = 128
TOKENS = 2048
TILES = TOKENS // P
SEQ = 64
E = 8
F = 512
FC = F // P
CAP = 640
ST = CAP // P
HALF = CAP // 2
SLOTS = E * CAP
ROW = D + 4
GROUPS = 4
EPS = 1e-5
EPS_L0 = 1e-6
HEAD = 8
WIDTH = (F + FC * D, 2 * F + FC * D)

f32 = mybir.dt.float32
f32r = mybir.dt.float32r
i32 = mybir.dt.int32
u32 = mybir.dt.uint32
ALU = mybir.AluOpType
ACT = mybir.ActivationFunctionType
AX = mybir.AxisListType

SHAPE_COLS = dict(ident=128, before=128, ones=128, heads=128, own=4, rev=E, expert_base=E, restart=2 * E * TILES, spare=ST, token=TILES, slot=E * ST)
VEC_COLS = dict(gamma=128, beta=128, dense_b=128, bv=128, gamma1=128, beta1=128,
                gamma_t=1, beta_t=1, bq=1, bk=1, gates=4, em=TILES, eps5=1, eps6=1)
W_COLS = dict(wq=128, wkv=256, dense=512, router0=E, wq1=128, wk1=128, wv1=128, router1=E)


def columns(spec):
    at, out = 0, {}
    for k, n in spec.items():
        out[k] = (at, n)
        at += n
    return out, at


class Order:

    def __init__(self, eng, sem, before=0):
        self.eng, self.sem, self.before, self.n = eng, sem, before, 0

    def mark(self, ins):
        ins.then_inc(self.sem, 1)
        self.n += 1
        return self.n

    def wait(self, n=None):
        self.eng.wait_ge(self.sem, self.before + (self.n if n is None else n))

    def wait_apart(self):
        wait_apart(self.eng, self.sem, self.before + self.n)


def build(nc, io, stop=4, debug=None):
    ctx = ExitStack()
    with ctx:
        def sb(name, shape, dt=f32):
            return ctx.enter_context(nc.sbuf_tensor(name, shape, dt))

        def sem(name):
            return ctx.enter_context(nc.semaphore(name))

        class S:
            pass
        s = S()
        s.sem, s.sb = sem, sb
        sc, n_sc = columns(SHAPE_COLS)
        vc, n_vc = columns(VEC_COLS)
        wc, n_wc = columns(W_COLS)
        shape_t = sb("shape_t", [P, n_sc])
        vec_t = sb("vec_t", [P, n_vc])
        w_t = sb("w_t", [P, n_wc])
        s.c = lambda k: shape_t[:, sc[k][0]:sc[k][0] + sc[k][1]]
        s.v = lambda k: vec_t[:, vc[k][0]:vc[k][0] + vc[k][1]]
        s.w = lambda k: w_t[:, wc[k][0]:wc[k][0] + wc[k][1]]
        s.shape_t, s.vec_t, s.w_t = shape_t, vec_t, w_t
        s.X = sb("rows", [P, TILES, D])
        s.XN = sb("normed", [P, TILES, ROW])
        s.XTH = sb("normed_t_high", [D, TOKENS], f32r)
        s.XTL = sb("normed_t_low", [D, TOKENS], f32r)
        s.LG = sb("logits", [P, TILES, E])
        s.tg = sb("tanh_gates", [P, 4])
        s.ps = [ctx.enter_context(nc.psum_tensor(f"bank{b}", [P, 512], f32)) for b in range(8)]
        s.slot = [sb(f"slot{k}", [P, TILES], u32) for k in range(2)]
        s.share = [sb(f"share{k}", [P, TILES]) for k in range(2)]
        s.bias = sb("bias", [P, (E + 1) * (FC + D)])
        s.warm = sb("warm", [P, 2])
        s.empty = sb("empty", [P, ST, ROW])
        s.zeroed = sem("slots_zeroed")
        s.shared_w = sb("shared_w", [P, 2 * F])
        s.shared_in, s.bias_in = sem("shared_in"), sem("bias_in")
        wait_apart.carrier = sem("carrier")
        linear_attention(nc, io, s)
        if stop >= 2:
            moe(nc, io, s, 0)
        if stop >= 3:
            softmax_attention(nc, io, s)
        if stop >= 4:
            moe(nc, io, s, 1)
        if debug:
            debug(nc, io, s)


def wait_apart(eng, sem, value):
    eng.wait_ge(sem, value)
    eng.sem_inc(wait_apart.carrier, 1)


def row_stats(nc, o, src, st, mv, n, done):
    for j in range(n):
        o.mark(nc.vector.bn_stats(st[:, j, :], src(j)))
    o.wait_apart()
    for j in range(n):
        last = nc.vector.bn_aggr(mv[:, j, :], st[:, j, :])
    last.then_inc(done, 1)


def linear_attention(nc, io, s):
    HD, PARTS = 2, 4
    TG = HD * PARTS
    N = TILES // TG
    sem = s.sem
    with ExitStack() as local:
        def lb(name, shape, dt=f32):
            return local.enter_context(nc.sbuf_tensor("a_" + name, shape, dt))

        def each(name, shape, dt=f32):
            return [lb(f"{name}{h}", shape, dt) for h in range(PARTS)]
        ctxT, xn, xnT = each("ctxT", [D, HD * P]), each("xn", [P, HD, D]), each("xnT", [D, HD * P])
        st, mv = each("st", [P, 3 * HD, 6]), each("mv", [P, 3 * HD, 2])
        rs, nm, rm = each("rs", [P, 3 * HD]), each("nm", [P, HD]), each("rm", [P, HD])
        kv, qn, qT = each("kv", [P, HD, 2, D]), each("qn", [P, HD, D]), each("qT", [D, HD * P])
        vv = each("vv", [P, HD, 2, D + 1])
        ks = each("ks", [D, HD, 2])
        kvb = each("kvb", [D, HD, 2, 2, D])
        den, attT, attS, attX = (each(n, [D, w * HD * P]) for n, w in (("den", 1), ("attT", 1), ("attS", 1), ("attX", 4)))
        o1, xb, emb = (each(n, [P, HD, D]) for n in ("o1", "xb", "emb"))
        gB, bB, em2 = lb("gB", [P, D]), lb("bB", [P, D]), lb("em2", [P, TILES])
        psX, psY = s.ps[0::2], s.ps[1::2]

        names = ("x_in gates_ok gB_ok xn_ok xnT_ps xnT_ok kv_ps q_ps nm_ok qn_ok kv_ok mask_ok qT_ps qTr_ok qT_ok m_ps ks_ok keys_ok kvb_ok n_ps "
                 "den_ok att_ok swapA_ok swapD_ok attX_ok o_ps xb_ok x1n_ok x1T_ps xT_ok x1T_ok lg_ps lg_ok low_ok agg_ok rs_ok "
                 "act_order dve_order pool_order empty_ok").split()
        m = {k: sem("a_" + k) for k in names}
        loaded = [sem(f"a_loaded{k}") for k in range(3)]
        ctx_in = [sem(f"a_ctx_in{h}") for h in range(PARTS)]
        x_rows = io["x"].rearrange("(t p) d -> p t d", p=P)
        ctx_at = lambda i, h: bass.ds(P * (TG * i + HD * h), P * HD)
        with nc.Block() as block:
            @block.sync
            def _(sp):
                sp.dma_start(s.X[:, 0:TG, :], x_rows[:, 0:TG, :]).then_inc(m["x_in"], 16)
                sp.dma_start(s.shape_t[:], io["shape"]).then_inc(loaded[0], 16)
                for h in range(PARTS):
                    sp.dma_start(ctxT[h][:], io["ctxT"][:, ctx_at(0, h)]).then_inc(ctx_in[h], 16)
                with sp.Fori(1, N) as i:
                    sp.wait_ge(m["x_in"], 16 * i)
                    sp.dma_start(s.X[:, bass.ds(TG * i, TG), :], x_rows[:, bass.ds(TG * i, TG), :]).then_inc(m["x_in"], 16)
                    for h in range(PARTS):
                        sp.wait_ge(m["kv_ps"], PARTS * (i - 1) + h + 1)
                        sp.dma_start(ctxT[h][:], io["ctxT"][:, ctx_at(i, h)]).then_inc(ctx_in[h], 16)
                sp.dma_start(s.shared_w[:], io["experts0"][E, :, :]).then_inc(s.shared_in, 16)
                sp.dma_start(s.bias[:], io["bias0"]).then_inc(s.bias_in, 16)
                sp.wait_ge(m["empty_ok"], 1)
                for k in range(2):
                    for e in range(E):
                        sp.dma_start(io[f"slots{k}"].rearrange("(e s p) d -> e p s d", s=ST, p=P)[e], s.empty[:]).then_inc(s.zeroed, 16)
                    sp.dma_start(io[f"sums{k}"][TOKENS:TOKENS + CAP, :].rearrange("(s p) d -> p s d", p=P), s.empty[:, :, 0:D]).then_inc(s.zeroed, 16)
                sp.wait_ge(s.zeroed, 16 * 2 * (E + 1))

            @block.scalar
            def _(act):
                act.dma_start(s.vec_t[:], io["vec"]).then_inc(loaded[1], 16)
                act.dma_start(s.w_t[:], io["w"]).then_inc(loaded[2], 16)
                act.wait_ge(loaded[1], 16)
                nc.scalar.activation(s.tg[:], s.v("gates"), ACT.Tanh).then_inc(m["gates_ok"], 1)
                nc.scalar.activation(s.warm[:, 0:1], s.v("eps5"), ACT.Sqrt)
                with act.Fori(0, N) as i:
                    A = nc.scalar.activation
                    at = lambda h: PARTS * i + h + 1

                    def deviation(h, stage, n, eps):
                        act.wait_ge(m["agg_ok"], 4 * PARTS * i + PARTS * stage + h + 1)
                        A(rs[h][:, 0:n], mv[h][:, 0:n, 1], ACT.Sqrt, bias=s.v(eps)).then_inc(m["rs_ok"], 1)

                    for h in range(PARTS):
                        deviation(h, 0, HD, "eps5")
                    for h in range(PARTS):
                        act.wait_ge(m["xnT_ps"], at(h))
                        A(xnT[h][:], psX[h][:, 0:256], ACT.Copy).then_inc(m["xnT_ok"], 1)
                    for h in range(PARTS):
                        deviation(h, 1, 3 * HD, "eps6")
                    for h in range(PARTS):
                        act.wait_ge(m["nm_ok"], at(h))
                        for j in range(HD):
                            last = A(qn[h][:, j, :], psX[h][:, 256 + 128 * j:384 + 128 * j], ACT.Identity,
                                     bias=nm[h][:, j:j + 1], scale=rs[h][:, 4 + j:5 + j])
                        last.then_inc(m["qn_ok"], 1)
                    for h in range(PARTS):
                        act.wait_ge(m["qT_ps"], at(h))
                        A(qT[h][:], psX[h][:, 0:256], ACT.Relu, bias=s.v("beta_t"), scale=s.v("gamma_t")).then_inc(m["qTr_ok"], 1)
                    for h in range(PARTS):
                        act.wait_ge(m["qTr_ok"], at(h))
                        A(qT[h][:], qT[h][:], ACT.Identity, bias=s.v("eps6")).then_inc(m["qT_ok"], 1)
                    for h in range(PARTS):
                        act.wait_ge(m["ks_ok"], at(h))
                        for j in range(HD):
                            for b in range(2):
                                last = A(kvb[h][:, j, b, 1, :], s.c("heads"), ACT.Copy, scale=ks[h][:, j, b:b + 1])
                        last.then_inc(m["keys_ok"], 1)

                    def denominators(h):
                        act.wait_ge(m["n_ps"], at(h))
                        A(den[h][:], psX[h][:, 256:512], ACT.Identity, bias=s.v("eps6")).then_inc(m["den_ok"], 1)

                    denominators(0)
                    for h in range(PARTS):
                        if h + 1 < PARTS:
                            denominators(h + 1)
                        act.wait_ge(m["att_ok"], at(h))
                        for q, a in SWAPS[0]:
                            last = A(*swap(attT[h], attS[h], q, a), ACT.Copy)
                        last.then_inc(m["swapA_ok"], 1)
                    for h in range(PARTS):
                        deviation(h, 2, HD, "eps6")
                    for h in range(PARTS):
                        deviation(h, 3, HD, "eps5")

                    def logits(h):
                        act.wait_ge(m["lg_ps"], at(h))
                        A(s.LG[:, bass.ds(TG * i + HD * h, HD), :], psY[h][:, 256:256 + HD * E].rearrange("p (t e) -> p t e", e=E),
                          ACT.Copy).then_inc(m["lg_ok"], 1)

                    for h in range(PARTS):
                        act.wait_ge(m["x1n_ok"], at(h))
                        A(s.XN[:, bass.ds(TG * i + HD * h, HD), 0:D], xn[h][:], ACT.Copy)
                        act.wait_ge(m["x1T_ps"], at(h))
                        A(xnT[h][:], psX[h][:, 0:256], ACT.Copy).then_inc(m["xT_ok"], 1)
                        A(s.XTH[:, ctx_at(i, h)], psX[h][:, 0:256], ACT.Copy).then_inc(m["x1T_ok"], 1)
                        if h:
                            logits(h - 1)
                    logits(PARTS - 1)

            @block.gpsimd
            def _(pool):
                G = nc.gpsimd
                o = Order(pool, m["pool_order"])
                for h in range(PARTS):
                    o.mark(G.memset(vv[h][:], 0.0))
                o.mark(G.memset(s.empty[:], 0.0))
                o.wait()
                pool.wait_ge(loaded[0], 16)
                G.tensor_copy(s.empty[:, :, D].bitcast(u32), s.c("spare")).then_inc(m["empty_ok"], 1)
                pool.wait_ge(loaded[1], 16)
                o.mark(G.tensor_tensor(em2[:], s.v("em"), s.v("em"), ALU.mult))
                o.wait()
                pool.wait_ge(m["gates_ok"], 1)
                G.tensor_scalar(gB[:], s.v("gamma"), s.tg[:, 0:1], None, ALU.mult)
                G.tensor_scalar(bB[:], s.v("beta"), s.tg[:, 0:1], None, ALU.mult).then_inc(m["gB_ok"], 1)
                pool.wait_ge(m["gB_ok"], 1)
                with pool.Fori(0, N) as i:
                    at = lambda h: PARTS * i + h + 1
                    for h in range(PARTS):
                        tiles = bass.ds(TG * i + HD * h, HD)
                        wide = lambda row: row.unsqueeze(1).broadcast_to([P, HD, D])
                        tall = lambda column: column[:, tiles].unsqueeze(2).broadcast_to([P, HD, D])
                        G.tensor_tensor(emb[h][:], wide(s.v("beta")), tall(em2[:]), ALU.mult).then_inc(m["mask_ok"], 1)
                    for h in range(PARTS):
                        wait_apart(pool, m["x_in"], 16 * i + 16)
                        G.tensor_tensor(xb[h][:], s.X[:, bass.ds(TG * i + HD * h, HD), :],
                                        bB[:].unsqueeze(1).broadcast_to([P, HD, D]), ALU.add).then_inc(m["xb_ok"], 1)
                    for h in range(PARTS):
                        pool.wait_ge(m["swapA_ok"], at(h))
                        pool.wait_ge(m["swapD_ok"], at(h))
                        G.tensor_tensor(attX[h][:].rearrange("p (m h n) -> p m h n", h=4, n=4),
                                        attS[h][:].rearrange("p (m n) -> p m n", n=4).unsqueeze(2).broadcast_to([P, 64, 4, 4]),
                                        s.c("own").unsqueeze(1).unsqueeze(3).broadcast_to([P, 64, 4, 4]), ALU.mult).then_inc(m["attX_ok"], 1)
                    for h in range(PARTS):
                        wait_apart(pool, m["x1T_ok"], at(h))
                        G.tensor_tensor(s.XTL[:, ctx_at(i, h)], xnT[h][:], s.XTH[:, ctx_at(i, h)].bitcast(f32), ALU.subtract).then_inc(m["low_ok"], 1)

            @block.vector
            def _(dve):
                V = nc.vector
                dve.wait_ge(loaded[1], 16)
                dve.wait_ge(loaded[0], 16)
                DO = 100
                with dve.Fori(0, N) as i:
                    o = Order(dve, m["dve_order"], DO * i)
                    at = lambda h: PARTS * i + h + 1
                    wait_apart(dve, m["x_in"], 16 * i + 16)
                    tile = lambda h, j: s.X[:, bass.ds(TG * i + HD * h + j, 1), :].rearrange("p a d -> p (a d)")

                    def inverse(h, stage, n):
                        dve.wait_ge(m["rs_ok"], 4 * PARTS * i + PARTS * stage + h + 1)
                        o.mark(V.reciprocal(rs[h][:, 0:n], rs[h][:, 0:n]))
                        o.wait()

                    def normalise(h, stage):
                        inverse(h, stage, HD)
                        for j in range(HD):
                            last = V.tensor_scalar(xn[h][:, j, :], tile(h, j), mv[h][:, j, 0:1], rs[h][:, j:j + 1], ALU.subtract, ALU.mult)
                        return last

                    for h in range(PARTS):
                        row_stats(nc, o, lambda j: tile(h, j), st[h], mv[h], HD, m["agg_ok"])
                    for h in range(PARTS):
                        normalise(h, 0).then_inc(m["xn_ok"], 1)
                    for h in range(PARTS):
                        wait_apart(dve, m["kv_ps"], at(h))
                        for n in range(4):
                            V.bn_stats(st[h][:, n, :], psY[h][:, 128 * n:128 * n + 128])
                    for h in range(PARTS):
                        wait_apart(dve, m["q_ps"], at(h))
                        for n in range(4, 6):
                            o.mark(V.bn_stats(st[h][:, n, :], psX[h][:, 128 * n - 256:128 * n - 128]))
                        o.wait_apart()
                        for n in range(6):
                            last = V.bn_aggr(mv[h][:, n, :], st[h][:, n, :])
                        last.then_inc(m["agg_ok"], 1)
                    for h in range(PARTS):
                        inverse(h, 1, 3 * HD)
                        V.scalar_tensor_tensor(nm[h][:], mv[h][:, 4:6, 0], -1.0, rs[h][:, 4:6], ALU.mult, ALU.mult).then_inc(m["nm_ok"], 1)
                        dve.wait_ge(m["mask_ok"], at(h))
                        o.mark(V.tensor_tensor(rm[h][:], rs[h][:, 1:4:2], em2[:, bass.ds(TG * i + HD * h, HD)], ALU.mult))
                        for n in range(4):
                            o.mark(V.scalar_tensor_tensor(kv[h][:, n // 2, n % 2, :], psY[h][:, 128 * n:128 * n + 128], mv[h][:, n, 0:1],
                                                          s.v("gamma"), ALU.subtract, ALU.mult))
                        o.wait()
                        for b in range(2):
                            rows = slice(SEQ * b, SEQ * b + SEQ)
                            V.tensor_copy(vv[h][rows, :, b, D], s.v("em")[rows, bass.ds(TG * i + HD * h, HD)])
                        for j in range(HD):
                            o.mark(V.scalar_tensor_tensor(kv[h][:, j, 0, :], kv[h][:, j, 0, :], rs[h][:, 2 * j:2 * j + 1], s.v("beta"),
                                                          ALU.mult, ALU.add))
                            for b in range(2):
                                rows = slice(SEQ * b, SEQ * b + SEQ)
                                V.scalar_tensor_tensor(vv[h][rows, j, b, 0:D], kv[h][rows, j, 1, :], rm[h][rows, j:j + 1], emb[h][rows, j, :],
                                                       ALU.mult, ALU.add)
                        o.wait()
                        V.tensor_scalar(kv[h][:, :, 0, :], kv[h][:, :, 0, :], 0.0, 1e-6, ALU.max, ALU.add).then_inc(m["kv_ok"], 1)
                    for h in range(PARTS):
                        dve.wait_ge(m["m_ps"], at(h))
                        made = [bank[:, 0:2 * (D + 1)].rearrange("d (b e) -> d b e", b=2) for bank in (psX[h], psY[h])]
                        for j in range(HD):
                            last = V.tensor_copy(ks[h][:, j, :], made[j][:, :, D])
                        last.then_inc(m["ks_ok"], 1)
                        for j in range(HD):
                            last = V.tensor_tensor(kvb[h][:, j, :, 0, :], made[j][:, :, 0:D],
                                                   s.c("heads").unsqueeze(1).broadcast_to([D, 2, D]), ALU.mult)
                        last.then_inc(m["kvb_ok"], 1)
                    for h in range(PARTS):
                        dve.wait_ge(m["den_ok"], at(h))
                        o.mark(V.reciprocal(den[h][:], den[h][:]))
                        o.wait()
                        V.tensor_tensor(attT[h][:], psX[h][:, 0:256], den[h][:], ALU.mult).then_inc(m["att_ok"], 1)
                        dve.wait_ge(m["att_ok"], at(h))
                        for q, a in SWAPS[1]:
                            last = V.tensor_copy(*swap(attT[h], attS[h], q, a))
                        last.then_inc(m["swapD_ok"], 1)
                    for h in range(PARTS):
                        dve.wait_ge(m["o_ps"], at(h))
                        o.mark(V.tensor_tensor(o1[h][:], psY[h][:, 0:256].rearrange("p (t d) -> p t d", d=D),
                                               s.v("dense_b").unsqueeze(1).broadcast_to([P, HD, D]), ALU.add))
                        o.wait_apart()
                        row_stats(nc, o, lambda j: o1[h][:, j, :], st[h], mv[h], HD, m["agg_ok"])
                    dve.wait_ge(m["gB_ok"], 1)
                    for h in range(PARTS):
                        inverse(h, 2, HD)
                        for j in range(HD):
                            o.mark(V.scalar_tensor_tensor(o1[h][:, j, :], o1[h][:, j, :], mv[h][:, j, 0:1], gB[:], ALU.subtract, ALU.mult))
                        dve.wait_ge(m["xb_ok"], at(h))
                        o.wait()
                        for j in range(HD):
                            o.mark(V.scalar_tensor_tensor(tile(h, j), o1[h][:, j, :], rs[h][:, j:j + 1], xb[h][:, j, :], ALU.mult, ALU.add))
                        o.wait_apart()
                        row_stats(nc, o, lambda j: tile(h, j), st[h], mv[h], HD, m["agg_ok"])
                    for h in range(PARTS):
                        normalise(h, 3).then_inc(m["x1n_ok"], 1)
                    assert o.n == DO, o.n

            @block.tensor
            def _(pe):
                pe.wait_ge(loaded[0], 16)
                pe.wait_ge(loaded[2], 16)
                mm = nc.tensor.matmul
                with pe.Fori(0, N) as i:
                    at = lambda h: PARTS * i + h + 1
                    for h in range(PARTS):
                        pe.wait_ge(ctx_in[h], 16 * i + 16)
                        for j in range(HD):
                            last = mm(psY[h][:, 256 * j:256 * j + 256], ctxT[h][:, 128 * j:128 * j + 128], s.w("wkv"), start=True, stop=True)
                        last.then_inc(m["kv_ps"], 1)
                    for h in range(PARTS):
                        pe.wait_ge(m["xn_ok"], at(h))
                        for j in range(HD):
                            last = nc.tensor.transpose(psX[h][:, 128 * j:128 * j + 128], xn[h][:, j, :], s.c("ident"))
                        last.then_inc(m["xnT_ps"], 1)
                    for h in range(PARTS):
                        pe.wait_ge(m["xnT_ok"], at(h))
                        for j in range(HD):
                            last = mm(psX[h][:, 256 + 128 * j:384 + 128 * j], xnT[h][:, 128 * j:128 * j + 128], s.w("wq"), start=True, stop=True)
                        last.then_inc(m["q_ps"], 1)
                    for h in range(PARTS):
                        pe.wait_ge(m["qn_ok"], at(h))
                        for j in range(HD):
                            last = nc.tensor.transpose(psX[h][:, 128 * j:128 * j + 128], qn[h][:, j, :], s.c("ident"))
                        last.then_inc(m["qT_ps"], 1)
                    for h in range(PARTS):
                        pe.wait_ge(m["kv_ok"], at(h))
                        pe.wait_ge(m["mask_ok"], at(h))
                        pe.wait_ge(m["qTr_ok"], at(h))
                        for j, bank in enumerate((psX[h], psY[h])):
                            last = mm(bank[:, 0:2 * (D + 1)], kv[h][:, j, 0, :], vv[h][:, j].rearrange("p b e -> p (b e)"), start=True, stop=True)
                        last.then_inc(m["m_ps"], 1)
                    for h in range(PARTS):
                        pe.wait_ge(m["kvb_ok"], at(h))
                        pe.wait_ge(m["keys_ok"], at(h))
                        pe.wait_ge(m["qT_ok"], at(h))
                        for j in range(HD):
                            for b in range(2):
                                for c in range(2):
                                    to = 128 * j + SEQ * b
                                    last = mm(psX[h][:, 256 * c + to:256 * c + to + SEQ], kvb[h][:, j, b, c, :], qT[h][:, to:to + SEQ],
                                              start=True, stop=True)
                        last.then_inc(m["n_ps"], 1)
                    for h in range(PARTS):
                        pe.wait_ge(m["attX_ok"], at(h))
                        for j in range(HD):
                            for b in range(4):
                                last = mm(psY[h][:, 128 * j:128 * j + 128], attX[h][:, 256 * b + 128 * j:256 * b + 128 * j + 128],
                                          s.w("dense")[:, 128 * b:128 * b + 128], start=b == 0, stop=b == 3)
                        last.then_inc(m["o_ps"], 1)

                    def logits(h):
                        pe.wait_ge(m["xT_ok"], at(h))
                        for j in range(HD):
                            last = mm(psY[h][:, 256 + E * j:256 + E * j + E], xnT[h][:, 128 * j:128 * j + 128], s.w("router0"), start=True, stop=True)
                        last.then_inc(m["lg_ps"], 1)

                    for h in range(PARTS):
                        pe.wait_ge(m["x1n_ok"], at(h))
                        for j in range(HD):
                            last = nc.tensor.transpose(psX[h][:, 128 * j:128 * j + 128], xn[h][:, j, :], s.c("ident"))
                        last.then_inc(m["x1T_ps"], 1)
                        if h:
                            logits(h - 1)
                    logits(PARTS - 1)
                    pe.wait_ge(m["lg_ok"], at(PARTS - 1))
                    pe.wait_ge(m["low_ok"], at(PARTS - 1))


SWAPS = [[(q, a) for q in range(4) for a in range(4) if (q < 2) == (k == 0)] for k in range(2)]


def swap(source, target, q, a):
    out = target[32 * a:32 * a + 32, :].rearrange("p (b j q n) -> p q b j n", b=4, j=4, q=4)[:, q]
    return out, source[32 * q:32 * q + 32, :].rearrange("p (j n a b) -> p a b j n", j=4, n=4, a=4)[:, a]


def moe(nc, io, s, layer):
    with ExitStack() as local:
        w = Weights(nc, io, s, layer, local)
        route(nc, io, s, layer, w)
        experts(nc, io, s, layer, w)


class Weights:

    def __init__(self, nc, io, s, layer, local):
        def two(name, shape, dt=f32):
            return [local.enter_context(nc.sbuf_tensor(f"w{layer}_{name}{q}", shape, dt)) for q in range(2)]
        self.nc, self.N1 = nc, F * (1 + layer)
        self.raw, self.w2 = two("raw", [P, self.N1]), two("w2", [P, FC * D])
        self.wh, self.wl = two("wh", [P, self.N1], f32r), two("wl", [P, self.N1], f32r)
        self.rows = two("rows", [P, ST, ROW])
        self.w_in, self.w2_in, self.rows_in = ([s.sem(f"w{layer}_{n}{q}") for q in range(2)] for n in ("w_in", "w2_in", "rows_in"))
        self.wh_ok, self.wl_ok = s.sem(f"w{layer}_wh_ok"), s.sem(f"w{layer}_wl_ok")
        self.dram = io[f"experts{layer}"]
        self.slot_rows = io[f"slots{layer}"].rearrange("(e s p) d -> e p s d", s=ST, p=P)

    def of(self, e):
        return self.dram[bass.ds(e, 1)].rearrange("e p n -> (e p) n")

    def load_rows(self, sp, e, q):
        sp.dma_start(self.rows[q][:], self.slot_rows[bass.ds(e, 1)].rearrange("e p s d -> (e p) s d")).then_inc(self.rows_in[q], 16)

    def load_first(self, sp, e, q):
        sp.dma_start(self.raw[q][:], self.of(e)[:, 0:self.N1]).then_inc(self.w_in[q], 16)

    def load_second(self, sp, e, q):
        sp.dma_start(self.w2[q][:], self.of(e)[:, self.N1:self.N1 + FC * D]).then_inc(self.w2_in[q], 16)

    def high(self, act, q, turn):
        act.wait_ge(self.w_in[q], 16 * turn)
        self.nc.scalar.activation(self.wh[q][:], self.raw[q][:], ACT.Copy).then_inc(self.wh_ok, 1)

    def low(self, dve, e, q):
        dve.wait_ge(self.wh_ok, e + 1)
        self.nc.vector.tensor_tensor(self.wl[q][:], self.raw[q][:], self.wh[q][:].bitcast(f32), ALU.subtract).then_inc(self.wl_ok, 1)


def route(nc, io, s, layer, w):
    sem = s.sem
    pre = f"g{layer}_"
    with ExitStack() as local:
        def lb(name, shape, dt=f32):
            return local.enter_context(nc.sbuf_tensor(pre + name, shape, dt))
        BLOCKS = TOKENS // 512
        top, total, inv, rank = (lb(n, [P, TILES]) for n in ("top", "total", "inv", "rank"))
        ex, gate, cand = (lb(n, [P, TILES, E]) for n in ("ex", "gate", "cand"))
        mask, pos, keep, val = (lb(n, [P, 2, TILES, E]) for n in ("mask", "pos", "keep", "val"))
        per_tile, upto = lb("per_tile", [P, 2, E, TILES]), lb("upto", [P, 2, E, TILES])
        base2 = lb("base2", [P, E])
        kept, slotf, weight = (lb(n, [P, 2, TILES]) for n in ("kept", "slotf", "weight"))
        psR = s.ps[0]
        sh_ok, ex_ok, mask_ok, r_ps, slots_ok = (sem(pre + n) for n in ("sh_ok", "ex_ok", "mask_ok", "r_ps", "slots_ok"))
        order, scattered, summed = sem(pre + "order"), sem(pre + "scattered"), sem(pre + "summed")
        if layer == 0:
            wh, wl = lb("wh", [P, 2 * F], f32r), lb("wl", [P, 2 * F], f32r)
            hf, hh, hl = lb("hf", [P, FC, 512]), lb("hh", [P, FC, 512], f32r), lb("hl", [P, FC, 512], f32r)
            c, cb2 = lb("c", [P, 1]), lb("cb2", [P, D])
            hb, psY = s.ps[1:5], s.ps[5:7]
            wh_ok, wl_ok = (sem(pre + n) for n in ("wh_ok", "wl_ok"))
            h_ps, hf_ok, hh_ok, hl_ok, y_ps, y_ok = (sem(pre + n) for n in ("h_ps", "hf_ok", "hh_ok", "hl_ok", "y_ps", "y_ok"))
        with nc.Block() as block:
            @block.sync
            def _(sp):
                for q in range(2):
                    w.load_first(sp, q, q)
                    w.load_second(sp, q, q)
                if layer == 0:
                    with sp.Fori(0, BLOCKS) as i:
                        sp.wait_ge(y_ok, i + 1)
                        sp.dma_start(io["sums0"][0:TOKENS, :].rearrange("(t p) d -> p t d", p=P)[:, bass.ds(4 * i, 4), :],
                                     s.X[:, bass.ds(4 * i, 4), :]).then_inc(summed, 16)
                else:
                    sp.dma_start(io["sums1"][0:TOKENS, :].rearrange("(t p) d -> p t d", p=P), s.X[:]).then_inc(summed, 16)
                sp.wait_ge(scattered, 16 * 2 * TILES)
                w.load_rows(sp, 0, 0)
                sp.wait_ge(summed, 16 * (BLOCKS if layer == 0 else 1))

            @block.scalar
            def _(act):
                A = nc.scalar.activation
                if layer == 0:
                    A(s.warm[:, 0:1], s.c("ones")[:, 0:1], ACT.Exp)
                act.wait_ge(sh_ok, 1)
                A(ex[:], ex[:], ACT.Exp).then_inc(ex_ok, 1)
                if layer == 0:
                    act.wait_ge(s.shared_in, 16)
                    A(wh[:], s.shared_w[:], ACT.Copy).then_inc(wh_ok, 1)
                w.high(act, 0, 1)
                A(s.warm[:, 1:2], s.c("ones")[:, 0:1], ACT.Silu)
                if layer == 0:
                    act.wait_ge(s.bias_in, 16)
                    with act.Fori(0, BLOCKS) as i:
                        for k in range(FC):
                            act.wait_ge(h_ps, FC * i + k + 1)
                            A(hf[:, k, :], hb[k][:], ACT.Silu, bias=s.bias[:, FC * E + k:FC * E + k + 1]).then_inc(hf_ok, 1)
                            act.wait_ge(hf_ok, FC * i + k + 1)
                            A(hh[:, k, :], hf[:, k, :], ACT.Copy).then_inc(hh_ok, 1)

            @block.gpsimd
            def _(pool):
                pool.wait_ge(slots_ok, 1)
                for t in range(TILES):
                    for k in range(2):
                        pool.indirect_dma_start(out=io[f"slots{layer}"], out_offset=bass.IndirectOffsetOnAxis(ap=s.slot[k][:, t:t + 1], axis=0),
                                                in_=s.XN[:, t, :], in_offset=None, bounds_check=SLOTS - 1, oob_is_err=False).then_inc(scattered, 16)
                pool.wait_ge(scattered, 16 * 2 * TILES)

            @block.vector
            def _(dve):
                o = Order(dve, order)

                def step(ins):
                    o.mark(ins)
                    o.wait()

                def b3(t):
                    return t.unsqueeze(2).broadcast_to([P, TILES, E])

                def rows(c):
                    return s.c(c).unsqueeze(1).broadcast_to([P, TILES, E])

                V = nc.vector
                logits = s.LG[:]
                if layer == 1:
                    step(V.tensor_scalar(logits, logits, -1e4, 1e4, ALU.max, ALU.min))
                step(V.tensor_reduce(top[:], logits, AX.X, ALU.max))
                V.tensor_tensor(ex[:], logits, b3(top[:]), ALU.subtract).then_inc(sh_ok, 1)
                if layer == 0:
                    step(V.tensor_scalar(c[:], s.tg[:, 2:3], 0.1, None, ALU.mult))
                    dve.wait_ge(s.bias_in, 16)
                    step(V.tensor_scalar(cb2[:], s.bias[:, FC * (E + 1) + D * E:FC * (E + 1) + D * (E + 1)], c[:, 0:1], None, ALU.mult))
                dve.wait_ge(ex_ok, 1)
                step(V.tensor_reduce(total[:], ex[:], AX.X, ALU.add))
                if layer == 1:
                    step(V.tensor_scalar(total[:], total[:], 1e-12, None, ALU.add))
                step(V.reciprocal(inv[:], total[:]))
                step(V.tensor_tensor(gate[:], ex[:], b3(inv[:]), ALU.mult))
                for k in range(2):
                    left = gate if k == 0 else ex
                    if k == 1 and layer == 0:
                        step(V.tensor_tensor(cand[:], gate[:], mask[:, 0], ALU.mult))
                        step(V.tensor_tensor(ex[:], gate[:], cand[:], ALU.subtract))
                    elif k == 1:
                        step(V.scalar_tensor_tensor(ex[:].rearrange("p t e -> p (t e)"), mask[:, 0].rearrange("p t e -> p (t e)"), -2.0,
                                                    gate[:].rearrange("p t e -> p (t e)"), ALU.mult, ALU.add))
                    step(V.tensor_reduce(top[:], left[:], AX.X, ALU.max))
                    step(V.tensor_tensor(cand[:], left[:], b3(top[:]), ALU.is_equal))
                    step(V.tensor_tensor(cand[:], cand[:], rows("rev"), ALU.mult))
                    step(V.tensor_reduce(rank[:], cand[:], AX.X, ALU.max))
                    ins = V.tensor_tensor(mask[:, k], rows("rev"), b3(rank[:]), ALU.is_equal)
                    step(ins) if k == 0 else ins.then_inc(mask_ok, 1)
                if layer == 0:
                    dve.wait_ge(wh_ok, 1)
                    V.tensor_tensor(wl[:], s.shared_w[:], wh[:].bitcast(f32), ALU.subtract).then_inc(wl_ok, 1)
                dve.wait_ge(r_ps, 1)
                step(V.tensor_copy(per_tile[:, 0], psR[:, 256:384].rearrange("p (t e) -> p e t", t=TILES)))
                step(V.tensor_copy(per_tile[:, 1], psR[:, 384:512].rearrange("p (t e) -> p e t", t=TILES)))
                flat = "p k e t -> p (k e t)"
                step(V.tensor_tensor_scan(upto[:].rearrange(flat), s.c("restart"), per_tile[:].rearrange(flat), 0.0, ALU.mult, ALU.add))
                if layer == 0:
                    step(V.tensor_scalar(base2[:], upto[:, 0, :, TILES - 1], float(CAP), None, ALU.min))
                step(V.tensor_tensor(per_tile[:].rearrange(flat), upto[:].rearrange(flat), per_tile[:].rearrange(flat), ALU.subtract))
                for k in range(2):
                    step(V.tensor_tensor(pos[:, k], psR[:, 128 * k:128 * k + 128].rearrange("p (t e) -> p t e", e=E),
                                         per_tile[:, k].rearrange("p e t -> p t e"), ALU.add))
                if layer == 0:
                    step(V.tensor_tensor(pos[:, 1], pos[:, 1], base2[:].unsqueeze(1).broadcast_to([P, TILES, E]), ALU.add))
                else:
                    step(V.tensor_tensor(pos[:, 0], pos[:, 0], pos[:, 1], ALU.add))
                    step(V.tensor_copy(pos[:, 1], pos[:, 0]))
                all_ = "p k t e -> p (k t) e"
                one = "p k t e -> p (k t e)"
                step(V.scalar_tensor_tensor(keep[:].rearrange(one), pos[:].rearrange(one), float(CAP), mask[:].rearrange(one), ALU.is_lt, ALU.mult))
                step(V.tensor_reduce(kept[:].rearrange("p k t -> p (k t)"), keep[:].rearrange(all_), AX.X, ALU.add))
                step(V.tensor_tensor(val[:].rearrange(all_), pos[:].rearrange(all_), s.c("expert_base").unsqueeze(1).broadcast_to([P, 2 * TILES, E]), ALU.add))
                step(V.tensor_tensor(val[:].rearrange(one), val[:].rearrange(one), keep[:].rearrange(one), ALU.mult))
                step(V.tensor_reduce(slotf[:].rearrange("p k t -> p (k t)"), val[:].rearrange(all_), AX.X, ALU.add))
                step(V.scalar_tensor_tensor(slotf[:].rearrange("p k t -> p (k t)"), kept[:].rearrange("p k t -> p (k t)"), -2.0 * SLOTS,
                                            slotf[:].rearrange("p k t -> p (k t)"), ALU.mult, ALU.add))
                for k in range(2):
                    step(V.tensor_scalar(s.slot[k][:], slotf[:, k], 2.0 * SLOTS, None, ALU.add))
                for k in range(2):
                    step(V.tensor_tensor(val[:, k], keep[:, k], gate[:], ALU.mult))
                step(V.tensor_reduce(weight[:].rearrange("p k t -> p (k t)"), val[:].rearrange(all_), AX.X, ALU.add))
                if layer == 0:
                    step(V.tensor_tensor(total[:], weight[:, 0], weight[:, 1], ALU.add))
                    step(V.tensor_scalar(total[:], total[:], float(np.finfo(np.float32).eps), None, ALU.max))
                    step(V.reciprocal(inv[:], total[:]))
                    for k in range(2):
                        step(V.tensor_tensor(weight[:, k], weight[:, k], inv[:], ALU.mult))
                for k in range(2):
                    step(V.tensor_scalar(s.share[k][:], weight[:, k], s.tg[:, 2 + layer:3 + layer], None, ALU.mult))
                step(V.tensor_copy(s.XN[:, :, D].bitcast(u32), s.c("token")))
                for k in range(2):
                    step(V.tensor_copy(s.XN[:, :, D + 1 + k], s.share[k][:]))
                V.tensor_copy(s.XN[:, :, D + 3], s.slot[0][:]).then_inc(slots_ok, 1)
                w.low(dve, 0, 0)
                if layer == 0:
                    DO, done = 2, o.n
                    with dve.Fori(0, BLOCKS // 2) as g:
                        p = Order(dve, order, DO * g + done)
                        for r in range(2):
                            i = 2 * g + r
                            for k in range(FC):
                                dve.wait_ge(hh_ok, FC * i + k + 1)
                                V.tensor_tensor(hl[:, k, :], hf[:, k, :], hh[:, k, :].bitcast(f32), ALU.subtract).then_inc(hl_ok, 1)
                            dve.wait_ge(y_ps, i + 1)
                            at = bass.ds(4 * i, 4)
                            p.mark(V.scalar_tensor_tensor(s.X[:, at, :].rearrange("p t d -> p (t d)"), psY[r][:], c[:, 0:1],
                                                          s.X[:, at, :].rearrange("p t d -> p (t d)"), ALU.mult, ALU.add))
                            p.wait()
                            V.tensor_tensor(s.X[:, at, :], s.X[:, at, :], cb2[:].unsqueeze(1).broadcast_to([P, 4, D]), ALU.add).then_inc(y_ok, 1)
                        assert p.n == DO

            @block.tensor
            def _(pe):
                pe.wait_ge(mask_ok, 1)
                flat = mask[:].rearrange("p k t e -> p (k t e)")
                nc.tensor.matmul(psR[:, 0:256], s.c("before"), flat, start=True, stop=True)
                nc.tensor.matmul(psR[:, 256:512], s.c("ones"), flat, start=True, stop=True).then_inc(r_ps, 1)
                if layer == 0:
                    pe.wait_ge(wl_ok, 1)
                    with pe.Fori(0, BLOCKS // 2) as g:
                        for r in range(2):
                            i = 2 * g + r
                            at = bass.ds(512 * i, 512)
                            for k in range(FC):
                                f = slice(P * k, P * k + P)
                                nc.tensor.matmul(hb[k][:], wh[:, f], s.XTH[:, at], start=True, stop=False)
                                nc.tensor.matmul(hb[k][:], wh[:, f], s.XTL[:, at], start=False, stop=False)
                                nc.tensor.matmul(hb[k][:], wl[:, f], s.XTH[:, at], start=False, stop=True).then_inc(h_ps, 1)
                            for k in range(FC):
                                pe.wait_ge(hl_ok, FC * i + k + 1)
                                f = slice(F + D * k, F + D * k + D)
                                for j in range(4):
                                    tok, out = slice(P * j, P * j + P), psY[r][:, P * j:P * j + P]
                                    nc.tensor.matmul(out, hh[:, k, tok], wh[:, f], start=k == 0 and j == 0, stop=False, skip_group_check=True)
                                    nc.tensor.matmul(out, hh[:, k, tok], wl[:, f], start=False, stop=False, skip_group_check=True)
                                    last = nc.tensor.matmul(out, hl[:, k, tok], wh[:, f], start=False, stop=k == FC - 1, skip_group_check=True)
                            last.then_inc(y_ps, 1)


def experts(nc, io, s, layer, w):
    sem = s.sem
    pre = f"e{layer}_"
    U = 2 * FC
    ADDS = 16 * ST
    with ExitStack() as local:
        def lb(name, shape, dt=f32):
            return local.enter_context(nc.sbuf_tensor(pre + name, shape, dt))

        def two(name, shape, dt=f32):
            return [lb(f"{name}{q}", shape, dt) for q in range(2)]
        wh, wl, w2, rows, w2_in, rows_in, wh_ok, wl_ok = w.wh, w.wl, w.w2, w.rows, w.w2_in, w.rows_in, w.wh_ok, w.wl_ok
        y, token = two("y", [P, ST, D]), two("token", [P, ST], u32)
        xh, xl = lb("xh", [D, CAP], f32r), lb("xl", [D, CAP], f32r)
        sg = [lb(f"sg{r}", [P, HALF]) for r in range(4)]
        hs = lb("hs", [P, FC, CAP])
        first, part, rest = lb("first", [P, ST]), lb("part", [P, ST]), lb("rest", [P, ST])
        hb, psX, psY = s.ps[0:4], s.ps[4:6], s.ps[6:8]
        added = [sem(f"{pre}added{q}") for q in range(2)]
        x_ps, xh_ok, xl_ok = (sem(pre + n) for n in ("x_ps", "xh_ok", "xl_ok"))
        h_ps, sg_ok, hs_ok, y_ps, y_ok, order, settled = (sem(pre + n) for n in ("h_ps", "sg_ok", "hs_ok", "y_ps", "y_ok", "order", "settled"))
        sums = io[f"sums{layer}"]

        def each(eng, body):
            with eng.Fori(0, E // 2 - 1) as i:
                body(i, 0, True, True)
                body(i, 1, True, True)
            body(E // 2 - 1, 0, True, False)
            body(E // 2 - 1, 1, False, False)

        def unit(n):
            return n // 2, slice(HALF * (n % 2), HALF * (n % 2) + HALF)

        with nc.Block() as block:
            @block.sync
            def _(sp):
                def body(i, q, more, two_more):
                    e = 2 * i + q
                    if more:
                        sp.wait_ge(y_ok, e + 1)
                        w.load_rows(sp, e + 1, 1 - q)
                    if two_more:
                        sp.wait_ge(wl_ok, e + 1)
                        w.load_first(sp, e + 2, q)
                        sp.wait_ge(y_ps, e + 1)
                        w.load_second(sp, e + 2, q)
                each(sp, body)

            @block.scalar
            def _(act):
                def high_rows(e):
                    act.wait_ge(x_ps, e + 1)
                    nc.scalar.activation(xh[:, 0:512], psX[0][:], ACT.Copy)
                    nc.scalar.activation(xh[:, 512:CAP], psX[1][:, 0:P], ACT.Copy).then_inc(xh_ok, 1)

                high_rows(0)

                def body(i, q, more, two_more):
                    e = 2 * i + q
                    for n in range(U):
                        k, half = unit(n)
                        if layer == 0:
                            wait_apart(act, h_ps, U * e + n + 1)
                            nc.scalar.activation(hs[:, k, half], hb[n % 4][:, 0:HALF], ACT.Silu,
                                                 bias=s.bias[:, bass.ds(FC * e + k, 1)]).then_inc(hs_ok, 1)
                        else:
                            act.wait_ge(h_ps, U * e + n + 1)
                            if n >= 4:
                                act.wait_ge(hs_ok, U * e + n - 3)
                            nc.scalar.activation(sg[n % 4][:], hb[2 * (n % 2)][:, 0:HALF], ACT.Silu).then_inc(sg_ok, 1)
                        if n == 3 and more:
                            w.high(act, 1 - q, i + 1 + q)
                    if more:
                        high_rows(e + 1)
                each(act, body)

            @block.gpsimd
            def _(pool):
                pool.sem_inc(settled, 2)

                def body(i, q, more, two_more):
                    wait_apart(pool, y_ok, 2 * i + q + 2)
                    for j in range(ST):
                        pool.indirect_dma_start(out=sums, out_offset=bass.IndirectOffsetOnAxis(ap=token[q][:, j:j + 1], axis=0),
                                                in_=y[q][:, j, :], in_offset=None, bounds_check=TOKENS + CAP - 1,
                                                oob_is_err=True, compute_op=ALU.add).then_inc(added[q], 16)
                    pool.wait_ge(added[q], ADDS * (i + 1))
                    pool.sem_inc(settled, 1)
                each(pool, body)

            @block.vector
            def _(dve):
                V = nc.vector

                def low_rows(e):
                    dve.wait_ge(xh_ok, e + 1)
                    V.tensor_tensor(xl[:, 0:512], psX[0][:], xh[:, 0:512].bitcast(f32), ALU.subtract)
                    V.tensor_tensor(xl[:, 512:CAP], psX[1][:, 0:P], xh[:, 512:CAP].bitcast(f32), ALU.subtract).then_inc(xl_ok, 1)

                dve.sem_inc(y_ok, 1)
                low_rows(0)
                OPS = 5

                def body(i, q, more, two_more):
                    e = 2 * i + q
                    o = Order(dve, order, OPS * e)
                    for n in range(U):
                        if layer == 1:
                            k, half = unit(n)
                            dve.wait_ge(sg_ok, U * e + n + 1)
                            V.tensor_tensor(hs[:, k, half], sg[n % 4][:], hb[2 * (n % 2) + 1][:, 0:HALF], ALU.mult).then_inc(hs_ok, 1)
                        if n == 4 and more:
                            w.low(dve, e + 1, 1 - q)
                    if more:
                        low_rows(e + 1)
                    dve.wait_ge(rows_in[q], 16 * i + 16)
                    dve.wait_ge(settled, e + 1)
                    meta = lambda c: rows[q][:, :, D + c]
                    V.tensor_copy(token[q][:], meta(0).bitcast(u32))
                    o.mark(V.tensor_tensor(first[:], meta(3), s.c("slot")[:, bass.ds(ST * e, ST)], ALU.is_equal))
                    o.wait()
                    o.mark(V.tensor_tensor(part[:], meta(1), first[:], ALU.mult))
                    o.mark(V.tensor_scalar(rest[:], first[:], -1.0, 1.0, ALU.mult, ALU.add))
                    o.wait()
                    o.mark(V.tensor_tensor(rest[:], rest[:], meta(2), ALU.mult))
                    o.wait()
                    o.mark(V.tensor_tensor(part[:], part[:], rest[:], ALU.add))
                    o.wait()
                    assert o.n == OPS
                    dve.wait_ge(y_ps, e + 1)
                    for at, bank in ((slice(0, 4), psY[0][:]), (slice(4, ST), psY[1][:, 0:D])):
                        n = at.stop - at.start
                        weight = part[:, at].unsqueeze(2).broadcast_to([P, n, D])
                        made = bank.rearrange("p (s d) -> p s d", d=D)
                        if layer == 0:
                            b2 = s.bias[:, bass.ds(FC * (E + 1) + D * e, D)].unsqueeze(1).broadcast_to([P, n, D])
                            V.tensor_tensor(y[q][:, at, :], made, b2, ALU.add).then_inc(order_b, 1)
                            dve.wait_ge(order_b, 2 * e + (1 if n > 1 else 2))
                            last = V.tensor_tensor(y[q][:, at, :], y[q][:, at, :], weight, ALU.mult)
                        else:
                            last = V.tensor_tensor(y[q][:, at, :], made, weight, ALU.mult)
                    last.then_inc(y_ok, 1)
                order_b = sem(pre + "order_b")
                each(dve, body)

            @block.tensor
            def _(pe):
                def transpose_rows(e, q, turn):
                    pe.wait_ge(rows_in[q], 16 * turn)
                    for j in range(ST):
                        last = nc.tensor.transpose(psX[j // 4][:, P * (j % 4):P * (j % 4) + P], rows[q][:, j, 0:D], s.c("ident"))
                    last.then_inc(x_ps, 1)

                def hidden(e, q, n):
                    k, half = unit(n)
                    ring = 4 if layer == 0 else 2
                    if n >= ring:
                        pe.wait_ge(hs_ok, U * e + n - ring + 1)
                    for g in range(1 + layer):
                        bank = hb[n % 4] if layer == 0 else hb[2 * (n % 2) + g]
                        f = slice(F * g + P * k, F * g + P * k + P)
                        nc.tensor.matmul(bank[:, 0:HALF], wh[q][:, f], xh[:, half], start=True, stop=False)
                        nc.tensor.matmul(bank[:, 0:HALF], wh[q][:, f], xl[:, half], start=False, stop=False)
                        last = nc.tensor.matmul(bank[:, 0:HALF], wl[q][:, f], xh[:, half], start=False, stop=True)
                    last.then_inc(h_ps, 1)

                def output(e, q, k):
                    pe.wait_ge(hs_ok, U * e + 2 * k + 2)
                    for j in range(ST):
                        last = nc.tensor.matmul(psY[j // 4][:, P * (j % 4):P * (j % 4) + P], hs[:, k, P * j:P * j + P],
                                                w2[q][:, D * k:D * k + D], start=k == 0 and j % 4 == 0, stop=k == FC - 1,
                                                skip_group_check=True)
                    return last

                transpose_rows(0, 0, 1)

                def body(i, q, more, two_more):
                    e = 2 * i + q
                    pe.wait_ge(xl_ok, e + 1)
                    pe.wait_ge(wl_ok, e + 1)
                    for n in range(4):
                        hidden(e, q, n)
                    pe.wait_ge(y_ok, e + 1)
                    pe.wait_ge(w2_in[q], 16 * i + 16)
                    output(e, q, 0)
                    for n in range(4, 6):
                        hidden(e, q, n)
                    output(e, q, 1)
                    for n in range(6, 8):
                        hidden(e, q, n)
                    if more:
                        transpose_rows(e + 1, 1 - q, i + 1 + q)
                    output(e, q, 2)
                    output(e, q, 3).then_inc(y_ps, 1)
                each(pe, body)


def softmax_attention(nc, io, s):
    HD, PARTS = 2, 4
    TG = HD * PARTS
    N = TILES // TG
    sem = s.sem
    scale = float(D) ** -0.5
    with ExitStack() as local:
        def lb(name, shape, dt=f32):
            return local.enter_context(nc.sbuf_tensor("c_" + name, shape, dt))

        def each(name, shape, dt=f32):
            return [lb(f"{name}{h}", shape, dt) for h in range(PARTS)]
        ctxT, xn, xnT = each("ctxT", [D, HD * P]), each("xn", [P, HD, D]), each("xnT", [D, HD * P])
        st, mv, ve, rs = each("st", [P, HD, 6]), each("mv", [P, HD, 2]), each("ve", [P, HD]), each("rs", [P, HD])
        QT, KT, V = each("QT", [D, HD * P]), each("KT", [D, HD * P]), each("V", [P, HD, D])
        sc, Pb, PT = each("sc", [P, HD, SEQ]), each("Pb", [P, HD, P]), each("PT", [P, HD * P])
        mx, sm = each("mx", [P, HD]), each("sm", [P, HD])
        valid, masked = lb("valid", [P, TILES, SEQ]), lb("masked", [P, TILES, SEQ])
        keymask = lb("keymask", [P, TILES, SEQ], i32)
        minus_half = lb("minus_half", [P, HD])
        psX, psY = s.ps[0::2], s.ps[1::2]
        ctx_in, rows_in = [sem(f"c_ctx_in{h}") for h in range(PARTS)], [sem(f"c_rows_in{h}") for h in range(PARTS)]
        sums = io["sums0"][0:TOKENS, :].rearrange("(t p) d -> p t d", p=P)
        names = ("mask_in zeros_ok agg_ok rs_ok xn_ok xnT_ps xnT_ok q_ps q_ok kv_ps kT_ok v_ok s_ps sc_ok "
                 "p_ok pT_ps pT_ok o_ps x3n_ok x3T_ps x3T_ok lg_ps lg_ok dve_order").split()
        m = {k: sem("c_" + k) for k in names}
        with nc.Block() as block:
            @block.sync
            def _(sp):
                def load_rows(i, h):
                    at = bass.ds(TG * i + HD * h, HD)
                    sp.dma_start(s.X[:, at, :], sums[:, at, :]).then_inc(rows_in[h], 16)

                def load_context(i, h):
                    sp.dma_start(ctxT[h][:], io["ctxT"][:, bass.ds(P * (TG * i + HD * h), P * HD)]).then_inc(ctx_in[h], 16)

                for h in range(PARTS):
                    load_rows(0, h)
                    load_context(0, h)
                    if h == 0:
                        sp.dma_start(keymask[:].rearrange("p t k -> p (t k)"), io["keymask"]).then_inc(m["mask_in"], 16)
                with sp.Fori(1, N) as i:
                    for h in range(PARTS):
                        sp.wait_ge(rows_in[h], 16 * i)
                        load_rows(i, h)
                        sp.wait_ge(m["kv_ps"], PARTS * (i - 1) + h + 1)
                        load_context(i, h)

            @block.gpsimd
            def _(pool):
                for h in range(PARTS):
                    nc.gpsimd.memset(Pb[h][:], 0.0)
                nc.gpsimd.memset(minus_half[:], -0.5).then_inc(m["zeros_ok"], 1)
                pool.wait_ge(m["zeros_ok"], 1)
                with pool.Fori(0, N) as i:
                    for k in range(2):
                        for h in range(PARTS):
                            pool.wait_ge(m["agg_ok"], 2 * PARTS * i + PARTS * k + h + 1)
                            nc.gpsimd.tensor_tensor(rs[h][:], ve[h][:], minus_half[:], ALU.pow).then_inc(m["rs_ok"], 1)

            @block.scalar
            def _(act):
                A = nc.scalar.activation
                A(s.warm[:, 0:1], s.c("ones")[:, 0:1], ACT.Exp)
                act.wait_ge(m["zeros_ok"], 1)
                act.sem_inc(m["lg_ok"], PARTS)
                with act.Fori(0, N) as i:
                    at = lambda h: PARTS * i + h + 1
                    for h in range(PARTS):
                        act.wait_ge(m["kv_ps"], at(h))
                        A(KT[h][:], psX[h][:, 0:256], ACT.Identity, bias=s.v("bk")).then_inc(m["kT_ok"], 1)
                    for h in range(PARTS):
                        act.wait_ge(m["xnT_ps"], at(h))
                        A(xnT[h][:], psX[h][:, 256:512], ACT.Copy).then_inc(m["xnT_ok"], 1)
                    for h in range(PARTS):
                        act.wait_ge(m["q_ps"], at(h))
                        A(QT[h][:], psX[h][:, 0:256], ACT.Identity, bias=s.v("bq")).then_inc(m["q_ok"], 1)
                    for h in range(PARTS):
                        act.wait_ge(m["sc_ok"], at(h))
                        for b in range(2):
                            rows = slice(SEQ * b, SEQ * b + SEQ)
                            last = A(Pb[h][rows, :, rows], sc[h][rows, :, :], ACT.Exp, scale=scale)
                        last.then_inc(m["p_ok"], 1)
                    for h in range(PARTS):
                        act.wait_ge(m["pT_ps"], at(h))
                        A(PT[h][:], psX[h][:, 256:512], ACT.Copy).then_inc(m["pT_ok"], 1)

                    def logits(h):
                        act.wait_ge(m["lg_ps"], at(h))
                        A(s.LG[:, bass.ds(TG * i + HD * h, HD), :], psY[h][:, 256:256 + HD * E].rearrange("p (t e) -> p t e", e=E),
                          ACT.Copy).then_inc(m["lg_ok"], 1)

                    for h in range(PARTS):
                        act.wait_ge(m["x3n_ok"], at(h))
                        A(s.XN[:, bass.ds(TG * i + HD * h, HD), 0:D], xn[h][:], ACT.Copy)
                        act.wait_ge(m["x3T_ps"], at(h))
                        A(xnT[h][:], psY[h][:, 0:256], ACT.Copy).then_inc(m["x3T_ok"], 1)
                        if h:
                            logits(h - 1)
                    logits(PARTS - 1)

            @block.vector
            def _(dve):
                V_ = nc.vector
                o = Order(dve, m["dve_order"])
                dve.wait_ge(m["mask_in"], 16)
                o.mark(V_.tensor_copy(masked[:], keymask[:]))
                o.wait()
                o.mark(V_.tensor_scalar(valid[:], masked[:], 0.0, None, ALU.not_equal))
                o.wait()
                big = 1e9 / scale
                o.mark(V_.tensor_scalar(masked[:], valid[:], big, -big, ALU.mult, ALU.add))
                o.wait()
                before = o.n
                DO = 72
                with dve.Fori(0, N) as i:
                    o = Order(dve, m["dve_order"], DO * i + before)
                    at = lambda h: PARTS * i + h + 1
                    tile = lambda h, j: s.X[:, bass.ds(TG * i + HD * h + j, 1), :].rearrange("p a d -> p (a d)")

                    def variance(h):
                        for j in range(HD):
                            o.mark(V_.bn_stats(st[h][:, j, :], tile(h, j)))
                        o.wait_apart()
                        for j in range(HD):
                            o.mark(V_.bn_aggr(mv[h][:, j, :], st[h][:, j, :]))
                        o.wait()

                    for h in range(PARTS):
                        wait_apart(dve, rows_in[h], 16 * i + 16)
                        variance(h)
                        V_.tensor_scalar(ve[h][:], mv[h][:, :, 1], EPS, None, ALU.add).then_inc(m["agg_ok"], 1)
                    for h in range(PARTS):
                        dve.wait_ge(m["kv_ps"], at(h))
                        V_.tensor_tensor(V[h][:], psY[h][:, 0:256].rearrange("p (t d) -> p t d", d=D),
                                         s.v("bv").unsqueeze(1).broadcast_to([P, HD, D]), ALU.add).then_inc(m["v_ok"], 1)
                    for h in range(PARTS):
                        dve.wait_ge(m["rs_ok"], 2 * PARTS * i + h + 1)
                        for j in range(HD):
                            last = V_.tensor_scalar(xn[h][:, j, :], tile(h, j), mv[h][:, j, 0:1], rs[h][:, j:j + 1], ALU.subtract, ALU.mult)
                        last.then_inc(m["xn_ok"], 1)
                    for h in range(PARTS):
                        dve.wait_ge(m["s_ps"], at(h))
                        tiles = bass.ds(TG * i + HD * h, HD)
                        o.mark(V_.tensor_tensor(sc[h][:], psY[h][:, 256:384].rearrange("p (t k) -> p t k", k=SEQ), valid[:, tiles, :], ALU.mult))
                        o.wait()
                        o.mark(V_.tensor_tensor(sc[h][:], sc[h][:], masked[:, tiles, :], ALU.add))
                        o.wait()
                        o.mark(V_.tensor_reduce(mx[h][:], sc[h][:], AX.X, ALU.max))
                        o.wait()
                        V_.tensor_tensor(sc[h][:], sc[h][:], mx[h][:].unsqueeze(2).broadcast_to([P, HD, SEQ]), ALU.subtract).then_inc(m["sc_ok"], 1)
                    for h in range(PARTS):
                        dve.wait_ge(m["p_ok"], at(h))
                        o.mark(V_.tensor_reduce(sm[h][:], Pb[h][:], AX.X, ALU.add))
                        o.wait()
                        o.mark(V_.reciprocal(sm[h][:], sm[h][:]))
                        o.wait()
                        o.mark(V_.tensor_scalar(sm[h][:], sm[h][:], s.tg[:, 1:2], None, ALU.mult))
                    for h in range(PARTS):
                        dve.wait_ge(m["o_ps"], at(h))
                        o.wait()
                        for j in range(HD):
                            o.mark(V_.scalar_tensor_tensor(tile(h, j), psX[h][:, 128 * j:128 * j + 128], sm[h][:, j:j + 1], tile(h, j),
                                                           ALU.mult, ALU.add))
                        o.wait_apart()
                        variance(h)
                        V_.tensor_scalar(ve[h][:], mv[h][:, :, 1], 1.0 + EPS, EPS * EPS, ALU.mult, ALU.add).then_inc(m["agg_ok"], 1)
                        for j in range(HD):
                            o.mark(V_.scalar_tensor_tensor(xn[h][:, j, :], tile(h, j), mv[h][:, j, 0:1], s.v("gamma1"), ALU.subtract, ALU.mult))
                    for h in range(PARTS):
                        dve.wait_ge(m["rs_ok"], 2 * PARTS * i + PARTS + h + 1)
                        o.wait()
                        for j in range(HD):
                            last = V_.scalar_tensor_tensor(xn[h][:, j, :], xn[h][:, j, :], rs[h][:, j:j + 1], s.v("beta1"), ALU.mult, ALU.add)
                        last.then_inc(m["x3n_ok"], 1)
                    assert o.n == DO, o.n

            @block.tensor
            def _(pe):
                mm = nc.tensor.matmul
                with pe.Fori(0, N) as i:
                    at = lambda h: PARTS * i + h + 1
                    for h in range(PARTS):
                        pe.wait_ge(ctx_in[h], 16 * i + 16)
                        pe.wait_ge(m["lg_ok"], at(h))
                        mm(psX[h][:, 0:256], s.w("wk1"), ctxT[h][:], start=True, stop=True)
                        for j in range(HD):
                            last = mm(psY[h][:, 128 * j:128 * j + 128], ctxT[h][:, 128 * j:128 * j + 128], s.w("wv1"), start=True, stop=True)
                        last.then_inc(m["kv_ps"], 1)
                    for h in range(PARTS):
                        pe.wait_ge(m["xn_ok"], at(h))
                        pe.wait_ge(m["kT_ok"], at(h))
                        for j in range(HD):
                            last = nc.tensor.transpose(psX[h][:, 256 + 128 * j:384 + 128 * j], xn[h][:, j, :], s.c("ident"))
                        last.then_inc(m["xnT_ps"], 1)
                    for h in range(PARTS):
                        pe.wait_ge(m["xnT_ok"], at(h))
                        mm(psX[h][:, 0:256], s.w("wq1"), xnT[h][:], start=True, stop=True).then_inc(m["q_ps"], 1)
                    for h in range(PARTS):
                        pe.wait_ge(m["q_ok"], at(h))
                        pe.wait_ge(m["v_ok"], at(h))
                        for j in range(HD):
                            for b in range(2):
                                tok = slice(128 * j + SEQ * b, 128 * j + SEQ * b + SEQ)
                                last = mm(psY[h][SEQ * b:SEQ * b + SEQ, 256 + SEQ * j:256 + SEQ * j + SEQ], QT[h][:, tok], KT[h][:, tok],
                                          start=True, stop=True)
                        last.then_inc(m["s_ps"], 1)
                    for h in range(PARTS):
                        pe.wait_ge(m["p_ok"], at(h))
                        for j in range(HD):
                            last = nc.tensor.transpose(psX[h][:, 256 + 128 * j:384 + 128 * j], Pb[h][:, j, :], s.c("ident"))
                        last.then_inc(m["pT_ps"], 1)
                    for h in range(PARTS):
                        pe.wait_ge(m["pT_ok"], at(h))
                        for j in range(HD):
                            last = mm(psX[h][:, 128 * j:128 * j + 128], PT[h][:, 128 * j:128 * j + 128], V[h][:, j, :], start=True, stop=True)
                        last.then_inc(m["o_ps"], 1)

                    def logits(h):
                        pe.wait_ge(m["x3T_ok"], at(h))
                        for j in range(HD):
                            last = mm(psY[h][:, 256 + E * j:256 + E * j + E], xnT[h][:, 128 * j:128 * j + 128], s.w("router1"), start=True, stop=True)
                        last.then_inc(m["lg_ps"], 1)

                    for h in range(PARTS):
                        pe.wait_ge(m["x3n_ok"], at(h))
                        for j in range(HD):
                            last = nc.tensor.transpose(psY[h][:, 128 * j:128 * j + 128], xn[h][:, j, :], s.c("ident"))
                        last.then_inc(m["x3T_ps"], 1)
                        if h:
                            logits(h - 1)
                    logits(PARTS - 1)


def layout(i):
    f = lambda k: np.asarray(i[k])
    row = lambda a: np.broadcast_to(a.reshape(1, -1), (P, a.size))
    e0 = lambda k, n: f(k)
    shape = np.zeros((P, columns(SHAPE_COLS)[1]), np.float32)
    sc = columns(SHAPE_COLS)[0]
    put = lambda k, a: shape.__setitem__((slice(None), slice(sc[k][0], sc[k][0] + sc[k][1])), a)
    put("ident", np.eye(P))
    put("before", np.triu(np.ones((P, P)), 1))
    put("ones", 1.0)
    put("heads", np.kron(np.eye(D // HEAD), np.ones((HEAD, HEAD))))
    put("own", np.kron(np.ones((4, 1)), np.kron(np.eye(4), np.ones((HEAD, 1)))))
    put("rev", E - np.arange(E))
    put("expert_base", CAP * np.arange(E))
    put("spare", TOKENS + P * np.arange(ST)[None, :] + np.arange(P)[:, None])
    put("token", P * np.arange(TILES)[None, :] + np.arange(P)[:, None])
    put("slot", P * np.arange(E * ST)[None, :] + np.arange(P)[:, None])
    put("restart", (np.arange(2 * E * TILES) % TILES > 0) * 1.0)
    vec = np.concatenate([row(f("L0_xattn_ln_gamma")), row(f("L0_xattn_ln_beta")), row(f("L0_xattn_dense_b")), row(f("L1_xattn_bv")),
                          row(f("L1_ffn_ln_gamma")), row(f("L1_ffn_ln_beta")), f("L0_xattn_ln_gamma")[:, None],
                          f("L0_xattn_ln_beta")[:, None], f("L1_xattn_bq")[:, None], f("L1_xattn_bk")[:, None],
                          row(f("g_xattn")), row(f("g_ffn")), f("mask_BxS2_ff1").reshape(TILES, P).T,
                          np.full((P, 1), EPS, np.float32), np.full((P, 1), EPS_L0, np.float32)], axis=1)
    dense = np.broadcast_to(f("L0_xattn_dense_w").reshape(4, 4, 1, HEAD, D), (4, 4, 4, HEAD, D)).transpose(0, 2, 3, 1, 4).reshape(P, 4 * D)
    w = np.concatenate([f("L0_xattn_wq"), f("L0_xattn_wk"), f("L0_xattn_wv"), dense, f("L0_ffn_router_w"),
                        f("L1_xattn_Wq"), f("L1_xattn_Wk"), f("L1_xattn_Wv"), f("L1_ffn_Wr").T], axis=1)
    second = lambda a: a.reshape(-1, FC, P, D).transpose(0, 2, 1, 3).reshape(-1, P, FC * D)
    w1 = np.concatenate([f("L0_ffn_w1"), f("L0_ffn_sw1")[None]])
    w2 = np.concatenate([f("L0_ffn_w2"), f("L0_ffn_sw2")[None]])
    b1 = np.concatenate([f("L0_ffn_b1"), f("L0_ffn_sb1")[None]])
    b2 = np.concatenate([f("L0_ffn_b2"), f("L0_ffn_sb2")[None]])
    bias0 = np.concatenate([b1.reshape((E + 1) * FC, P).T, row(b2)], axis=1)
    pack1 = np.concatenate([f("L1_ffn_W12").transpose(0, 2, 1), second(f("L1_ffn_W3").transpose(0, 2, 1))], axis=2)
    return {
        "x": f("x").reshape(TOKENS, D), "ctxT": f("ctx_1024").reshape(TOKENS, D).T, "shape": shape, "vec": vec, "w": w,
        "experts0": np.concatenate([w1, second(w2)], axis=2), "bias0": bias0, "experts1": pack1,
        "keymask": np.repeat(f("mask_BxS2_ik0").reshape(TILES, 2, SEQ).transpose(1, 0, 2).reshape(2, -1), SEQ, axis=0),
    }


def declare(nc, arrays):
    io = {}
    for name, a in arrays.items():
        io[name] = nc.dram_tensor(f"in_{name}", a.shape, mybir.dt.from_np(a.dtype), kind="ExternalInput").ap()
    for k in range(2):
        io[f"slots{k}"] = nc.dram_tensor(f"slots{k}", (SLOTS, ROW), f32, kind="Internal").ap()
    io["sums0"] = nc.dram_tensor("sums0", (TOKENS + CAP, D), f32, kind="Internal").ap()
    io["sums1"] = nc.dram_tensor("out_dram", (TOKENS + CAP, D), f32, kind="ExternalOutput").ap()
    return io


def kernel(**inputs):
    import concourse.bacc as _bacc
    from concourse.bass_utils import run_bass_kernel_spmd as _run

    nc = _bacc.Bacc("TRN2", target_bir_lowering=False, num_devices=1)
    arrays = {k: np.ascontiguousarray(a) for k, a in layout(inputs).items()}
    build(nc, declare(nc, arrays))
    r = _run(nc, [{f"in_{k}": a for k, a in arrays.items()}], core_ids=[0])
    return r.results[0]["out_dram"][:TOKENS].reshape(32, SEQ, D)
```

```python
from contextlib import ExitStack

import numpy as np
import concourse.bass as bass
from concourse import mybir

P = 128
D = 128
TOKENS = 2048
TILES = TOKENS // P
SEQ = 64
E = 8
F = 512
FC = F // P
CAP = 640
ST = CAP // P
HALF = CAP // 2
SLOTS = E * CAP
ROW = D + 4
EPS = 1e-5
MASKED = 1e9 * D ** 0.5
EPS_L0 = 1e-6
HEAD = 8
STORES = (TOKENS // 512, 2)

f32 = mybir.dt.float32
f32r = mybir.dt.float32r
i32 = mybir.dt.int32
u32 = mybir.dt.uint32
ALU = mybir.AluOpType
ACT = mybir.ActivationFunctionType
AX = mybir.AxisListType

SHAPE_COLS = dict(ident=128, before=128, ones=128, heads=128, own=4, rev=E, expert_base=E,
                  restart=2 * E * TILES, restart_half=E * TILES // 2, spare=ST, token=TILES, slot=E * ST)
VEC_COLS = dict(gamma=128, beta=128, dense_b=128, bv=128, gamma1=128, beta1=128,
                gamma_t=1, beta_t=1, bq=1, bk=1, gates=4, em=TILES, eps5=1, eps6=1)
W_COLS = dict(wq=128, wkv=256, dense=512, router0=E, wq1=128, wk1=128, wv1=128, router1=E)


def columns(spec):
    at, out = 0, {}
    for k, n in spec.items():
        out[k] = (at, n)
        at += n
    return out, at


class Order:

    def __init__(self, eng, sem, before=0):
        self.eng, self.sem, self.before, self.n = eng, sem, before, 0

    def mark(self, ins):
        ins.then_inc(self.sem, 1)
        self.n += 1
        return self.n

    def wait(self, n=None):
        self.eng.wait_ge(self.sem, self.before + (self.n if n is None else n))

    def wait_apart(self, n=None):
        wait_apart(self.eng, self.sem, self.before + (self.n if n is None else n))


def build(nc, io):
    ctx = ExitStack()
    with ctx:
        def sb(name, shape, dt=f32):
            return ctx.enter_context(nc.sbuf_tensor(name, shape, dt))

        def sem(name):
            return ctx.enter_context(nc.semaphore(name))

        class S:
            pass
        s = S()
        s.sem = sem
        sc, n_sc = columns(SHAPE_COLS)
        vc, n_vc = columns(VEC_COLS)
        wc, n_wc = columns(W_COLS)
        shape_t = sb("shape_t", [P, n_sc])
        vec_t = sb("vec_t", [P, n_vc])
        w_t = sb("w_t", [P, n_wc])
        s.c = lambda k: shape_t[:, sc[k][0]:sc[k][0] + sc[k][1]]
        s.v = lambda k: vec_t[:, vc[k][0]:vc[k][0] + vc[k][1]]
        s.w = lambda k: w_t[:, wc[k][0]:wc[k][0] + wc[k][1]]
        s.shape_t, s.vec_t, s.w_t = shape_t, vec_t, w_t
        s.X = sb("rows", [P, TILES, D])
        s.XN = sb("normed", [P, TILES, ROW])
        s.XTH = sb("normed_t_high", [D, TOKENS], f32r)
        s.XTL = sb("normed_t_low", [D, TOKENS], f32r)
        s.LG = sb("logits", [P, TILES, E])
        s.tg = sb("tanh_gates", [P, 4])
        s.ps = [ctx.enter_context(nc.psum_tensor(f"bank{b}", [P, 512], f32)) for b in range(8)]
        s.bias = sb("bias", [P, (E + 1) * (FC + D)])
        s.warm = sb("warm", [P, 2])
        s.empty = sb("empty", [P, ST, ROW])
        s.zeroed = sem("slots_zeroed")
        s.summed = [sem("rows_stored0"), sem("rows_stored1")]
        s.shared_w = sb("shared_w", [P, 2 * F])
        s.valid, s.masked = sb("valid", [P, TILES, SEQ]), sb("masked", [P, TILES, SEQ])
        s.keymask, s.keymask_in = sb("keymask", [P, TILES, SEQ], i32), sem("keymask_in")
        s.shared_in, s.bias_in = sem("shared_in"), sem("bias_in")
        wait_apart.carrier = sem("carrier")
        linear_attention(nc, io, s)
        with ExitStack() as local:
            w = Weights(nc, io, s, 0, local)
            route(nc, io, s, w)
            experts(nc, io, s, 0, w)
        with ExitStack() as local:
            w = Weights(nc, io, s, 1, local)
            softmax_attention(nc, io, s, w)
            experts(nc, io, s, 1, w)


def wait_apart(eng, sem, value):
    eng.wait_ge(sem, value)
    eng.sem_inc(wait_apart.carrier, 1)


def row_stats(nc, o, src, st, mv, n, done):
    for j in range(n):
        o.mark(nc.vector.bn_stats(st[:, j, :], src(j)))
    o.wait_apart()
    for j in range(n):
        last = nc.vector.bn_aggr(mv[:, j, :], st[:, j, :])
    last.then_inc(done, 1)


def linear_attention(nc, io, s):
    HD, PARTS = 2, 4
    TG = HD * PARTS
    N = TILES // TG
    sem = s.sem
    with ExitStack() as local:
        def lb(name, shape, dt=f32):
            return local.enter_context(nc.sbuf_tensor("a_" + name, shape, dt))

        def each(name, shape, dt=f32):
            return [lb(f"{name}{h}", shape, dt) for h in range(PARTS)]
        ctxT, xn, xnT = each("ctxT", [D, HD * P]), each("xn", [P, HD, D]), each("xnT", [D, HD * P])
        st, mv = each("st", [P, 3 * HD, 6]), each("mv", [P, 3 * HD, 2])
        rs, nm, rm = each("rs", [P, 3 * HD]), each("nm", [P, HD]), each("rm", [P, HD])
        keys, qn, qT = each("keys", [P, HD, D]), each("qn", [P, HD, D]), each("qT", [D, HD * P])
        W = D + 2
        vv = each("vv", [P, HD, 2, W])
        ks = each("ks", [D, HD, 2, 2])
        kb = each("kb", [D, HD, 2, D])
        nv = each("nv", [P, HD])
        kvb = each("kvb", [D, HD, 2, D])
        qk = each("qk", [D, HD * P])
        den, attT, attS, attX = (each(n, [D, w * HD * P]) for n, w in (("den", 1), ("attT", 1), ("attS", 1), ("attX", 4)))
        o1, xb = each("o1", [P, HD, D]), each("xb", [P, HD, D])
        gB, bB = lb("gB", [P, D]), lb("bB", [P, D])
        heads_g, heads_b = lb("heads_g", [D, D]), lb("heads_b", [D, D])
        em = lb("em", [P, TILES, 2])
        psX, psY = s.ps[0::2], s.ps[1::2]

        names = ("x_in gates_ok gB_ok xn_ok xnT_ps xnT_ok kv_ps q_ps nm0_ok nm_ok qn_ok v_ok kv_ok const_ok "
                 "qT_ps qTr_ok qT_ok m_ps ks_ok kb_ok qk_ok kvb_ok n_ps "
                 "den_ok att_ok swapA_ok swapD_ok attX_ok o_ps xb_ok x1n_ok x1T_ps xT_ok x1T_ok lg_ps lg_ok low_ok agg_ok rs_ok "
                 "dve_order pool_order empty_ok").split()
        m = {k: sem("a_" + k) for k in names}
        loaded = [sem(f"a_loaded{k}") for k in range(3)]
        ctx_in = [sem(f"a_ctx_in{h}") for h in range(PARTS)]
        x_rows = io["x"].rearrange("(t p) d -> p t d", p=P)
        ctx_at = lambda i, h: bass.ds(P * (TG * i + HD * h), P * HD)
        with nc.Block() as block:
            @block.sync
            def _(sp):
                sp.dma_start(s.X[:, 0:TG, :], x_rows[:, 0:TG, :]).then_inc(m["x_in"], 16)
                sp.dma_start(s.shape_t[:], io["shape"]).then_inc(loaded[0], 16)
                for h in range(PARTS):
                    sp.dma_start(ctxT[h][:], io["ctxT"][:, ctx_at(0, h)]).then_inc(ctx_in[h], 16)
                with sp.Fori(1, N) as i:
                    sp.wait_ge(m["x_in"], 16 * i)
                    sp.dma_start(s.X[:, bass.ds(TG * i, TG), :], x_rows[:, bass.ds(TG * i, TG), :]).then_inc(m["x_in"], 16)
                    for h in range(PARTS):
                        sp.wait_ge(m["kv_ps"], PARTS * (i - 1) + h + 1)
                        sp.dma_start(ctxT[h][:], io["ctxT"][:, ctx_at(i, h)]).then_inc(ctx_in[h], 16)
                sp.dma_start(s.shared_w[:], io["experts0"][E, :, :]).then_inc(s.shared_in, 16)
                sp.dma_start(s.bias[:], io["bias0"]).then_inc(s.bias_in, 16)
                sp.dma_start(s.keymask[:].rearrange("p t k -> p (t k)"), io["keymask"]).then_inc(s.keymask_in, 16)
                sp.wait_ge(m["empty_ok"], 1)
                for k in range(2):
                    for e in range(E):
                        sp.dma_start(io[f"slots{k}"].rearrange("(e s p) d -> e p s d", s=ST, p=P)[e], s.empty[:]).then_inc(s.zeroed, 16)
                    sp.dma_start(io[f"sums{k}"][TOKENS:TOKENS + CAP, :].rearrange("(s p) d -> p s d", p=P), s.empty[:, :, 0:D]).then_inc(s.zeroed, 16)
                sp.wait_ge(s.zeroed, 16 * 2 * (E + 1))

            @block.scalar
            def _(act):
                act.dma_start(s.vec_t[:], io["vec"]).then_inc(loaded[1], 16)
                act.dma_start(s.w_t[:], io["w"]).then_inc(loaded[2], 16)
                act.wait_ge(loaded[1], 16)
                nc.scalar.activation(s.tg[:], s.v("gates"), ACT.Tanh).then_inc(m["gates_ok"], 1)
                nc.scalar.activation(s.warm[:, 0:1], s.v("eps5"), ACT.Sqrt)
                with act.Fori(0, N) as i:
                    A = nc.scalar.activation
                    at = lambda h: PARTS * i + h + 1

                    def deviation(h, stage, n, eps):
                        act.wait_ge(m["agg_ok"], 4 * PARTS * i + PARTS * stage + h + 1)
                        A(rs[h][:, 0:n], mv[h][:, 0:n, 1], ACT.Sqrt, bias=s.v(eps)).then_inc(m["rs_ok"], 1)

                    for h in range(PARTS):
                        deviation(h, 0, HD, "eps5")
                    for h in range(PARTS):
                        wait_apart(act, m["nm0_ok"], at(h))
                        for j in range(HD):
                            last = A(xn[h][:, j, :], s.X[:, bass.ds(TG * i + HD * h + j, 1), :].rearrange("p a d -> p (a d)"), ACT.Identity,
                                     bias=nm[h][:, j:j + 1], scale=rs[h][:, j:j + 1])
                        last.then_inc(m["xn_ok"], 1)
                    for h in range(PARTS):
                        act.wait_ge(m["xnT_ps"], at(h))
                        A(xnT[h][:], psX[h][:, 0:256], ACT.Copy).then_inc(m["xnT_ok"], 1)
                    for h in range(PARTS):
                        deviation(h, 1, 3 * HD, "eps6")
                    for h in range(PARTS):
                        act.wait_ge(m["nm_ok"], at(h))
                        for j in range(HD):
                            for b in range(2):
                                rows = slice(SEQ * b, SEQ * b + SEQ)
                                last = A(vv[h][rows, j, b, 0:D], psY[h][rows, 256 * j + 128:256 * j + 256], ACT.Identity,
                                         bias=nv[h][rows, j:j + 1], scale=rm[h][rows, j:j + 1])
                        last.then_inc(m["v_ok"], 1)
                        for j in range(HD):
                            last = A(qn[h][:, j, :], psX[h][:, 256 + 128 * j:384 + 128 * j], ACT.Identity,
                                     bias=nm[h][:, j:j + 1], scale=rs[h][:, 4 + j:5 + j])
                        last.then_inc(m["qn_ok"], 1)
                    for h in range(PARTS):
                        act.wait_ge(m["qT_ps"], at(h))
                        A(qT[h][:], psX[h][:, 0:256], ACT.Relu, bias=s.v("beta_t"), scale=s.v("gamma_t")).then_inc(m["qTr_ok"], 1)
                    for h in range(PARTS):
                        act.wait_ge(m["qTr_ok"], at(h))
                        A(qT[h][:], qT[h][:], ACT.Identity, bias=s.v("eps6")).then_inc(m["qT_ok"], 1)
                    for h in range(PARTS):
                        act.wait_ge(m["ks_ok"], at(h))
                        act.wait_ge(m["qT_ok"], at(h))
                        for j in range(HD):
                            for b in range(2):
                                tok = slice(P * j + SEQ * b, P * j + SEQ * b + SEQ)
                                last = A(qk[h][:, tok], qT[h][:, tok], ACT.Copy, scale=ks[h][:, j, b, 0:1])
                        last.then_inc(m["qk_ok"], 1)

                    def denominators(h):
                        act.wait_ge(m["n_ps"], at(h))
                        A(den[h][:], psX[h][:, 256:512], ACT.Identity, bias=s.v("eps6")).then_inc(m["den_ok"], 1)

                    denominators(0)
                    for h in range(PARTS):
                        if h + 1 < PARTS:
                            denominators(h + 1)
                        act.wait_ge(m["att_ok"], at(h))
                        for q, a in SWAPS[0]:
                            last = A(*swap(attT[h], attS[h], q, a), ACT.Copy)
                        last.then_inc(m["swapA_ok"], 1)
                    for h in range(PARTS):
                        deviation(h, 2, HD, "eps6")
                    for h in range(PARTS):
                        deviation(h, 3, HD, "eps5")

                    def logits(h):
                        act.wait_ge(m["lg_ps"], at(h))
                        A(s.LG[:, bass.ds(TG * i + HD * h, HD), :], psY[h][:, 256:256 + HD * E].rearrange("p (t e) -> p t e", e=E),
                          ACT.Copy).then_inc(m["lg_ok"], 1)

                    for h in range(PARTS):
                        act.wait_ge(m["x1n_ok"], at(h))
                        A(s.XN[:, bass.ds(TG * i + HD * h, HD), 0:D], xn[h][:], ACT.Copy)
                        act.wait_ge(m["x1T_ps"], at(h))
                        A(xnT[h][:], psX[h][:, 0:256], ACT.Copy).then_inc(m["xT_ok"], 1)
                        A(s.XTH[:, ctx_at(i, h)], psX[h][:, 0:256], ACT.Copy).then_inc(m["x1T_ok"], 1)
                        if h:
                            logits(h - 1)
                    logits(PARTS - 1)

            @block.gpsimd
            def _(pool):
                G = nc.gpsimd
                o = Order(pool, m["pool_order"])
                for h in range(PARTS):
                    o.mark(G.memset(vv[h][:], 0.0))
                o.mark(G.memset(s.empty[:], 0.0))
                o.wait()
                pool.wait_ge(loaded[0], 16)
                G.tensor_copy(s.empty[:, :, D].bitcast(u32), s.c("spare")).then_inc(m["empty_ok"], 1)
                pool.wait_ge(loaded[1], 16)
                o.mark(G.tensor_tensor(em[:, :, 0], s.v("em"), s.c("ones")[:, 0:TILES], ALU.mult))
                o.mark(G.tensor_tensor(em[:, :, 1], s.v("em"), s.v("em"), ALU.mult))
                o.mark(G.tensor_tensor(heads_g[:], s.c("heads"), s.v("gamma"), ALU.mult))
                G.tensor_tensor(heads_b[:], s.c("heads"), s.v("beta"), ALU.mult).then_inc(m["const_ok"], 1)
                pool.wait_ge(m["gates_ok"], 1)
                G.tensor_scalar(gB[:], s.v("gamma"), s.tg[:, 0:1], None, ALU.mult)
                G.tensor_scalar(bB[:], s.v("beta"), s.tg[:, 0:1], None, ALU.mult).then_inc(m["gB_ok"], 1)
                pool.wait_ge(m["gB_ok"], 1)
                with pool.Fori(0, N) as i:
                    at = lambda h: PARTS * i + h + 1
                    for h in range(PARTS):
                        wait_apart(pool, m["x_in"], 16 * i + 16)
                        G.tensor_tensor(xb[h][:], s.X[:, bass.ds(TG * i + HD * h, HD), :],
                                        bB[:].unsqueeze(1).broadcast_to([P, HD, D]), ALU.add).then_inc(m["xb_ok"], 1)
                    for h in range(PARTS):
                        pool.wait_ge(m["ks_ok"], at(h))
                        sums = lambda c: ks[h][:].rearrange("d j b c -> d (j b) c")[:, :, c].unsqueeze(2).broadcast_to([D, 4, D])
                        blocks = lambda t: t.unsqueeze(1).broadcast_to([D, 4, D])
                        G.tensor_tensor(kb[h][:].rearrange("d j b e -> d (j b) e"), blocks(heads_b[:]), sums(1), ALU.mult).then_inc(m["kb_ok"], 1)
                    for h in range(PARTS):
                        pool.wait_ge(m["swapA_ok"], at(h))
                        pool.wait_ge(m["swapD_ok"], at(h))
                        G.tensor_tensor(attX[h][:].rearrange("p (m h n) -> p m h n", h=4, n=4),
                                        attS[h][:].rearrange("p (m n) -> p m n", n=4).unsqueeze(2).broadcast_to([P, 64, 4, 4]),
                                        s.c("own").unsqueeze(1).unsqueeze(3).broadcast_to([P, 64, 4, 4]), ALU.mult).then_inc(m["attX_ok"], 1)
                    for h in range(PARTS):
                        wait_apart(pool, m["x1T_ok"], at(h))
                        G.tensor_tensor(s.XTL[:, ctx_at(i, h)], xnT[h][:], s.XTH[:, ctx_at(i, h)].bitcast(f32), ALU.subtract).then_inc(m["low_ok"], 1)

            @block.vector
            def _(dve):
                V = nc.vector
                DO = 100
                with dve.Fori(0, N) as i:
                    o = Order(dve, m["dve_order"], DO * i)
                    at = lambda h: PARTS * i + h + 1
                    wait_apart(dve, m["x_in"], 16 * i + 16)
                    tile = lambda h, j: s.X[:, bass.ds(TG * i + HD * h + j, 1), :].rearrange("p a d -> p (a d)")

                    def inverse(h, stage, n):
                        dve.wait_ge(m["rs_ok"], 4 * PARTS * i + PARTS * stage + h + 1)
                        return o.mark(V.reciprocal(rs[h][:, 0:n], rs[h][:, 0:n]))

                    for h in range(PARTS):
                        row_stats(nc, o, lambda j: tile(h, j), st[h], mv[h], HD, m["agg_ok"])
                    inverses = inverse(0, 0, HD)
                    for h in range(PARTS):
                        this = inverses
                        if h + 1 < PARTS:
                            inverses = inverse(h + 1, 0, HD)
                        o.wait(this)
                        V.scalar_tensor_tensor(nm[h][:], mv[h][:, 0:2, 0], -1.0, rs[h][:, 0:2], ALU.mult, ALU.mult).then_inc(m["nm0_ok"], 1)
                    for h in range(PARTS):
                        wait_apart(dve, m["kv_ps"], at(h))
                        for n in range(4):
                            V.bn_stats(st[h][:, n, :], psY[h][:, 128 * n:128 * n + 128])
                    for h in range(PARTS):
                        wait_apart(dve, m["q_ps"], at(h))
                        for n in range(4, 6):
                            o.mark(V.bn_stats(st[h][:, n, :], psX[h][:, 128 * n - 256:128 * n - 128]))
                        o.wait_apart()
                        for n in range(6):
                            last = V.bn_aggr(mv[h][:, n, :], st[h][:, n, :])
                        last.then_inc(m["agg_ok"], 1)
                    dve.wait_ge(m["const_ok"], 1)
                    inverses = inverse(0, 1, 3 * HD)
                    for h in range(PARTS):
                        tiles = bass.ds(TG * i + HD * h, HD)
                        for b in range(2):
                            rows = slice(SEQ * b, SEQ * b + SEQ)
                            V.tensor_copy(vv[h][rows, :, b, D:W], em[rows, tiles, :])
                        o.wait(inverses)
                        masked = o.mark(V.tensor_tensor(rm[h][:], rs[h][:, 1:4:2], em[:, tiles, 1], ALU.mult))
                        V.scalar_tensor_tensor(nm[h][:], mv[h][:, 4:6, 0], -1.0, rs[h][:, 4:6], ALU.mult, ALU.mult)
                        if h + 1 < PARTS:
                            inverses = inverse(h + 1, 1, 3 * HD)
                        o.wait(masked)
                        V.scalar_tensor_tensor(nv[h][:], mv[h][:, 1:4:2, 0], -1.0, rm[h][:], ALU.mult, ALU.mult).then_inc(m["nm_ok"], 1)

                    def centred_keys(h):
                        dve.wait_ge(m["v_ok"], at(h))
                        for j in range(HD):
                            n = o.mark(V.scalar_tensor_tensor(keys[h][:, j, :], psY[h][:, 256 * j:256 * j + 128], mv[h][:, 2 * j, 0:1],
                                                              s.v("gamma"), ALU.subtract, ALU.mult))
                        return n

                    def rectified(h, normed):
                        o.wait(normed)
                        V.tensor_scalar(keys[h][:], keys[h][:], 0.0, 1e-6, ALU.max, ALU.add).then_inc(m["kv_ok"], 1)

                    normed = {}
                    centred_at = centred_keys(0)
                    for h in range(PARTS):
                        this = centred_at
                        if h + 1 < PARTS:
                            centred_at = centred_keys(h + 1)
                        o.wait(this)
                        for j in range(HD):
                            normed[h] = o.mark(V.scalar_tensor_tensor(keys[h][:, j, :], keys[h][:, j, :], rs[h][:, 2 * j:2 * j + 1], s.v("beta"),
                                                                      ALU.mult, ALU.add))
                        if h >= 1:
                            rectified(h - 1, normed[h - 1])
                    rectified(PARTS - 1, normed[PARTS - 1])
                    for h in range(PARTS):
                        dve.wait_ge(m["m_ps"], at(h))
                        made = [bank[:, 0:2 * W].rearrange("d (b e) -> d b e", b=2) for bank in (psX[h], psY[h])]
                        for j in range(HD):
                            last = V.tensor_copy(ks[h][:, j], made[j][:, :, D:W])
                        last.then_inc(m["ks_ok"], 1)
                        for j in range(HD):
                            o.mark(V.tensor_tensor(kvb[h][:, j], made[j][:, :, 0:D],
                                                   heads_g[:].unsqueeze(1).broadcast_to([D, 2, D]), ALU.mult))
                    o.wait()
                    for h in range(PARTS):
                        dve.wait_ge(m["kb_ok"], at(h))
                        V.tensor_tensor(kvb[h][:].rearrange("d j b e -> d (j b) e"), kvb[h][:].rearrange("d j b e -> d (j b) e"),
                                        kb[h][:].rearrange("d j b e -> d (j b) e"), ALU.add).then_inc(m["kvb_ok"], 1)
                    for h in range(PARTS):
                        dve.wait_ge(m["den_ok"], at(h))
                        o.mark(V.reciprocal(den[h][:], den[h][:]))
                        o.wait()
                        V.tensor_tensor(attT[h][:], psX[h][:, 0:256], den[h][:], ALU.mult).then_inc(m["att_ok"], 1)
                        dve.wait_ge(m["att_ok"], at(h))
                        for q, a in SWAPS[1]:
                            last = V.tensor_copy(*swap(attT[h], attS[h], q, a))
                        last.then_inc(m["swapD_ok"], 1)
                    for h in range(PARTS):
                        dve.wait_ge(m["o_ps"], at(h))
                        o.mark(V.tensor_tensor(o1[h][:], psY[h][:, 0:256].rearrange("p (t d) -> p t d", d=D),
                                               s.v("dense_b").unsqueeze(1).broadcast_to([P, HD, D]), ALU.add))
                        o.wait_apart()
                        row_stats(nc, o, lambda j: o1[h][:, j, :], st[h], mv[h], HD, m["agg_ok"])
                    dve.wait_ge(m["gB_ok"], 1)
                    def centred(h):
                        for j in range(HD):
                            n = o.mark(V.scalar_tensor_tensor(o1[h][:, j, :], o1[h][:, j, :], mv[h][:, j, 0:1], gB[:], ALU.subtract, ALU.mult))
                        return n

                    added, counted = {}, {}
                    centred(0)
                    for h in range(PARTS + 1):
                        if h < PARTS:
                            scaled = inverse(h, 2, HD)
                        if h + 1 < PARTS:
                            centred(h + 1)
                        if h >= 1:
                            o.wait_apart(added[h - 1])
                            for j in range(HD):
                                counted[h - 1] = o.mark(V.bn_stats(st[h - 1][:, j, :], tile(h - 1, j)))
                        if h < PARTS:
                            dve.wait_ge(m["xb_ok"], at(h))
                            o.wait(scaled)
                            for j in range(HD):
                                added[h] = o.mark(V.scalar_tensor_tensor(tile(h, j), o1[h][:, j, :], rs[h][:, j:j + 1], xb[h][:, j, :],
                                                                         ALU.mult, ALU.add))
                        if h >= 1:
                            o.wait_apart(counted[h - 1])
                            for j in range(HD):
                                last = V.bn_aggr(mv[h - 1][:, j, :], st[h - 1][:, j, :])
                            last.then_inc(m["agg_ok"], 1)
                    inverses = inverse(0, 3, HD)
                    for h in range(PARTS):
                        this = inverses
                        if h + 1 < PARTS:
                            inverses = inverse(h + 1, 3, HD)
                        o.wait(this)
                        for j in range(HD):
                            last = V.tensor_scalar(xn[h][:, j, :], tile(h, j), mv[h][:, j, 0:1], rs[h][:, j:j + 1], ALU.subtract, ALU.mult)
                        last.then_inc(m["x1n_ok"], 1)
                    assert o.n == DO, o.n

            @block.tensor
            def _(pe):
                for load in loaded:
                    pe.wait_ge(load, 16)
                mm = nc.tensor.matmul
                with pe.Fori(0, N) as i:
                    at = lambda h: PARTS * i + h + 1
                    for h in range(PARTS):
                        pe.wait_ge(ctx_in[h], 16 * i + 16)
                        for j in range(HD):
                            last = mm(psY[h][:, 256 * j:256 * j + 256], ctxT[h][:, 128 * j:128 * j + 128], s.w("wkv"), start=True, stop=True)
                        last.then_inc(m["kv_ps"], 1)
                    for h in range(PARTS):
                        pe.wait_ge(m["xn_ok"], at(h))
                        for j in range(HD):
                            last = nc.tensor.transpose(psX[h][:, 128 * j:128 * j + 128], xn[h][:, j, :], s.c("ident"))
                        last.then_inc(m["xnT_ps"], 1)
                    for h in range(PARTS):
                        pe.wait_ge(m["xnT_ok"], at(h))
                        for j in range(HD):
                            last = mm(psX[h][:, 256 + 128 * j:384 + 128 * j], xnT[h][:, 128 * j:128 * j + 128], s.w("wq"), start=True, stop=True)
                        last.then_inc(m["q_ps"], 1)
                    for h in range(PARTS):
                        pe.wait_ge(m["qn_ok"], at(h))
                        for j in range(HD):
                            last = nc.tensor.transpose(psX[h][:, 128 * j:128 * j + 128], qn[h][:, j, :], s.c("ident"))
                        last.then_inc(m["qT_ps"], 1)
                    for h in range(PARTS):
                        pe.wait_ge(m["kv_ok"], at(h))
                        pe.wait_ge(m["qTr_ok"], at(h))
                        for j, bank in enumerate((psX[h], psY[h])):
                            last = mm(bank[:, 0:2 * W], keys[h][:, j, :], vv[h][:, j].rearrange("p b e -> p (b e)"), start=True, stop=True)
                        last.then_inc(m["m_ps"], 1)
                    for h in range(PARTS):
                        pe.wait_ge(m["kvb_ok"], at(h))
                        pe.wait_ge(m["qT_ok"], at(h))
                        for j in range(HD):
                            for b in range(2):
                                to = 128 * j + SEQ * b
                                mm(psX[h][:, to:to + SEQ], kvb[h][:, j, b, :], qT[h][:, to:to + SEQ], start=True, stop=True)
                        pe.wait_ge(m["qk_ok"], at(h))
                        mm(psX[h][:, 256:512], s.c("heads"), qk[h][:], start=True, stop=True).then_inc(m["n_ps"], 1)
                    for h in range(PARTS):
                        pe.wait_ge(m["attX_ok"], at(h))
                        for j in range(HD):
                            for b in range(4):
                                last = mm(psY[h][:, 128 * j:128 * j + 128], attX[h][:, 256 * b + 128 * j:256 * b + 128 * j + 128],
                                          s.w("dense")[:, 128 * b:128 * b + 128], start=b == 0, stop=b == 3)
                        last.then_inc(m["o_ps"], 1)

                    def logits(h):
                        pe.wait_ge(m["xT_ok"], at(h))
                        for j in range(HD):
                            last = mm(psY[h][:, 256 + E * j:256 + E * j + E], xnT[h][:, 128 * j:128 * j + 128], s.w("router0"), start=True, stop=True)
                        last.then_inc(m["lg_ps"], 1)

                    for h in range(PARTS):
                        pe.wait_ge(m["x1n_ok"], at(h))
                        for j in range(HD):
                            last = nc.tensor.transpose(psX[h][:, 128 * j:128 * j + 128], xn[h][:, j, :], s.c("ident"))
                        last.then_inc(m["x1T_ps"], 1)
                        if h:
                            logits(h - 1)
                    logits(PARTS - 1)
                    pe.wait_ge(m["lg_ok"], at(PARTS - 1))
                    pe.wait_ge(m["low_ok"], at(PARTS - 1))


SWAPS = [[(q, a) for q in range(4) for a in range(4) if (q < 3) == (k == 0)] for k in range(2)]


def swap(source, target, q, a):
    out = target[32 * a:32 * a + 32, :].rearrange("p (b j q n) -> p q b j n", b=4, j=4, q=4)[:, q]
    return out, source[32 * q:32 * q + 32, :].rearrange("p (j n a b) -> p a b j n", j=4, n=4, a=4)[:, a]


class Weights:

    def __init__(self, nc, io, s, layer, local):
        def two(name, shape, dt=f32):
            return [local.enter_context(nc.sbuf_tensor(f"w{layer}_{name}{q}", shape, dt)) for q in range(2)]
        self.nc, self.N1 = nc, F * (1 + layer)
        self.raw, self.w2 = two("raw", [P, self.N1]), two("w2", [P, FC * D])
        self.wh, self.wl = two("wh", [P, self.N1], f32r), two("wl", [P, self.N1], f32r)
        self.rows = two("rows", [P, ST, ROW])
        self.w_in, self.w2_in, self.rows_in = ([s.sem(f"w{layer}_{n}{q}") for q in range(2)] for n in ("w_in", "w2_in", "rows_in"))
        self.wh_ok, self.wl_ok = s.sem(f"w{layer}_wh_ok"), s.sem(f"w{layer}_wl_ok")
        self.dram = io[f"experts{layer}"]
        self.slot_rows = io[f"slots{layer}"].rearrange("(e s p) d -> e p s d", s=ST, p=P)

    def of(self, e):
        return self.dram[bass.ds(e, 1)].rearrange("e p n -> (e p) n")

    def load_rows(self, sp, e, q):
        sp.dma_start(self.rows[q][:], self.slot_rows[bass.ds(e, 1)].rearrange("e p s d -> (e p) s d")).then_inc(self.rows_in[q], 16)

    def load_first(self, sp, e, q):
        sp.dma_start(self.raw[q][:], self.of(e)[:, 0:self.N1]).then_inc(self.w_in[q], 16)

    def load_second(self, sp, e, q):
        sp.dma_start(self.w2[q][:], self.of(e)[:, self.N1:self.N1 + FC * D]).then_inc(self.w2_in[q], 16)

    def high(self, act, q, turn):
        act.wait_ge(self.w_in[q], 16 * turn)
        self.nc.scalar.activation(self.wh[q][:], self.raw[q][:], ACT.Copy).then_inc(self.wh_ok, 1)

    def low(self, dve, e, q):
        dve.wait_ge(self.wh_ok, e + 1)
        self.nc.vector.tensor_tensor(self.wl[q][:], self.raw[q][:], self.wh[q][:].bitcast(f32), ALU.subtract).then_inc(self.wl_ok, 1)


def route(nc, io, s, w):
    sem = s.sem
    pre = "g_"
    with ExitStack() as local:
        def lb(name, shape, dt=f32):
            return local.enter_context(nc.sbuf_tensor(pre + name, shape, dt))
        BLOCKS = TOKENS // 512
        top, total, inv, rank = (lb(n, [P, TILES]) for n in ("top", "total", "inv", "rank"))
        ex, gate, cand = (lb(n, [P, TILES, E]) for n in ("ex", "gate", "cand"))
        mask, pos, keep, val = (lb(n, [P, 2, TILES, E]) for n in ("mask", "pos", "keep", "val"))
        per_tile, upto = lb("per_tile", [P, 2, E, TILES]), lb("upto", [P, 2, E, TILES])
        base2 = lb("base2", [P, E])
        slot = [lb(f"slot{k}", [P, TILES], u32) for k in range(2)]
        kept, slotf, weight = (lb(n, [P, 2, TILES]) for n in ("kept", "slotf", "weight"))
        psR = s.ps[0]
        sh_ok, ex_ok, mask_ok, r_ps, slots_ok = (sem(pre + n) for n in ("sh_ok", "ex_ok", "mask_ok", "r_ps", "slots_ok"))
        order, scattered = sem(pre + "order"), sem(pre + "scattered")
        wh, wl = lb("wh", [P, 2 * F], f32r), lb("wl", [P, 2 * F], f32r)
        hf, hh, hl = lb("hf", [P, FC, 512]), lb("hh", [P, FC, 512], f32r), lb("hl", [P, FC, 512], f32r)
        c, cb2 = lb("c", [P, 1]), lb("cb2", [P, D])
        hb, psY = s.ps[1:5], s.ps[5:7]
        wh_ok, wl_ok = (sem(pre + n) for n in ("wh_ok", "wl_ok"))
        h_ps, hf_ok, hh_ok, hl_ok, y_ps, y_ok = (sem(pre + n) for n in ("h_ps", "hf_ok", "hh_ok", "hl_ok", "y_ps", "y_ok"))
        with nc.Block() as block:
            @block.sync
            def _(sp):
                for q in range(2):
                    w.load_first(sp, q, q)
                    w.load_second(sp, q, q)
                with sp.Fori(0, BLOCKS) as i:
                    sp.wait_ge(y_ok, i + 1)
                    sp.dma_start(io["sums0"][0:TOKENS, :].rearrange("(t p) d -> p t d", p=P)[:, bass.ds(4 * i, 4), :],
                                 s.X[:, bass.ds(4 * i, 4), :]).then_inc(s.summed[0], 16)

            @block.scalar
            def _(act):
                A = nc.scalar.activation
                A(s.warm[:, 0:1], s.c("ones")[:, 0:1], ACT.Exp)
                act.wait_ge(sh_ok, 1)
                A(ex[:], ex[:], ACT.Exp).then_inc(ex_ok, 1)
                act.wait_ge(s.shared_in, 16)
                A(wh[:], s.shared_w[:], ACT.Copy).then_inc(wh_ok, 1)
                w.high(act, 0, 1)
                A(s.warm[:, 1:2], s.c("ones")[:, 0:1], ACT.Silu)
                act.wait_ge(s.bias_in, 16)
                with act.Fori(0, BLOCKS) as i:
                    for k in range(FC):
                        act.wait_ge(h_ps, FC * i + k + 1)
                        A(hf[:, k, :], hb[k][:], ACT.Silu, bias=s.bias[:, FC * E + k:FC * E + k + 1]).then_inc(hf_ok, 1)
                        act.wait_ge(hf_ok, FC * i + k + 1)
                        A(hh[:, k, :], hf[:, k, :], ACT.Copy).then_inc(hh_ok, 1)
                act.wait_ge(scattered, 16 * 2 * TILES)
                w.load_rows(act, 0, 0)

            @block.gpsimd
            def _(pool):
                pool.wait_ge(slots_ok, 1)
                for t in range(TILES):
                    for k in range(2):
                        pool.indirect_dma_start(out=io["slots0"], out_offset=bass.IndirectOffsetOnAxis(ap=slot[k][:, t:t + 1], axis=0),
                                                in_=s.XN[:, t, :], in_offset=None, bounds_check=SLOTS - 1, oob_is_err=False).then_inc(scattered, 16)
                pool.wait_ge(scattered, 16 * 2 * TILES)

            @block.vector
            def _(dve):
                o = Order(dve, order)

                def step(ins):
                    o.mark(ins)
                    o.wait()

                def b3(t):
                    return t.unsqueeze(2).broadcast_to([P, TILES, E])

                def rows(c):
                    return s.c(c).unsqueeze(1).broadcast_to([P, TILES, E])

                V = nc.vector
                logits = s.LG[:]
                step(V.tensor_reduce(top[:], logits, AX.X, ALU.max))
                V.tensor_tensor(ex[:], logits, b3(top[:]), ALU.subtract).then_inc(sh_ok, 1)
                o.mark(V.tensor_copy(s.XN[:, :, D].bitcast(u32), s.c("token")))
                step(V.tensor_scalar(c[:], s.tg[:, 2:3], 0.1, None, ALU.mult))
                dve.wait_ge(s.bias_in, 16)
                step(V.tensor_scalar(cb2[:], s.bias[:, FC * (E + 1) + D * E:FC * (E + 1) + D * (E + 1)], c[:, 0:1], None, ALU.mult))
                dve.wait_ge(ex_ok, 1)
                step(V.tensor_reduce(total[:], ex[:], AX.X, ALU.add))
                step(V.reciprocal(inv[:], total[:]))
                step(V.tensor_tensor(gate[:], ex[:], b3(inv[:]), ALU.mult))
                for k in range(2):
                    left = gate if k == 0 else ex
                    if k == 1:
                        step(V.tensor_tensor(cand[:], gate[:], mask[:, 0], ALU.mult))
                        step(V.tensor_tensor(ex[:], gate[:], cand[:], ALU.subtract))
                    step(V.tensor_reduce(top[:], left[:], AX.X, ALU.max))
                    step(V.tensor_tensor(cand[:], left[:], b3(top[:]), ALU.is_equal))
                    step(V.tensor_tensor(cand[:], cand[:], rows("rev"), ALU.mult))
                    step(V.tensor_reduce(rank[:], cand[:], AX.X, ALU.max))
                    ins = V.tensor_tensor(mask[:, k], rows("rev"), b3(rank[:]), ALU.is_equal)
                    ins.then_inc(mask_ok, 1)
                    if k == 0:
                        dve.wait_ge(mask_ok, 1)
                dve.wait_ge(wh_ok, 1)
                V.tensor_tensor(wl[:], s.shared_w[:], wh[:].bitcast(f32), ALU.subtract).then_inc(wl_ok, 1)
                dve.wait_ge(r_ps, 1)
                step(V.tensor_copy(per_tile[:].rearrange("p k e t -> p k t e"), psR[:, 256:512].rearrange("p (k t e) -> p k t e", k=2, e=E)))
                flat = "p k e t -> p (k e t)"
                step(V.tensor_tensor_scan(upto[:].rearrange(flat), s.c("restart"), per_tile[:].rearrange(flat), 0.0, ALU.mult, ALU.add))
                o.mark(V.tensor_scalar(base2[:], upto[:, 0, :, TILES - 1], float(CAP), None, ALU.min))
                step(V.tensor_tensor(per_tile[:].rearrange(flat), upto[:].rearrange(flat), per_tile[:].rearrange(flat), ALU.subtract))
                step(V.tensor_tensor(pos[:], psR[:, 0:256].rearrange("p (k t e) -> p k t e", k=2, e=E),
                                     per_tile[:].rearrange("p k e t -> p k t e"), ALU.add))
                step(V.tensor_tensor(pos[:, 1], pos[:, 1], base2[:].unsqueeze(1).broadcast_to([P, TILES, E]), ALU.add))
                all_ = "p k t e -> p (k t) e"
                one = "p k t e -> p (k t e)"
                step(V.scalar_tensor_tensor(keep[:].rearrange(one), pos[:].rearrange(one), float(CAP), mask[:].rearrange(one), ALU.is_lt, ALU.mult))
                o.mark(V.tensor_reduce(kept[:].rearrange("p k t -> p (k t)"), keep[:].rearrange(all_), AX.X, ALU.add))
                step(V.tensor_tensor(val[:].rearrange(all_), pos[:].rearrange(all_), s.c("expert_base").unsqueeze(1).broadcast_to([P, 2 * TILES, E]), ALU.add))
                step(V.tensor_tensor(val[:].rearrange(one), val[:].rearrange(one), keep[:].rearrange(one), ALU.mult))
                step(V.tensor_reduce(slotf[:].rearrange("p k t -> p (k t)"), val[:].rearrange(all_), AX.X, ALU.add))
                step(V.scalar_tensor_tensor(slotf[:].rearrange("p k t -> p (k t)"), kept[:].rearrange("p k t -> p (k t)"), -2.0 * SLOTS,
                                            slotf[:].rearrange("p k t -> p (k t)"), ALU.mult, ALU.add))
                for k in range(2):
                    o.mark(V.tensor_scalar(slot[k][:], slotf[:, k], 2.0 * SLOTS, None, ALU.add))
                step(V.tensor_tensor(val[:], keep[:], gate[:].unsqueeze(1).broadcast_to([P, 2, TILES, E]), ALU.mult))
                step(V.tensor_reduce(weight[:].rearrange("p k t -> p (k t)"), val[:].rearrange(all_), AX.X, ALU.add))
                step(V.tensor_tensor(total[:], weight[:, 0], weight[:, 1], ALU.add))
                step(V.tensor_scalar(total[:], total[:], float(np.finfo(np.float32).eps), None, ALU.max))
                step(V.reciprocal(inv[:], total[:]))
                step(V.tensor_scalar(inv[:], inv[:], s.tg[:, 2:3], None, ALU.mult))
                for k in range(2):
                    V.tensor_tensor(s.XN[:, :, D + 1 + k], weight[:, k], inv[:], ALU.mult)
                V.tensor_copy(s.XN[:, :, D + 3], slot[0][:]).then_inc(slots_ok, 1)
                DO, done = 2, o.n
                with dve.Fori(0, BLOCKS // 2) as g:
                    p = Order(dve, order, DO * g + done)
                    for r in range(2):
                        i = 2 * g + r
                        for k in range(FC):
                            dve.wait_ge(hh_ok, FC * i + k + 1)
                            V.tensor_tensor(hl[:, k, :], hf[:, k, :], hh[:, k, :].bitcast(f32), ALU.subtract).then_inc(hl_ok, 1)
                        dve.wait_ge(y_ps, i + 1)
                        at = bass.ds(4 * i, 4)
                        p.mark(V.scalar_tensor_tensor(s.X[:, at, :].rearrange("p t d -> p (t d)"), psY[r][:], c[:, 0:1],
                                                      s.X[:, at, :].rearrange("p t d -> p (t d)"), ALU.mult, ALU.add))
                        p.wait()
                        V.tensor_tensor(s.X[:, at, :], s.X[:, at, :], cb2[:].unsqueeze(1).broadcast_to([P, 4, D]), ALU.add).then_inc(y_ok, 1)
                    assert p.n == DO
                w.low(dve, 0, 0)

            @block.tensor
            def _(pe):
                for k in range(2):
                    pe.wait_ge(mask_ok, k + 1)
                    flat = mask[:, k].rearrange("p t e -> p (t e)")
                    nc.tensor.matmul(psR[:, P * k:P * k + P], s.c("before"), flat, start=True, stop=True)
                    last = nc.tensor.matmul(psR[:, 2 * P + P * k:3 * P + P * k], s.c("ones"), flat, start=True, stop=True)
                last.then_inc(r_ps, 1)
                pe.wait_ge(wl_ok, 1)
                with pe.Fori(0, BLOCKS // 2) as g:
                    for r in range(2):
                        i = 2 * g + r
                        at = bass.ds(512 * i, 512)
                        for k in range(FC):
                            f = slice(P * k, P * k + P)
                            nc.tensor.matmul(hb[k][:], wh[:, f], s.XTH[:, at], start=True, stop=False)
                            nc.tensor.matmul(hb[k][:], wh[:, f], s.XTL[:, at], start=False, stop=False)
                            nc.tensor.matmul(hb[k][:], wl[:, f], s.XTH[:, at], start=False, stop=True).then_inc(h_ps, 1)
                        for k in range(FC):
                            pe.wait_ge(hl_ok, FC * i + k + 1)
                            f = slice(F + D * k, F + D * k + D)
                            for j in range(4):
                                tok, out = slice(P * j, P * j + P), psY[r][:, P * j:P * j + P]
                                nc.tensor.matmul(out, hh[:, k, tok], wh[:, f], start=k == 0 and j == 0, stop=False, skip_group_check=True)
                                nc.tensor.matmul(out, hh[:, k, tok], wl[:, f], start=False, stop=False, skip_group_check=True)
                                last = nc.tensor.matmul(out, hl[:, k, tok], wh[:, f], start=False, stop=k == FC - 1, skip_group_check=True)
                        last.then_inc(y_ps, 1)


def experts(nc, io, s, layer, w):
    sem = s.sem
    pre = f"e{layer}_"
    U = 2 * FC
    ADDS = 16 * ST
    with ExitStack() as local:
        def lb(name, shape, dt=f32):
            return local.enter_context(nc.sbuf_tensor(pre + name, shape, dt))

        def two(name, shape, dt=f32):
            return [lb(f"{name}{q}", shape, dt) for q in range(2)]
        wh, wl, w2, rows, w2_in, rows_in, wh_ok, wl_ok = w.wh, w.wl, w.w2, w.rows, w.w2_in, w.rows_in, w.wh_ok, w.wl_ok
        y, token = two("y", [P, ST, D]), two("token", [P, ST], u32)
        xh, xl = lb("xh", [D, CAP], f32r), lb("xl", [D, CAP], f32r)
        sg = [lb(f"sg{r}", [P, HALF]) for r in range(4)]
        hs = lb("hs", [P, FC, CAP])
        first, part, rest = lb("first", [P, ST]), lb("part", [P, ST]), lb("rest", [P, ST])
        hb, psX, psY = s.ps[0:4], s.ps[4:6], s.ps[6:8]
        added = [sem(f"{pre}added{q}") for q in range(2)]
        x_ps, xh_ok, xl_ok = (sem(pre + n) for n in ("x_ps", "xh_ok", "xl_ok"))
        h_ps, sg_ok, hs_ok, y_ps, y_ok, order, settled = (sem(pre + n) for n in ("h_ps", "sg_ok", "hs_ok", "y_ps", "y_ok", "order", "settled"))
        sums = io[f"sums{layer}"]

        def each(eng, body):
            with eng.Fori(0, E // 2 - 1) as i:
                body(i, 0, True, True)
                body(i, 1, True, True)
            body(E // 2 - 1, 0, True, False)
            body(E // 2 - 1, 1, False, False)

        def unit(n):
            return n // 2, slice(HALF * (n % 2), HALF * (n % 2) + HALF)

        with nc.Block() as block:
            @block.sync
            def _(sp):
                def body(i, q, more, two_more):
                    e = 2 * i + q
                    if more:
                        sp.wait_ge(y_ok, e + 1)
                        w.load_rows(sp, e + 1, 1 - q)
                    if two_more:
                        sp.wait_ge(wl_ok, e + 1)
                        w.load_first(sp, e + 2, q)
                        sp.wait_ge(y_ps, e + 1)
                        w.load_second(sp, e + 2, q)
                each(sp, body)

            @block.scalar
            def _(act):
                def high_rows(e):
                    act.wait_ge(x_ps, e + 1)
                    nc.scalar.activation(xh[:, 0:512], psX[0][:], ACT.Copy)
                    nc.scalar.activation(xh[:, 512:CAP], psX[1][:, 0:P], ACT.Copy).then_inc(xh_ok, 1)

                high_rows(0)

                def body(i, q, more, two_more):
                    e = 2 * i + q
                    for n in range(U):
                        k, half = unit(n)
                        if layer == 0:
                            wait_apart(act, h_ps, U * e + n + 1)
                            nc.scalar.activation(hs[:, k, half], hb[n % 4][:, 0:HALF], ACT.Silu,
                                                 bias=s.bias[:, bass.ds(FC * e + k, 1)]).then_inc(hs_ok, 1)
                        else:
                            act.wait_ge(h_ps, U * e + n + 1)
                            if n >= 4:
                                act.wait_ge(hs_ok, U * e + n - 3)
                            nc.scalar.activation(sg[n % 4][:], hb[2 * (n % 2)][:, 0:HALF], ACT.Silu).then_inc(sg_ok, 1)
                        if n == 3 and more:
                            w.high(act, 1 - q, i + 1 + q)
                    if more:
                        high_rows(e + 1)
                each(act, body)

            @block.gpsimd
            def _(pool):
                pool.sem_inc(settled, 2)
                pool.wait_ge(s.summed[layer], STORES[layer] * 16)

                def body(i, q, more, two_more):
                    wait_apart(pool, y_ok, 2 * i + q + 2)
                    for j in range(ST):
                        pool.indirect_dma_start(out=sums, out_offset=bass.IndirectOffsetOnAxis(ap=token[q][:, j:j + 1], axis=0),
                                                in_=y[q][:, j, :], in_offset=None, bounds_check=TOKENS + CAP - 1,
                                                oob_is_err=True, compute_op=ALU.add).then_inc(added[q], 16)
                    pool.wait_ge(added[q], ADDS * (i + 1))
                    pool.sem_inc(settled, 1)
                each(pool, body)

            @block.vector
            def _(dve):
                V = nc.vector

                def low_rows(e):
                    dve.wait_ge(xh_ok, e + 1)
                    V.tensor_tensor(xl[:, 0:512], psX[0][:], xh[:, 0:512].bitcast(f32), ALU.subtract)
                    V.tensor_tensor(xl[:, 512:CAP], psX[1][:, 0:P], xh[:, 512:CAP].bitcast(f32), ALU.subtract).then_inc(xl_ok, 1)

                dve.sem_inc(y_ok, 1)
                low_rows(0)
                p = Order(dve, order)
                if layer == 0:
                    dve.wait_ge(s.keymask_in, 16)
                    p.mark(V.tensor_copy(s.masked[:], s.keymask[:]))
                    p.wait()
                    p.mark(V.tensor_scalar(s.valid[:], s.masked[:], 0.0, None, ALU.not_equal))
                    p.wait()
                    p.mark(V.tensor_scalar(s.masked[:], s.valid[:], MASKED, -MASKED, ALU.mult, ALU.add))
                OPS = 5

                def body(i, q, more, two_more):
                    e = 2 * i + q
                    o = Order(dve, order, OPS * e + p.n)
                    for n in range(U):
                        if layer == 1:
                            k, half = unit(n)
                            dve.wait_ge(sg_ok, U * e + n + 1)
                            V.tensor_tensor(hs[:, k, half], sg[n % 4][:], hb[2 * (n % 2) + 1][:, 0:HALF], ALU.mult).then_inc(hs_ok, 1)
                        if n == 4 and more:
                            w.low(dve, e + 1, 1 - q)
                    if more:
                        low_rows(e + 1)
                    dve.wait_ge(rows_in[q], 16 * i + 16)
                    dve.wait_ge(settled, e + 1)
                    meta = lambda c: rows[q][:, :, D + c]
                    V.tensor_copy(token[q][:], meta(0).bitcast(u32))
                    o.mark(V.tensor_tensor(first[:], meta(3), s.c("slot")[:, bass.ds(ST * e, ST)], ALU.is_equal))
                    o.wait()
                    o.mark(V.tensor_tensor(part[:], meta(1), first[:], ALU.mult))
                    o.mark(V.tensor_scalar(rest[:], first[:], -1.0, 1.0, ALU.mult, ALU.add))
                    o.wait()
                    o.mark(V.tensor_tensor(rest[:], rest[:], meta(2), ALU.mult))
                    o.wait()
                    o.mark(V.tensor_tensor(part[:], part[:], rest[:], ALU.add))
                    o.wait()
                    assert o.n == OPS
                    dve.wait_ge(y_ps, e + 1)
                    for at, bank in ((slice(0, 4), psY[0][:]), (slice(4, ST), psY[1][:, 0:D])):
                        n = at.stop - at.start
                        weight = part[:, at].unsqueeze(2).broadcast_to([P, n, D])
                        made = bank.rearrange("p (s d) -> p s d", d=D)
                        if layer == 0:
                            b2 = s.bias[:, bass.ds(FC * (E + 1) + D * e, D)].unsqueeze(1).broadcast_to([P, n, D])
                            V.tensor_tensor(y[q][:, at, :], made, b2, ALU.add).then_inc(order_b, 1)
                            dve.wait_ge(order_b, 2 * e + (1 if n > 1 else 2))
                            last = V.tensor_tensor(y[q][:, at, :], y[q][:, at, :], weight, ALU.mult)
                        else:
                            last = V.tensor_tensor(y[q][:, at, :], made, weight, ALU.mult)
                    last.then_inc(y_ok, 1)
                order_b = sem(pre + "order_b")
                each(dve, body)

            @block.tensor
            def _(pe):
                def transpose_rows(e, q, turn):
                    pe.wait_ge(rows_in[q], 16 * turn)
                    for j in range(ST):
                        last = nc.tensor.transpose(psX[j // 4][:, P * (j % 4):P * (j % 4) + P], rows[q][:, j, 0:D], s.c("ident"))
                    last.then_inc(x_ps, 1)

                def hidden(e, q, n):
                    k, half = unit(n)
                    ring = 4 if layer == 0 else 2
                    for g in range(1 + layer):
                        if n >= ring:
                            pe.wait_ge(sg_ok if g < layer else hs_ok, U * e + n - ring + 1)
                        bank = hb[n % 4] if layer == 0 else hb[2 * (n % 2) + g]
                        f = slice(F * g + P * k, F * g + P * k + P)
                        nc.tensor.matmul(bank[:, 0:HALF], wh[q][:, f], xh[:, half], start=True, stop=False)
                        nc.tensor.matmul(bank[:, 0:HALF], wh[q][:, f], xl[:, half], start=False, stop=False)
                        last = nc.tensor.matmul(bank[:, 0:HALF], wl[q][:, f], xh[:, half], start=False, stop=True)
                    last.then_inc(h_ps, 1)

                def output(e, q, k):
                    pe.wait_ge(hs_ok, U * e + 2 * k + 2)
                    for j in range(ST):
                        last = nc.tensor.matmul(psY[j // 4][:, P * (j % 4):P * (j % 4) + P], hs[:, k, P * j:P * j + P],
                                                w2[q][:, D * k:D * k + D], start=k == 0 and j % 4 == 0, stop=k == FC - 1,
                                                skip_group_check=True)
                    return last

                transpose_rows(0, 0, 1)

                def body(i, q, more, two_more):
                    e = 2 * i + q
                    pe.wait_ge(xl_ok, e + 1)
                    pe.wait_ge(wl_ok, e + 1)
                    ahead = 6 if layer == 0 else 4
                    for n in range(ahead):
                        hidden(e, q, n)
                    pe.wait_ge(y_ok, e + 1)
                    pe.wait_ge(w2_in[q], 16 * i + 16)
                    output(e, q, 0)
                    for n in range(ahead, 6):
                        hidden(e, q, n)
                    if layer == 1:
                        output(e, q, 1)
                    for n in range(6, U):
                        hidden(e, q, n)
                    if layer == 0:
                        output(e, q, 1)
                    if more:
                        transpose_rows(e + 1, 1 - q, i + 1 + q)
                    output(e, q, 2)
                    output(e, q, 3).then_inc(y_ps, 1)
                each(pe, body)


def softmax_attention(nc, io, s, w):
    HD, PARTS = 2, 4
    TG = HD * PARTS
    N = TILES // TG
    sem = s.sem
    scale = float(D) ** -0.5
    with ExitStack() as local:
        def lb(name, shape, dt=f32):
            return local.enter_context(nc.sbuf_tensor("c_" + name, shape, dt))

        def each(name, shape, dt=f32):
            return [lb(f"{name}{h}", shape, dt) for h in range(PARTS)]
        ctxT, xn, xnT = each("ctxT", [D, HD * P]), each("xn", [P, HD, D]), each("xnT", [D, HD * P])
        st, mv, ve, rs = each("st", [P, HD, 6]), each("mv", [P, HD, 2]), each("ve", [P, HD]), each("rs", [P, HD])
        st0, mv0, ve0, rs0 = lb("first_st", [P, TILES, 6]), lb("first_mv", [P, TILES, 2]), lb("first_ve", [P, TILES]), lb("first_rs", [P, TILES])
        QT, KT, V = each("QT", [D, HD * P]), each("KT", [D, HD * P]), each("V", [P, HD, D])
        sc, Pb, PT = each("sc", [P, HD, SEQ]), each("Pb", [P, HD, P]), each("PT", [P, HD * P])
        mx, sm = each("mx", [P, HD]), lb("sm", [P, PARTS, HD])
        minus_half = lb("minus_half", [P, TILES])
        total, inv, rank = (lb(n, [P, TG]) for n in ("total", "inv", "rank"))
        logit, ex, gate, cand, both, pos, place = (lb(n, [P, TG, E]) for n in ("logit", "ex", "gate", "cand", "both", "pos", "place"))
        mask, keep, val = (lb(n, [P, 2, TG, E]) for n in ("mask", "keep", "val"))
        top, kept, slotf, weight = (lb(n, [P, 2, TG]) for n in ("top", "kept", "slotf", "weight"))
        per_tile, upto, used = lb("per_tile", [P, E, TG]), lb("upto", [P, E, TG]), lb("used", [P, E])
        slot = [lb(f"slot{k}", [P, TG], u32) for k in range(2)]
        routed = s.XN[:, 0:TG, :]
        psX, psY = s.ps[0::2], s.ps[1::2]
        ctx_in = [sem(f"c_ctx_in{h}") for h in range(PARTS)]
        LOADS = 4
        rows_in = [sem(f"c_rows_in{n}") for n in range(LOADS)]
        sums = io["sums0"][0:TOKENS, :].rearrange("(t p) d -> p t d", p=P)
        names = ("zeros_ok agg0_ok rs0_ok agg_ok rs_ok xn_ok xnT_ps xnT_ok q_ps q_ok kv_ps kT_ok v_ok s_ps sc_ok "
                 "p_ok pT_ps pT_ok o_ps x3n_ok x3T_ps x3T_ok lg_ps lg_ok sh_ok ex_ok both_ok r_ps ranks_ok slots_ok free scattered dve_order").split()
        m = {k: sem("c_" + k) for k in names}
        with nc.Block() as block:
            @block.sync
            def _(sp):
                def load_context(i, h):
                    sp.dma_start(ctxT[h][:], io["ctxT"][:, bass.ds(P * (TG * i + HD * h), P * HD)]).then_inc(ctx_in[h], 16)

                def store_rows(i):
                    at = bass.ds(TG * i, TG)
                    sp.dma_start(io["sums1"][0:TOKENS, :].rearrange("(t p) d -> p t d", p=P)[:, at, :], s.X[:, at, :]).then_inc(s.summed[1], 16)

                for n in range(LOADS):
                    at = slice(TILES // LOADS * n, TILES // LOADS * (n + 1))
                    sp.dma_start(s.X[:, at, :], sums[:, at, :]).then_inc(rows_in[n], 16)
                    load_context(0, n)
                for q in range(2):
                    w.load_first(sp, q, q)
                    w.load_second(sp, q, q)
                with sp.Fori(1, N) as i:
                    for h in range(PARTS):
                        sp.wait_ge(m["kv_ps"], PARTS * (i - 1) + h + 1)
                        load_context(i, h)
                    sp.wait_ge(m["x3n_ok"], PARTS * i)
                    store_rows(i - 1)
                sp.wait_ge(m["x3n_ok"], PARTS * N)
                store_rows(N - 1)
                sp.wait_ge(m["scattered"], 16 * 2 * TILES)
                w.load_rows(sp, 0, 0)

            @block.gpsimd
            def _(pool):
                for h in range(PARTS):
                    nc.gpsimd.memset(Pb[h][:], 0.0)
                nc.gpsimd.memset(minus_half[:], -0.5).then_inc(m["zeros_ok"], 1)
                pool.wait_ge(m["zeros_ok"], 1)
                for n in range(2):
                    half = slice(TILES // 2 * n, TILES // 2 * (n + 1))
                    pool.wait_ge(m["agg0_ok"], n + 1)
                    nc.gpsimd.tensor_tensor(rs0[:, half], ve0[:, half], minus_half[:, half], ALU.pow).then_inc(m["rs0_ok"], 1)
                pool.sem_inc(m["free"], 1)
                with pool.Fori(0, N) as i:
                    for h in range(PARTS):
                        pool.wait_ge(m["agg_ok"], PARTS * i + h + 1)
                        nc.gpsimd.tensor_tensor(rs[h][:], ve[h][:], minus_half[:, 0:HD], ALU.pow).then_inc(m["rs_ok"], 1)
                    wait_apart(pool, m["slots_ok"], i + 1)
                    for t in range(TG):
                        for k in range(2):
                            pool.indirect_dma_start(out=io["slots1"], out_offset=bass.IndirectOffsetOnAxis(ap=slot[k][:, t:t + 1], axis=0),
                                                    in_=routed[:, t, :], in_offset=None, bounds_check=SLOTS - 1,
                                                    oob_is_err=False).then_inc(m["scattered"], 16)
                    pool.wait_ge(m["scattered"], 16 * 2 * TG * (i + 1))
                    pool.sem_inc(m["free"], 1)

            @block.scalar
            def _(act):
                A = nc.scalar.activation
                A(s.warm[:, 0:1], s.c("ones")[:, 0:1], ACT.Exp)
                act.wait_ge(m["zeros_ok"], 1)
                act.sem_inc(m["lg_ok"], PARTS)
                act.sem_inc(m["ranks_ok"], 1)
                with act.Fori(0, N) as i:
                    at = lambda h: PARTS * i + h + 1
                    for h in range(PARTS):
                        act.wait_ge(m["kv_ps"], at(h))
                        A(KT[h][:], psX[h][:, 0:256], ACT.Identity, bias=s.v("bk")).then_inc(m["kT_ok"], 1)
                    for h in range(PARTS):
                        act.wait_ge(m["xnT_ps"], at(h))
                        A(xnT[h][:], psX[h][:, 256:512], ACT.Copy).then_inc(m["xnT_ok"], 1)
                    for h in range(PARTS):
                        act.wait_ge(m["q_ps"], at(h))
                        A(QT[h][:], psX[h][:, 0:256], ACT.Identity, bias=s.v("bq")).then_inc(m["q_ok"], 1)
                    for h in range(PARTS):
                        act.wait_ge(m["sc_ok"], at(h))
                        for b in range(2):
                            rows = slice(SEQ * b, SEQ * b + SEQ)
                            last = A(Pb[h][rows, :, rows], sc[h][rows, :, :], ACT.Exp, scale=scale)
                        last.then_inc(m["p_ok"], 1)
                    for h in range(PARTS):
                        act.wait_ge(m["pT_ps"], at(h))
                        A(PT[h][:], psX[h][:, 256:512], ACT.Copy).then_inc(m["pT_ok"], 1)

                    def logits(h):
                        act.wait_ge(m["lg_ps"], at(h))
                        A(logit[:, HD * h:HD * h + HD, :], psY[h][:, 256:256 + HD * E].rearrange("p (t e) -> p t e", e=E),
                          ACT.Copy).then_inc(m["lg_ok"], 1)

                    act.wait_ge(m["free"], i + 1)
                    for h in range(PARTS):
                        act.wait_ge(m["x3n_ok"], at(h))
                        A(routed[:, HD * h:HD * h + HD, 0:D], xn[h][:], ACT.Copy)
                        act.wait_ge(m["x3T_ps"], at(h))
                        A(xnT[h][:], psY[h][:, 0:256], ACT.Copy).then_inc(m["x3T_ok"], 1)
                        if h:
                            logits(h - 1)
                    logits(PARTS - 1)
                    act.wait_ge(m["sh_ok"], i + 1)
                    A(ex[:], ex[:], ACT.Exp).then_inc(m["ex_ok"], 1)
                w.high(act, 0, 1)
                A(s.warm[:, 1:2], s.c("ones")[:, 0:1], ACT.Silu)

            @block.vector
            def _(dve):
                V_ = nc.vector
                o = Order(dve, m["dve_order"])
                o.mark(V_.memset(used[:], 0.0))
                for n in range(LOADS):
                    wait_apart(dve, rows_in[n], 16)
                    tiles = range(TILES // LOADS * n, TILES // LOADS * (n + 1))
                    for t in tiles:
                        o.mark(V_.bn_stats(st0[:, t, :], s.X[:, t, :]))
                    o.wait_apart()
                    for t in tiles:
                        o.mark(V_.bn_aggr(mv0[:, t, :], st0[:, t, :]))
                    if n % 2 == 1:
                        o.wait()
                        half = slice(TILES // 2 * (n // 2), TILES // 2 * (n // 2 + 1))
                        V_.tensor_scalar(ve0[:, half], mv0[:, half, 1], EPS, None, ALU.add).then_inc(m["agg0_ok"], 1)
                before = o.n
                DO = 85
                with dve.Fori(0, N) as i:
                    o = Order(dve, m["dve_order"], DO * i + before)
                    at = lambda h: PARTS * i + h + 1
                    tile = lambda h, j: s.X[:, bass.ds(TG * i + HD * h + j, 1), :].rearrange("p a d -> p (a d)")

                    for h in range(PARTS):
                        dve.wait_ge(m["kv_ps"], at(h))
                        V_.tensor_tensor(V[h][:], psY[h][:, 0:256].rearrange("p (t d) -> p t d", d=D),
                                         s.v("bv").unsqueeze(1).broadcast_to([P, HD, D]), ALU.add).then_inc(m["v_ok"], 1)
                    dve.wait_ge(m["rs0_ok"], i + 1)
                    for h in range(PARTS):
                        for j in range(HD):
                            t = bass.ds(TG * i + HD * h + j, 1)
                            last = V_.tensor_scalar(xn[h][:, j, :], tile(h, j), mv0[:, t, 0], rs0[:, t], ALU.subtract, ALU.mult)
                        last.then_inc(m["xn_ok"], 1)
                    for pair in ((0, 1), (2, 3)):
                        for h in pair:
                            dve.wait_ge(m["s_ps"], at(h))
                            o.mark(V_.tensor_tensor(sc[h][:], psY[h][:, 256:384].rearrange("p (t k) -> p t k", k=SEQ),
                                                    s.valid[:, bass.ds(TG * i + HD * h, HD), :], ALU.mult))
                        for h in pair:
                            o.wait(o.n - 1)
                            o.mark(V_.tensor_tensor(sc[h][:], sc[h][:], s.masked[:, bass.ds(TG * i + HD * h, HD), :], ALU.add))
                        for h in pair:
                            o.wait(o.n - 1)
                            o.mark(V_.tensor_reduce(mx[h][:], sc[h][:], AX.X, ALU.max))
                        for h in pair:
                            o.wait(o.n - 1 + h % 2)
                            V_.tensor_tensor(sc[h][:], sc[h][:], mx[h][:].unsqueeze(2).broadcast_to([P, HD, SEQ]), ALU.subtract).then_inc(m["sc_ok"], 1)
                    for h in range(PARTS):
                        dve.wait_ge(m["p_ok"], at(h))
                        o.mark(V_.tensor_reduce(sm[:, h, :], Pb[h][:], AX.X, ALU.add))
                    o.wait()
                    o.mark(V_.reciprocal(sm[:], sm[:]))
                    o.wait()
                    weighed = o.mark(V_.tensor_scalar(sm[:], sm[:], s.tg[:, 1:2], None, ALU.mult))

                    def residual(h):
                        dve.wait_ge(m["o_ps"], at(h))
                        o.wait(weighed)
                        for j in range(HD):
                            n = o.mark(V_.scalar_tensor_tensor(tile(h, j), psX[h][:, 128 * j:128 * j + 128], sm[:, h, j:j + 1], tile(h, j),
                                                               ALU.mult, ALU.add))
                        return n

                    added = residual(0)
                    for h in range(PARTS):
                        o.wait_apart(added)
                        for j in range(HD):
                            counted = o.mark(V_.bn_stats(st[h][:, j, :], tile(h, j)))
                        if h + 1 < PARTS:
                            added = residual(h + 1)
                        o.wait_apart(counted)
                        for j in range(HD):
                            o.mark(V_.bn_aggr(mv[h][:, j, :], st[h][:, j, :]))
                        o.wait()
                        V_.tensor_scalar(ve[h][:], mv[h][:, :, 1], 1.0 + EPS, EPS * EPS, ALU.mult, ALU.add).then_inc(m["agg_ok"], 1)
                        for j in range(HD):
                            o.mark(V_.scalar_tensor_tensor(xn[h][:, j, :], tile(h, j), mv[h][:, j, 0:1], s.v("gamma1"), ALU.subtract, ALU.mult))
                    for h in range(PARTS):
                        dve.wait_ge(m["rs_ok"], PARTS * i + h + 1)
                        o.wait()
                        for j in range(HD):
                            last = V_.scalar_tensor_tensor(xn[h][:, j, :], xn[h][:, j, :], rs[h][:, j:j + 1], s.v("beta1"), ALU.mult, ALU.add)
                        last.then_inc(m["x3n_ok"], 1)

                    def step(ins):
                        o.mark(ins)
                        o.wait()

                    def b3(t):
                        return t.unsqueeze(2).broadcast_to([P, TG, E])

                    rev = s.c("rev").unsqueeze(1).broadcast_to([P, TG, E])
                    dve.wait_ge(m["lg_ok"], PARTS * i + 2 * PARTS)
                    step(V_.tensor_scalar(logit[:], logit[:], -1e4, 1e4, ALU.max, ALU.min))
                    step(V_.tensor_reduce(rank[:], logit[:], AX.X, ALU.max))
                    V_.tensor_tensor(ex[:], logit[:], b3(rank[:]), ALU.subtract).then_inc(m["sh_ok"], 1)
                    dve.wait_ge(m["ex_ok"], i + 1)
                    step(V_.tensor_reduce(total[:], ex[:], AX.X, ALU.add))
                    step(V_.tensor_scalar(total[:], total[:], 1e-12, None, ALU.add))
                    step(V_.reciprocal(inv[:], total[:]))
                    step(V_.tensor_tensor(gate[:], ex[:], b3(inv[:]), ALU.mult))
                    for k in range(2):
                        left = gate if k == 0 else ex
                        if k == 1:
                            step(V_.scalar_tensor_tensor(ex[:].rearrange("p t e -> p (t e)"), mask[:, 0].rearrange("p t e -> p (t e)"), -2.0,
                                                        gate[:].rearrange("p t e -> p (t e)"), ALU.mult, ALU.add))
                        step(V_.tensor_reduce(top[:, k], left[:], AX.X, ALU.max))
                        step(V_.tensor_tensor(cand[:], left[:], b3(top[:, k]), ALU.is_equal))
                        step(V_.tensor_tensor(cand[:], cand[:], rev, ALU.mult))
                        step(V_.tensor_reduce(rank[:], cand[:], AX.X, ALU.max))
                        step(V_.tensor_tensor(mask[:, k], rev, b3(rank[:]), ALU.is_equal))
                    V_.tensor_tensor(both[:], mask[:, 0], mask[:, 1], ALU.add).then_inc(m["both_ok"], 1)
                    dve.wait_ge(m["r_ps"], i + 1)
                    step(V_.tensor_copy(per_tile[:], psX[PARTS - 1][:, TG * E:2 * TG * E].rearrange("p (t e) -> p e t", t=TG)))
                    flat = "p e t -> p (e t)"
                    step(V_.tensor_tensor_scan(upto[:].rearrange(flat), s.c("restart_half"), per_tile[:].rearrange(flat), 0.0, ALU.mult, ALU.add))
                    step(V_.tensor_tensor(per_tile[:], upto[:], per_tile[:], ALU.subtract))
                    step(V_.tensor_tensor(per_tile[:], per_tile[:], used[:].unsqueeze(2).broadcast_to([P, E, TG]), ALU.add))
                    V_.tensor_tensor(pos[:], psX[PARTS - 1][:, 0:TG * E].rearrange("p (t e) -> p t e", e=E),
                                    per_tile[:].rearrange("p e t -> p t e"), ALU.add).then_inc(m["ranks_ok"], 1)
                    o.mark(V_.tensor_tensor(used[:], used[:], upto[:, :, TG - 1], ALU.add))
                    dve.wait_ge(m["ranks_ok"], i + 2)
                    all_, one = "p k t e -> p (k t) e", "p t e -> p (t e)"
                    o.mark(V_.tensor_tensor(place[:], pos[:], s.c("expert_base").unsqueeze(1).broadcast_to([P, TG, E]), ALU.add))
                    for k in range(2):
                        o.mark(V_.scalar_tensor_tensor(keep[:, k].rearrange(one), pos[:].rearrange(one), float(CAP), mask[:, k].rearrange(one),
                                                       ALU.is_lt, ALU.mult))
                    o.wait()
                    step(V_.tensor_tensor(val[:], place[:].unsqueeze(1).broadcast_to([P, 2, TG, E]), keep[:], ALU.mult))
                    o.mark(V_.tensor_reduce(kept[:].rearrange("p k t -> p (k t)"), keep[:].rearrange(all_), AX.X, ALU.add))
                    step(V_.tensor_reduce(slotf[:].rearrange("p k t -> p (k t)"), val[:].rearrange(all_), AX.X, ALU.add))
                    step(V_.scalar_tensor_tensor(slotf[:].rearrange("p k t -> p (k t)"), kept[:].rearrange("p k t -> p (k t)"), -2.0 * SLOTS,
                                                slotf[:].rearrange("p k t -> p (k t)"), ALU.mult, ALU.add))
                    step(V_.tensor_tensor(weight[:], kept[:], top[:], ALU.mult))
                    dve.wait_ge(m["free"], i + 1)
                    for k in range(2):
                        o.mark(V_.tensor_scalar(slot[k][:], slotf[:, k], 2.0 * SLOTS, None, ALU.add))
                    o.wait()
                    o.mark(V_.tensor_copy(routed[:, :, D].bitcast(u32), s.c("token")[:, bass.ds(TG * i, TG)]))
                    for k in range(2):
                        o.mark(V_.tensor_scalar(routed[:, :, D + 1 + k], weight[:, k], s.tg[:, 3:4], None, ALU.mult))
                    V_.tensor_copy(routed[:, :, D + 3], slot[0][:]).then_inc(m["slots_ok"], 1)
                    assert o.n == DO, o.n
                w.low(dve, 0, 0)

            @block.tensor
            def _(pe):
                mm = nc.tensor.matmul
                with pe.Fori(0, N) as i:
                    at = lambda h: PARTS * i + h + 1
                    for h in range(PARTS):
                        pe.wait_ge(ctx_in[h], 16 * i + 16)
                        pe.wait_ge(m["lg_ok"], at(h))
                        if h == PARTS - 1:
                            pe.wait_ge(m["ranks_ok"], i + 1)
                        mm(psX[h][:, 0:256], s.w("wk1"), ctxT[h][:], start=True, stop=True)
                        for j in range(HD):
                            last = mm(psY[h][:, 128 * j:128 * j + 128], ctxT[h][:, 128 * j:128 * j + 128], s.w("wv1"), start=True, stop=True)
                        last.then_inc(m["kv_ps"], 1)
                    for h in range(PARTS):
                        pe.wait_ge(m["xn_ok"], at(h))
                        pe.wait_ge(m["kT_ok"], at(h))
                        for j in range(HD):
                            last = nc.tensor.transpose(psX[h][:, 256 + 128 * j:384 + 128 * j], xn[h][:, j, :], s.c("ident"))
                        last.then_inc(m["xnT_ps"], 1)
                    for h in range(PARTS):
                        pe.wait_ge(m["xnT_ok"], at(h))
                        mm(psX[h][:, 0:256], s.w("wq1"), xnT[h][:], start=True, stop=True).then_inc(m["q_ps"], 1)
                    for h in range(PARTS):
                        pe.wait_ge(m["q_ok"], at(h))
                        pe.wait_ge(m["v_ok"], at(h))
                        for j in range(HD):
                            for b in range(2):
                                tok = slice(128 * j + SEQ * b, 128 * j + SEQ * b + SEQ)
                                last = mm(psY[h][SEQ * b:SEQ * b + SEQ, 256 + SEQ * j:256 + SEQ * j + SEQ], QT[h][:, tok], KT[h][:, tok],
                                          start=True, stop=True)
                        last.then_inc(m["s_ps"], 1)
                    for h in range(PARTS):
                        pe.wait_ge(m["p_ok"], at(h))
                        for j in range(HD):
                            last = nc.tensor.transpose(psX[h][:, 256 + 128 * j:384 + 128 * j], Pb[h][:, j, :], s.c("ident"))
                        last.then_inc(m["pT_ps"], 1)
                    for h in range(PARTS):
                        pe.wait_ge(m["pT_ok"], at(h))
                        for j in range(HD):
                            last = mm(psX[h][:, 128 * j:128 * j + 128], PT[h][:, 128 * j:128 * j + 128], V[h][:, j, :], start=True, stop=True)
                        last.then_inc(m["o_ps"], 1)

                    def logits(h):
                        pe.wait_ge(m["x3T_ok"], at(h))
                        for j in range(HD):
                            last = mm(psY[h][:, 256 + E * j:256 + E * j + E], xnT[h][:, 128 * j:128 * j + 128], s.w("router1"), start=True, stop=True)
                        last.then_inc(m["lg_ps"], 1)

                    for h in range(PARTS):
                        pe.wait_ge(m["x3n_ok"], at(h))
                        for j in range(HD):
                            last = nc.tensor.transpose(psY[h][:, 128 * j:128 * j + 128], xn[h][:, j, :], s.c("ident"))
                        last.then_inc(m["x3T_ps"], 1)
                        if h:
                            logits(h - 1)
                    logits(PARTS - 1)
                    pe.wait_ge(m["both_ok"], i + 1)
                    flat = both[:].rearrange("p t e -> p (t e)")
                    mm(psX[PARTS - 1][:, 0:TG * E], s.c("before"), flat, start=True, stop=True)
                    mm(psX[PARTS - 1][:, TG * E:2 * TG * E], s.c("ones"), flat, start=True, stop=True).then_inc(m["r_ps"], 1)


def layout(i):
    f = lambda k: np.asarray(i[k])
    row = lambda a: np.broadcast_to(a.reshape(1, -1), (P, a.size))
    shape = np.zeros((P, columns(SHAPE_COLS)[1]), np.float32)
    sc = columns(SHAPE_COLS)[0]
    put = lambda k, a: shape.__setitem__((slice(None), slice(sc[k][0], sc[k][0] + sc[k][1])), a)
    put("ident", np.eye(P))
    put("before", np.triu(np.ones((P, P)), 1))
    put("ones", 1.0)
    put("heads", np.kron(np.eye(D // HEAD), np.ones((HEAD, HEAD))))
    put("own", np.kron(np.ones((4, 1)), np.kron(np.eye(4), np.ones((HEAD, 1)))))
    put("rev", E - np.arange(E))
    put("expert_base", CAP * np.arange(E))
    put("spare", TOKENS + P * np.arange(ST)[None, :] + np.arange(P)[:, None])
    put("token", P * np.arange(TILES)[None, :] + np.arange(P)[:, None])
    put("slot", P * np.arange(E * ST)[None, :] + np.arange(P)[:, None])
    put("restart_half", (np.arange(E * TILES // 2) % (TILES // 2) > 0) * 1.0)
    put("restart", (np.arange(2 * E * TILES) % TILES > 0) * 1.0)
    vec = np.concatenate([row(f("L0_xattn_ln_gamma")), row(f("L0_xattn_ln_beta")), row(f("L0_xattn_dense_b")), row(f("L1_xattn_bv")),
                          row(f("L1_ffn_ln_gamma")), row(f("L1_ffn_ln_beta")), f("L0_xattn_ln_gamma")[:, None],
                          f("L0_xattn_ln_beta")[:, None], f("L1_xattn_bq")[:, None], f("L1_xattn_bk")[:, None],
                          row(f("g_xattn")), row(f("g_ffn")), f("mask_BxS2_ff1").reshape(TILES, P).T,
                          np.full((P, 1), EPS, np.float32), np.full((P, 1), EPS_L0, np.float32)], axis=1)
    dense = np.broadcast_to(f("L0_xattn_dense_w").reshape(4, 4, 1, HEAD, D), (4, 4, 4, HEAD, D)).transpose(0, 2, 3, 1, 4).reshape(P, 4 * D)
    w = np.concatenate([f("L0_xattn_wq"), f("L0_xattn_wk"), f("L0_xattn_wv"), dense, f("L0_ffn_router_w"),
                        f("L1_xattn_Wq"), f("L1_xattn_Wk"), f("L1_xattn_Wv"), f("L1_ffn_Wr").T], axis=1)
    second = lambda a: a.reshape(-1, FC, P, D).transpose(0, 2, 1, 3).reshape(-1, P, FC * D)
    w1 = np.concatenate([f("L0_ffn_w1"), f("L0_ffn_sw1")[None]])
    w2 = np.concatenate([f("L0_ffn_w2"), f("L0_ffn_sw2")[None]])
    b1 = np.concatenate([f("L0_ffn_b1"), f("L0_ffn_sb1")[None]])
    b2 = np.concatenate([f("L0_ffn_b2"), f("L0_ffn_sb2")[None]])
    bias0 = np.concatenate([b1.reshape((E + 1) * FC, P).T, row(b2)], axis=1)
    pack1 = np.concatenate([f("L1_ffn_W12").transpose(0, 2, 1), second(f("L1_ffn_W3").transpose(0, 2, 1))], axis=2)
    return {
        "x": f("x").reshape(TOKENS, D), "ctxT": f("ctx_1024").reshape(TOKENS, D).T, "shape": shape, "vec": vec, "w": w,
        "experts0": np.concatenate([w1, second(w2)], axis=2), "bias0": bias0, "experts1": pack1,
        "keymask": np.repeat(f("mask_BxS2_ik0").reshape(TILES, 2, SEQ).transpose(1, 0, 2).reshape(2, -1), SEQ, axis=0),
    }


def declare(nc, arrays):
    io = {}
    for name, a in arrays.items():
        io[name] = nc.dram_tensor(f"in_{name}", a.shape, mybir.dt.from_np(a.dtype), kind="ExternalInput").ap()
    for k in range(2):
        io[f"slots{k}"] = nc.dram_tensor(f"slots{k}", (SLOTS, ROW), f32, kind="Internal").ap()
    io["sums0"] = nc.dram_tensor("sums0", (TOKENS + CAP, D), f32, kind="Internal").ap()
    io["sums1"] = nc.dram_tensor("out_dram", (TOKENS + CAP, D), f32, kind="ExternalOutput").ap()
    return io


def kernel(**inputs):
    import concourse.bacc as _bacc
    from concourse.bass_utils import run_bass_kernel_spmd as _run

    nc = _bacc.Bacc("TRN2", target_bir_lowering=False, num_devices=1)
    arrays = {k: np.ascontiguousarray(a) for k, a in layout(inputs).items()}
    build(nc, declare(nc, arrays))
    r = _run(nc, [{f"in_{k}": a for k, a in arrays.items()}], core_ids=[0])
    return r.results[0]["out_dram"][:TOKENS].reshape(32, SEQ, D)
```
